# Optimizing a Trainium2 kernel written in Bass

```python
import numpy as np
import jax
import jax.numpy as jnp

def _softmax(x, axis=-1):
    return jax.nn.softmax(x, axis=axis)

def _gelu(x):
    return jax.nn.gelu(x, approximate=True)

def _silu(x):
    return jax.nn.silu(x)

def _sigmoid(x):
    return jax.nn.sigmoid(x)

def _layernorm(x, axis=-1, eps=1e-05):
    m = jnp.mean(x, axis=axis, keepdims=True)
    v = jnp.var(x, axis=axis, keepdims=True)
    return (x - m) / jnp.sqrt(v + eps)

def _scatter_add(tgt, idx, src, axis=0):
    return tgt.at[idx].add(src)

def _segment_sum(src, seg, n):
    return jax.ops.segment_sum(src, seg, n)
kernel_name = 'mk_prb_d2_jaxref_r8_b16a71'

def setup_inputs(seed: int=0):
    np.random.seed(seed)
    _w = jnp.asarray

    def _L0_attn_setup():
        import jax, jax.numpy as jnp
        import numpy as np
        EPS = 1.1920929e-07

        def _rms(x):
            return x * jax.lax.rsqrt(jnp.mean(x * x, axis=-1, keepdims=True) + EPS)
        key = jax.random.key(seed)
        k0, k1, k2, k3 = jax.random.split(key, 4)
        B, S, D, DFF = (4, 256, 256, 1024)
        x = jax.random.normal(k0, (B, S, D), dtype=jnp.float32)
        w_qkv = jax.random.normal(k1, (3 * D, D), dtype=jnp.float32) * 0.02
        w_swiglu = jax.random.normal(k2, (2 * DFF, D), dtype=jnp.float32) * 0.02
        w_out = jax.random.normal(k3, (D, DFF), dtype=jnp.float32) * 0.02
        return {'x': x, 'w_qkv': w_qkv, 'w_swiglu': w_swiglu, 'w_out': w_out}
    _L0_attn_in = _L0_attn_setup()

    def _L0_ffn_setup():
        import jax, jax.numpy as jnp
        import numpy as np
        B, S, H = (2, 256, 256)
        E, I = (32, 128)
        SI = 512
        K = 4
        G = 4
        TKG = 2
        SCALE = 2.5

        def _relu2(v):
            r = jax.nn.relu(v)
            return r * r
        key = jax.random.key(seed)
        ks = jax.random.split(key, 7)
        w = 0.02
        return {'x': jax.random.normal(ks[0], (B, S, H), jnp.float32), 'gate_w': jax.random.normal(ks[1], (H, E), jnp.float32) * w, 'e_bias': jax.random.normal(ks[2], (E,), jnp.float32) * 0.01, 'Wu': jax.random.normal(ks[3], (E, H, I), jnp.float32) * w, 'Wd': jax.random.normal(ks[4], (E, I, H), jnp.float32) * w, 'Wsu': jax.random.normal(ks[5], (H, SI), jnp.float32) * w, 'Wsd': jax.random.normal(ks[6], (SI, H), jnp.float32) * w}
    _L0_ffn_in = _L0_ffn_setup()

    def _L1_attn_setup():
        import jax, jax.numpy as jnp
        import numpy as np
        import math
        EPS = float(jnp.finfo(jnp.float32).eps)
        ROPE_BASE = 10000.0
        B, S, D_MODEL, H = (2, 256, 256, 16)
        D_K = D_MODEL // H

        def _rope_tables(seq_len, d_k, dtype):
            inv_freq = 1.0 / ROPE_BASE ** (jnp.arange(0, d_k, 2, dtype=dtype) / d_k)
            ang = jnp.arange(seq_len, dtype=dtype)[:, None] * inv_freq[None, :]
            cos = jnp.concatenate([jnp.cos(ang), jnp.cos(ang)], axis=-1)
            sin = jnp.concatenate([jnp.sin(ang), jnp.sin(ang)], axis=-1)
            return (cos, sin)

        def _rotate_half(x):
            half = x.shape[-1] // 2
            return jnp.concatenate([-x[..., half:], x[..., :half]], axis=-1)
        key = jax.random.key(seed)
        ks = jax.random.split(key, 5)
        scale = 1.0 / math.sqrt(D_MODEL)
        return {'X': jax.random.normal(ks[0], (B, S, D_MODEL), dtype=jnp.float32), 'Wq_w': jax.random.normal(ks[1], (D_MODEL, D_MODEL), dtype=jnp.float32) * scale, 'Wq_b': jax.random.normal(ks[2], (D_MODEL,), dtype=jnp.float32) * 0.01, 'Wo_w': jax.random.normal(ks[3], (D_MODEL, D_MODEL), dtype=jnp.float32) * scale, 'Wo_b': jax.random.normal(ks[4], (D_MODEL,), dtype=jnp.float32) * 0.01, 'rms_w': jnp.ones((D_MODEL,), dtype=jnp.float32)}
    _L1_attn_in = _L1_attn_setup()

    def _L1_ffn_setup():
        import jax, jax.numpy as jnp
        import numpy as np
        B, S, DIM = (2, 256, 256)
        INTER = 176
        E = 8
        K = 2
        SHARED = 1
        ROUTE_SCALE = 1.0

        def _expert(xt, w1, w2, w3, cw=None):
            h = jax.nn.silu((xt @ w1.T).astype(jnp.float32)) * (xt @ w3.T).astype(jnp.float32)
            if cw is not None:
                h = cw[:, None] * h
            return h.astype(xt.dtype) @ w2.T
        key = jax.random.key(seed)
        ks = jax.random.split(key, 9)
        bf = lambda k, shape: (jax.random.normal(k, shape, dtype=jnp.float32) * 0.02).astype(jnp.bfloat16)
        return {'x': jax.random.normal(ks[0], (B, S, DIM), dtype=jnp.float32).astype(jnp.bfloat16), 'gate_w': jax.random.normal(ks[1], (E, DIM), dtype=jnp.float32) * 0.02, 'gate_b': jax.random.normal(ks[2], (E,), dtype=jnp.float32) * 0.01, 'w1': bf(ks[3], (E, INTER, DIM)), 'w2': bf(ks[4], (E, DIM, INTER)), 'w3': bf(ks[5], (E, INTER, DIM)), 'sw1': bf(ks[6], (SHARED * INTER, DIM)), 'sw2': bf(ks[7], (DIM, SHARED * INTER)), 'sw3': bf(ks[8], (SHARED * INTER, DIM))}
    _L1_ffn_in = _L1_ffn_setup()
    _d = {'L0_attn_x': _L0_attn_in['x'], 'L0_attn_w_qkv': _L0_attn_in['w_qkv'], 'L0_attn_w_swiglu': _L0_attn_in['w_swiglu'], 'L0_attn_w_out': _L0_attn_in['w_out'], 'L0_ffn_gate_w': _L0_ffn_in['gate_w'], 'L0_ffn_e_bias': _L0_ffn_in['e_bias'], 'L0_ffn_Wu': _L0_ffn_in['Wu'], 'L0_ffn_Wd': _L0_ffn_in['Wd'], 'L0_ffn_Wsu': _L0_ffn_in['Wsu'], 'L0_ffn_Wsd': _L0_ffn_in['Wsd'], 'L1_attn_Wq_w': _L1_attn_in['Wq_w'], 'L1_attn_Wq_b': _L1_attn_in['Wq_b'], 'L1_attn_Wo_w': _L1_attn_in['Wo_w'], 'L1_attn_Wo_b': _L1_attn_in['Wo_b'], 'L1_attn_rms_w': _L1_attn_in['rms_w'], 'L1_ffn_gate_w': _L1_ffn_in['gate_w'], 'L1_ffn_gate_b': _L1_ffn_in['gate_b'], 'L1_ffn_w1': _L1_ffn_in['w1'], 'L1_ffn_w2': _L1_ffn_in['w2'], 'L1_ffn_w3': _L1_ffn_in['w3'], 'L1_ffn_sw1': _L1_ffn_in['sw1'], 'L1_ffn_sw2': _L1_ffn_in['sw2'], 'L1_ffn_sw3': _L1_ffn_in['sw3']}
    _x0 = _d['L0_attn_x']
    _d['L0_attn_x'] = jax.random.normal(jax.random.fold_in(jax.random.key(seed), 1), (16, 256, 256), dtype=_x0.dtype)
    del _x0
    return _d

def reference(L0_attn_x, L0_attn_w_qkv, L0_attn_w_swiglu, L0_attn_w_out, L0_ffn_gate_w, L0_ffn_e_bias, L0_ffn_Wu, L0_ffn_Wd, L0_ffn_Wsu, L0_ffn_Wsd, L1_attn_Wq_w, L1_attn_Wq_b, L1_attn_Wo_w, L1_attn_Wo_b, L1_attn_rms_w, L1_ffn_gate_w, L1_ffn_gate_b, L1_ffn_w1, L1_ffn_w2, L1_ffn_w3, L1_ffn_sw1, L1_ffn_sw2, L1_ffn_sw3):

    def _L0_attn_ref(x, w_qkv, w_swiglu, w_out):
        import jax, jax.numpy as jnp
        import numpy as np
        EPS = 1.1920929e-07

        def _rms(x):
            return x * jax.lax.rsqrt(jnp.mean(x * x, axis=-1, keepdims=True) + EPS)
        qkv = _rms(x) @ w_qkv.T
        q, k, v = jnp.split(qkv, 3, axis=-1)
        q = _rms(q)
        k = _rms(k)
        w = jnp.exp(k)
        kv_cum = jnp.cumsum(w * v, axis=1)
        w_cum = jnp.cumsum(w, axis=1)
        y = jax.nn.sigmoid(q) * (kv_cum / (w_cum + 1e-06))
        uv = y @ w_swiglu.T
        u, g = jnp.split(uv, 2, axis=-1)
        return x + u * jax.nn.silu(g) @ w_out.T

    def _L0_ffn_ref(x, gate_w, e_bias, Wu, Wd, Wsu, Wsd):
        import jax, jax.numpy as jnp
        import numpy as np
        B, S, H = (2, 256, 256)
        E, I = (32, 128)
        SI = 512
        K = 4
        G = 4
        TKG = 2
        SCALE = 2.5

        def _relu2(v):
            r = jax.nn.relu(v)
            return r * r
        orig_shape = x.shape
        h = x.reshape(-1, H)
        T = h.shape[0]
        logits = h @ gate_w
        scores = jax.nn.sigmoid(logits)
        sfc = scores + e_bias[None, :]
        per_group = sfc.reshape(T, G, E // G)
        group_scores = jnp.sum(jax.lax.top_k(per_group, 2)[0], axis=-1)
        _, gidx = jax.lax.top_k(group_scores, TKG)
        group_mask = jnp.sum(jax.nn.one_hot(gidx, G, dtype=sfc.dtype), axis=1)
        score_mask = jnp.repeat(group_mask, E // G, axis=-1)
        sfc_masked = jnp.where(score_mask > 0, sfc, 0.0)
        _, topk_idx = jax.lax.top_k(sfc_masked, K)
        topk_w = jnp.take_along_axis(scores, topk_idx, axis=1)
        topk_w = topk_w / (jnp.sum(topk_w, axis=-1, keepdims=True) + 1e-20)
        topk_w = topk_w * SCALE
        combine = jnp.zeros((T, E), scores.dtype).at[jnp.arange(T)[:, None], topk_idx].add(topk_w)
        up = jnp.einsum('th,ehi->tei', h, Wu)
        act = _relu2(up)
        routed = jnp.einsum('tei,te,eih->th', act, combine, Wd)
        shared = _relu2(h @ Wsu) @ Wsd
        out = (routed + shared).reshape(orig_shape)
        return out

    def _L1_attn_ref(X, Wq_w, Wq_b, Wo_w, Wo_b, rms_w):
        import jax, jax.numpy as jnp
        import numpy as np
        import math
        EPS = float(jnp.finfo(jnp.float32).eps)
        ROPE_BASE = 10000.0
        B, S, D_MODEL, H = (2, 256, 256, 16)
        D_K = D_MODEL // H

        def _rope_tables(seq_len, d_k, dtype):
            inv_freq = 1.0 / ROPE_BASE ** (jnp.arange(0, d_k, 2, dtype=dtype) / d_k)
            ang = jnp.arange(seq_len, dtype=dtype)[:, None] * inv_freq[None, :]
            cos = jnp.concatenate([jnp.cos(ang), jnp.cos(ang)], axis=-1)
            sin = jnp.concatenate([jnp.sin(ang), jnp.sin(ang)], axis=-1)
            return (cos, sin)

        def _rotate_half(x):
            half = x.shape[-1] // 2
            return jnp.concatenate([-x[..., half:], x[..., :half]], axis=-1)
        pre_X = X
        ms = jnp.mean(X * X, axis=-1, keepdims=True)
        Xn = X * jax.lax.rsqrt(ms + EPS) * rms_w
        b, s, _ = X.shape
        Q = (Xn @ Wq_w.T + Wq_b).reshape(b, s, H, D_K).transpose(0, 2, 1, 3)
        K = Q
        V = Q
        cos, sin = _rope_tables(s, D_K, X.dtype)
        Qr = Q * cos + _rotate_half(Q) * sin
        Kr = K * cos + _rotate_half(K) * sin
        A = jnp.einsum('bhqd,bhkd->bhqk', Qr, Kr) / math.sqrt(D_K)
        causal = jnp.tril(jnp.ones((s, s), dtype=bool))
        A = jnp.where(causal, A, -jnp.inf)
        A = jax.nn.softmax(A, axis=-1)
        O = jnp.einsum('bhqk,bhkd->bhqd', A, V)
        O = O.transpose(0, 2, 1, 3).reshape(b, s, H * D_K)
        O = O @ Wo_w.T + Wo_b
        return pre_X + O

    def _L1_ffn_ref(x, gate_w, gate_b, w1, w2, w3, sw1, sw2, sw3):
        import jax, jax.numpy as jnp
        import numpy as np
        B, S, DIM = (2, 256, 256)
        INTER = 176
        E = 8
        K = 2
        SHARED = 1
        ROUTE_SCALE = 1.0

        def _expert(xt, w1, w2, w3, cw=None):
            h = jax.nn.silu((xt @ w1.T).astype(jnp.float32)) * (xt @ w3.T).astype(jnp.float32)
            if cw is not None:
                h = cw[:, None] * h
            return h.astype(xt.dtype) @ w2.T
        Bx, Sx, D = x.shape
        xt = x.reshape(-1, D)
        T = xt.shape[0]
        scores = xt.astype(jnp.float32) @ gate_w.T
        scores = jnp.sqrt(jax.nn.softplus(scores))
        biased = scores + gate_b
        _, idx = jax.lax.top_k(biased, K)
        weights = jnp.take_along_axis(scores, idx, axis=1) * ROUTE_SCALE
        cw = jnp.einsum('tk,tke->te', weights, jax.nn.one_hot(idx, E, dtype=jnp.float32))
        y = jnp.zeros((T, D), dtype=xt.dtype)
        for e in range(E):
            y = y + _expert(xt, w1[e], w2[e], w3[e], cw[:, e])
        z = _expert(xt, sw1, sw2, sw3)
        return (y + z).reshape(Bx, Sx, D)
    x = L0_attn_x
    xn = _layernorm(x, axis=-1)
    x = x + _L0_attn_ref(xn, L0_attn_w_qkv, L0_attn_w_swiglu, L0_attn_w_out) + _L0_ffn_ref(xn, L0_ffn_gate_w, L0_ffn_e_bias, L0_ffn_Wu, L0_ffn_Wd, L0_ffn_Wsu, L0_ffn_Wsd)
    xn = _layernorm(x, axis=-1)
    x = x + _L1_attn_ref(xn, L1_attn_Wq_w, L1_attn_Wq_b, L1_attn_Wo_w, L1_attn_Wo_b, L1_attn_rms_w) + _L1_ffn_ref(xn, L1_ffn_gate_w, L1_ffn_gate_b, L1_ffn_w1, L1_ffn_w2, L1_ffn_w3, L1_ffn_sw1, L1_ffn_sw2, L1_ffn_sw3)
    return x

_drawn_inputs = setup_inputs


def setup_inputs(seed=0):
    import zlib

    import numpy as np

    out = dict(_drawn_inputs(seed))
    spreads = {'L1_attn_rms_w': (1.0, 0.6)}
    factors = {'L0_attn_w_qkv': 8.0,
     'L0_attn_w_swiglu': 8.0,
     'L0_attn_w_out': 8.0,
     'L0_ffn_gate_w': 3.318,
     'L0_ffn_e_bias': 7.972,
     'L0_ffn_Wu': 3.391,
     'L0_ffn_Wd': 3.107,
     'L1_attn_Wq_b': 129.28,
     'L1_attn_Wo_b': 164.271,
     'L1_ffn_gate_w': 200.0,
     'L1_ffn_gate_b': 200.0,
     'L0_ffn_Wsu': 7.936,
     'L0_ffn_Wsd': 7.186}
    for name, (base, spread) in spreads.items():
        noise = np.random.default_rng([zlib.crc32(name.encode()), seed]).standard_normal(out[name].shape)
        drawn = base * np.exp(spread * noise) if base else spread * noise
        out[name] = jnp.asarray(drawn.astype(out[name].dtype))
    for name, factor in factors.items():
        out[name] = (out[name] * factor).astype(out[name].dtype)
    return out
```

```python
from contextlib import ExitStack

import concourse.bass as bass
from concourse import mybir

F32 = mybir.dt.float32
F32R = mybir.dt.float32r
BF16 = mybir.dt.bfloat16
I32 = mybir.dt.int32
U32 = mybir.dt.uint32
ALU = mybir.AluOpType
ACT = mybir.ActivationFunctionType
AX = mybir.AxisListType.X

P = 128
D = 256
KT = D // P
T = 4096
CH = 512
NCH = T // CH
TP = CH // P
NT = T // P
E0, TOP0, I0 = 32, 4, 128
G0 = 4
EG = E0 // G0
SCALE0 = 2.5
NB = (T * TOP0 + E0 * (P - 1)) // P + 1
SLOTS = NB * P
UG = 1024
SI = 512
E1, TOP1, I1 = 8, 2, 176
ROWS1 = (E1 + 1) * I1
SLOTS1 = -(-ROWS1 // P)
ROUTED1 = E1 * I1 // P
H1, S1 = 16, 256
DK = D // H1
LN_EPS = 1e-5
RMS_EPS = 1.1920929e-07


class Shared:
    pass


class Chain:

    def __init__(self, eng, sem, per_round, done=None):
        self.eng, self.sem, self.per_round, self.done = eng, sem, per_round, done
        self.base, self.n = 0, 0

    def begin(self, rounds_before):
        self.base, self.n = rounds_before * self.per_round, 0

    def count(self, ins):
        self.n += 1
        ins.then_inc(self.sem, 1)

    def link(self, ins, apart=False):
        self.count(ins)
        self.eng.wait_ge(self.sem, self.base + self.n)
        if apart:
            self.eng.sem_inc(self.done, 1)

    def end(self):
        assert self.n == self.per_round, self.n


def route_tokens(nc, k, st):
    sem, sb = k.sem, lambda name, shape, dt=F32: k.sb(st, name, shape, dt)
    E, K = E0, TOP0
    x_t = sb("a_x", [P, 2, TP, D])
    xn = sb("a_xn", [P, 2, TP, D])
    xnT = sb("a_xnT", [P, 2, KT, CH])
    gate_w = sb("a_gate_w", [P, KT, E])
    bias = sb("a_bias", [P, E])
    stats = sb("a_stats", [P, TP, 6])
    mv = sb("a_mv", [P, TP, 2])
    var = sb("a_var", [P, 2, TP])
    rstd = sb("a_rstd", [P, 2, TP])
    expn = sb("a_expn", [P, TP * E])
    score = sb("a_score", [P, TP, E])
    biased = sb("a_biased", [P, TP, E])
    top8g = sb("a_top8g", [P, TP * G0, 8])
    gscore = sb("a_gscore", [P, TP, G0])
    beats = sb("a_beats", [P, TP, G0, G0])
    gmask = sb("a_gmask", [P, TP, G0])
    top8 = sb("a_top8", [P, TP, 8])
    index8 = sb("a_index8", [P, TP, 8], U32)
    chosen = sb("a_chosen", [P, TP, K])
    onehot = sb("a_onehot", [P, TP, K, E])
    picked = sb("a_picked", [P, TP, K, E])
    weight = sb("a_weight", [P, TP, K])
    wsum = sb("a_wsum", [P, TP])
    takes = sb("a_takes", [P, 2, TP, E], BF16)
    rank = sb("a_rank", [P, TP, E])
    count = sb("a_count", [P, E])
    blocks = sb("a_blocks", [P, E])
    blocks_i = sb("a_blocks_i", [P, E], I32)
    upto_blocks = sb("a_upto_blocks", [P, E])
    start = sb("a_start", [P, E])
    zeros = sb("a_zeros", [P, 2048])
    wide = sb("a_wide", [P, 40 * E])

    w_in, x_in = sem("a_w_in"), [sem("a_x_in0"), sem("a_x_in1")]
    var_ok, rstd_ok, xn_ok = sem("a_var_ok"), sem("a_rstd_ok"), sem("a_xn_ok")
    turned, xnT_ok, logits_ok, exp_ok = sem("a_turned"), sem("a_xnT_ok"), sem("a_logits_ok"), sem("a_exp_ok")
    takes_ok, ranks_ok, rank_read = sem("a_takes_ok"), sem("a_ranks_ok"), sem("a_rank_read")
    xn_out, xnT_out, zeros_ok, zero_out = [sem("a_xn_out0"), sem("a_xn_out1")], [sem("a_xnT_out0"), sem("a_xnT_out1")], sem("a_zeros_ok"), k.zero_out
    dve_own = sem("a_dve_own")

    turn_bank = [ [k.ps[0], k.ps[1]], [k.ps[2], k.ps[3]] ]
    logits = [k.ps[4], k.ps[5]]
    ranks = [k.ps[6], k.ps[7]]
    x_v = k.io["x"].rearrange("(c t p) d -> c p t d", p=P, t=TP)
    xn_v = k.dram["xn"].rearrange("(c t p) d -> c p t d", p=P, t=TP)
    xnT_v = k.dram["xnT"].rearrange("(f p) (c n) -> c p f n", p=P, n=CH)

    with nc.Block() as block:

        @block.sync
        def _(sp):
            consts = [(k.ident, "ident"), (k.upto, "upto"), (k.ones, "ones"), (k.iota, "iota"),
                      (k.before_bf, "before_bf"), (k.ones_bf, "ones_bf"), (k.power, "power")]
            for u in range(2):
                sp.dma_start(x_t[:, u], x_v[u]).then_inc(x_in[u], 16)
            for tile, name in consts:
                sp.dma_start(tile[:], k.io[name]).then_inc(k.consts_in, 16)
            sp.dma_start(gate_w[:], k.io["gate_w0"].rearrange("(f p) e -> p f e", p=P)).then_inc(w_in, 16)
            sp.dma_start(bias[:], k.io["bias0"]).then_inc(w_in, 16)
            sp.wait_ge(zeros_ok, 1)
            zv = k.dram["xg"].rearrange("(z p r) d -> z p (r d)", p=P, r=8)
            for z in range(SLOTS // (8 * P)):
                sp.dma_start(zv[z], zeros[:, 0:8 * D]).then_inc(zero_out, 16)

            def stores(c, u):
                sp.wait_ge(xn_ok, TP * c + TP)
                sp.dma_start(xn_v[c], xn[:, u]).then_inc(xn_out[u], 16)
                sp.wait_ge(xnT_ok, KT * c + KT)
                sp.dma_start(xnT_v[c], xnT[:, u]).then_inc(xnT_out[u], 16)

            with sp.Fori(0, NCH // 2 - 1) as i:
                for u in range(2):
                    c = 2 * i + u
                    sp.wait_ge(xn_ok, TP * c + TP)
                    sp.dma_start(x_t[:, u], x_v[c + 2]).then_inc(x_in[u], 16)
                    stores(c, u)
            for u in range(2):
                stores(NCH - 2 + u, u)
            for u in range(2):
                sp.wait_ge(xn_out[u], 16 * NCH // 2)
                sp.wait_ge(xnT_out[u], 16 * NCH // 2)

        @block.gpsimd
        def _(pool):
            nc.gpsimd.memset(zeros[:], 0.0).then_inc(zeros_ok, 1)
            pool.wait_ge(k.consts_in, k.NCONST)
            with pool.Fori(0, NCH // 2) as i:
                for u in range(2):
                    c = 2 * i + u
                    pool.wait_ge(var_ok, c + 1)
                    nc.gpsimd.tensor_tensor(rstd[:, u], var[:, u], k.power[:, 0:TP], ALU.pow).then_inc(rstd_ok, 1)

        @block.scalar
        def _(act):
            with act.Fori(0, NCH // 2) as i:
                for u in range(2):
                    c = 2 * i + u
                    for f in range(KT):
                        act.wait_ge(turned, KT * c + f + 1)
                        act.wait_ge(xnT_out[u], 16 * i)
                        nc.scalar.activation(xnT[:, u, f], turn_bank[u][f][:], ACT.Copy).then_inc(xnT_ok, 1)
                    act.wait_ge(logits_ok, c + 1)
                    act.wait_ge(dve_own, k.DVE_A * c)
                    nc.scalar.activation(expn[:], logits[u][:, 0:TP * E], ACT.Exp, scale=-1.0).then_inc(exp_ok, 1)

        @block.tensor
        def _(pe):
            pe.wait_ge(k.consts_in, k.NCONST)
            pe.wait_ge(w_in, 32)
            with pe.Fori(0, NCH // 2) as i:
                for u in range(2):
                    c = 2 * i + u
                    pe.wait_ge(xnT_ok, KT * c)
                    for f in range(KT):
                        for t in range(TP):
                            pe.wait_ge(xn_ok, TP * c + t + 1)
                            m = nc.tensor.transpose(turn_bank[u][f][:, t * P:(t + 1) * P],
                                                    xn[:, u, t, f * P:(f + 1) * P], k.ident[:])
                        m.then_inc(turned, 1)
                    pe.wait_ge(xnT_ok, KT * c + KT)
                    for t in range(TP):
                        for f in range(KT):
                            m = nc.tensor.matmul(logits[u][:, t * E:(t + 1) * E], xnT[:, u, f, t * P:(t + 1) * P],
                                                 gate_w[:, f], start=(f == 0), stop=(f == KT - 1))
                    m.then_inc(logits_ok, 1)
                    pe.wait_ge(takes_ok, c + 1)
                    for t in range(TP + 1):
                        o = ranks[u][:, t * E:(t + 1) * E]
                        for s in range(min(t + 1, TP)):
                            m = nc.tensor.matmul(o, (k.before_bf if s == t else k.ones_bf)[:], takes[:, u, s],
                                                 start=(s == 0), stop=(s == min(t, TP - 1)))
                    m.then_inc(ranks_ok, 1)

        @block.vector
        def _(dve):
            v = nc.vector
            own = Chain(dve, dve_own, k.DVE_A, sem("a_stand"))
            dve.wait_ge(k.consts_in, k.NCONST)
            dve.wait_ge(w_in, 32)
            with nc.allow_low_precision("0 and 1 are exact in bf16"):
                v.memset(count[:], 0.0)
                v.memset(beats[:], 0.0)
                with dve.Fori(0, NCH // 2) as i:
                    for u in range(2):
                        c = 2 * i + u
                        own.begin(c)
                        dve.wait_ge(x_in[u], 16 * i + 16)
                        for t in range(TP):
                            ins = v.bn_stats(stats[:, t], x_t[:, u, t])
                        own.link(ins, apart=True)
                        for t in range(TP - 1):
                            v.bn_aggr(mv[:, t], stats[:, t])
                        own.link(v.bn_aggr(mv[:, TP - 1], stats[:, TP - 1]))
                        v.tensor_scalar(var[:, u], mv[:, :, 1], LN_EPS, None, ALU.add).then_inc(var_ok, 1)
                        dve.wait_ge(rstd_ok, c + 1)
                        dve.wait_ge(xn_out[u], 16 * i)
                        dve.wait_ge(turned, KT * c)
                        for t in range(TP):
                            v.tensor_scalar(xn[:, u, t], x_t[:, u, t], mv[:, t, 0:1], rstd[:, u, t:t + 1],
                                            ALU.subtract, ALU.mult).then_inc(xn_ok, 1)
                        dve.wait_ge(exp_ok, c + 1)
                        own.link(v.tensor_scalar(biased[:].rearrange("p t e -> p (t e)"), expn[:], 1.0, None, ALU.add))
                        own.link(v.reciprocal(score[:], biased[:]))
                        own.link(v.tensor_tensor(biased[:], score[:], bias[:].unsqueeze(1).to_broadcast([P, TP, E]), ALU.add), apart=True)
                        grouped = biased[:].rearrange("p t (g e) -> p (t g) e", e=EG)
                        for g in range(TP * G0):
                            ins = v.max(top8g[:, g], grouped[:, g])
                        own.link(ins)
                        own.link(v.tensor_tensor(gscore[:].rearrange("p t g -> p (t g)"), top8g[:, :, 0], top8g[:, :, 1], ALU.add))
                        for g in range(G0):
                            for lo, hi, op in ((0, g, ALU.is_ge), (g + 1, G0, ALU.is_gt)):
                                if lo < hi:
                                    ins = v.tensor_tensor(beats[:, :, g, lo:hi], gscore[:, :, lo:hi],
                                                          gscore[:, :, g:g + 1].to_broadcast([P, TP, hi - lo]), op)
                        own.link(ins)
                        own.link(v.tensor_reduce(gmask[:], beats[:], AX, ALU.add))
                        own.link(v.tensor_scalar(gmask[:], gmask[:], 2.0, None, ALU.is_lt))
                        own.link(v.tensor_tensor(biased[:].rearrange("p t (g e) -> p (t g) e", e=EG), grouped,
                                                 gmask[:].rearrange("p t g -> p (t g)").unsqueeze(2).to_broadcast([P, TP * G0, EG]), ALU.mult), apart=True)
                        choose(nc, k, own, c, u, E, K, biased, score, top8, index8, chosen, onehot, picked, weight,
                               takes, takes_ok, ranks_ok, ranks, rank, count)
                        own.link(v.tensor_reduce(wsum[:], weight[:], AX, ALU.add))
                        own.link(v.tensor_scalar(wsum[:], wsum[:], 1e-20, None, ALU.add))
                        own.link(v.reciprocal(wsum[:], wsum[:]))
                        own.link(v.scalar_tensor_tensor(k.weight_of[:, bass.ds(c * TP * K, TP * K)].rearrange("p (t k) -> p t k", k=K),
                                                        weight[:], SCALE0, wsum[:].unsqueeze(2).to_broadcast([P, TP, K]), ALU.mult, ALU.mult))
                        own.end()
                last = Chain(dve, sem("a_dve_last"), 0)
                last.link(v.tensor_scalar(blocks_i[:], count[:], float(P - 1), None, ALU.add))
                last.link(v.tensor_scalar(blocks_i[:], blocks_i[:], 7, None, ALU.arith_shift_right))
                last.link(v.tensor_copy(blocks[:], blocks_i[:]))
                last.link(v.tensor_tensor_scan(upto_blocks[:], k.ones[:, 0:E], blocks[:], 0.0, ALU.mult, ALU.add))
                last.link(v.tensor_tensor(start[:], upto_blocks[:], blocks[:], ALU.subtract))
                last.link(v.tensor_scalar(start[:], start[:], float(P), None, ALU.mult))
                step = 40
                for j in range(0, NB, step):
                    w = wide[:].rearrange("p (j e) -> p j e", e=E)
                    last.link(v.tensor_tensor(w, upto_blocks[:].unsqueeze(1).to_broadcast([P, step, E]),
                                              k.iota[:, j:j + step].unsqueeze(2).to_broadcast([P, step, E]), ALU.is_le))
                    last.link(v.tensor_reduce(k.block_f[:, j:j + step], w, AX, ALU.add))
                last.link(v.tensor_scalar(k.block_expert[:], k.block_f[:], float(E - 1), None, ALU.min))
                for j in range(0, NT * K, 32):
                    w = wide[:, 0:32 * E].rearrange("p (j e) -> p j e", e=E)
                    last.link(v.tensor_tensor(w, k.iota[:, 0:E].unsqueeze(1).to_broadcast([P, 32, E]),
                                              k.expert_of[:, j:j + 32].unsqueeze(2).to_broadcast([P, 32, E]), ALU.is_equal))
                    last.link(v.tensor_tensor(w, w, start[:].unsqueeze(1).to_broadcast([P, 32, E]), ALU.mult))
                    last.link(v.tensor_reduce(k.block_f[:, 0:32], w, AX, ALU.add))
                    last.link(v.tensor_tensor(k.slot_of[:, j:j + 32], k.block_f[:, 0:32], k.rank_of[:, j:j + 32], ALU.add))


def choose(nc, k, own, c, u, E, K, biased, score, top8, index8, chosen, onehot, picked, weight, takes, takes_ok, ranks_ok, ranks, rank, count):
    v, dve = nc.vector, nc.vector
    for t in range(TP):
        ins = v.max(top8[:, t], biased[:, t])
    own.link(ins, apart=True)
    for t in range(TP):
        ins = v.max_index(index8[:, t], top8[:, t], biased[:, t])
    own.link(ins)
    own.link(v.tensor_copy(chosen[:], index8[:, :, 0:K]))
    v.tensor_copy(k.expert_of[:, bass.ds(c * TP * K, TP * K)].rearrange("p (t k) -> p t k", k=K), chosen[:])
    own.link(v.tensor_tensor(onehot[:], k.iota[:, 0:E].unsqueeze(1).unsqueeze(1).to_broadcast([P, TP, K, E]),
                             chosen[:].unsqueeze(3).to_broadcast([P, TP, K, E]), ALU.is_equal))
    v.tensor_reduce(takes[:, u], onehot[:].rearrange("p t k e -> p t e k"), AX, ALU.add).then_inc(takes_ok, 1)
    own.link(v.tensor_tensor(picked[:], onehot[:], score[:].unsqueeze(2).to_broadcast([P, TP, K, E]), ALU.mult))
    own.link(v.tensor_reduce(weight[:], picked[:], AX, ALU.add))
    dve.wait_ge(ranks_ok, c + 1)
    own.link(v.tensor_tensor(rank[:], ranks[u][:, 0:TP * E].rearrange("p (t e) -> p t e", e=E),
                             count[:].unsqueeze(1).to_broadcast([P, TP, E]), ALU.add))
    own.link(v.tensor_tensor(count[:], count[:], ranks[u][:, TP * E:TP * E + E], ALU.add))
    own.link(v.tensor_tensor(picked[:], onehot[:], rank[:].unsqueeze(2).to_broadcast([P, TP, K, E]), ALU.mult))
    own.link(v.tensor_reduce(k.rank_of[:, bass.ds(c * TP * K, TP * K)].rearrange("p (t k) -> p t k", k=K), picked[:], AX, ALU.add))


def mix_tokens(nc, k, st):
    sem, sb = k.sem, lambda name, shape, dt=F32: k.sb(st, name, shape, dt)
    x_t = sb("m_x", [P, 2, TP, D])
    xn = sb("m_xn", [P, 2, TP, D])
    xnT = sb("m_xnT", [P, 2, KT, CH])
    w_qkv = sb("m_w_qkv", [P, KT, 3 * D])
    w_ug = sb("m_w_ug", [P, KT, 2 * UG])
    w_out = sb("m_w_out", [P, UG // P, D])
    w_su = sb("m_w_su", [P, KT, SI])
    w_sd = sb("m_w_sd", [P, SI // P, D])
    squares = sb("m_squares", [P, TP, D])
    squares_qk = sb("m_squares_qk", [P, 2, D])
    ssx = sb("m_ssx", [P, TP])
    rms = sb("m_rms", [P, 2, TP])
    rms_sq = sb("m_rms_sq", [P, 2, TP])
    rms_pm = sb("m_rms_pm", [P, 2, TP, 2])
    ssqk = sb("m_ssqk", [P, 2])
    qk_mean = sb("m_qk_mean", [P, 2])
    qk_pow = sb("m_qk_pow", [P, 2])
    qk_scale = sb("m_qk_scale", [P, 2])
    eq = sb("m_eq", [P, TP, D])
    wv = sb("m_wv", [P, TP, 2 * D])
    den = sb("m_den", [P, D])
    y = sb("m_y", [P, TP, D])
    yT = sb("m_yT", [P, KT, CH])
    gate = sb("m_gate", [P, 2, CH])
    gated = sb("m_gated", [P, 2, CH])
    h = sb("m_h", [P, 3, CH])
    slots = sb("m_slots", [P, 2, TP * TOP0], I32)

    NS, SW = UG // P + SI // P, UG // P
    w_in = sem("m_w_in")
    x_in, xnT_in = [sem("m_x_in0"), sem("m_x_in1")], [sem("m_xnT_in0"), sem("m_xnT_in1")]
    up_ok, gate_ok, h_ok, down_ok = sem("m_up_ok"), sem("m_gate_ok"), sem("m_h_ok"), sem("m_down_ok")
    xx_ok, res_ok, r_out = sem("m_xx_ok"), sem("m_res_ok"), [sem("m_r_out0"), sem("m_r_out1")]
    ssx_ok, mean_ok, pow_ok, rms_ok = sem("m_ssx_ok"), sem("m_mean_ok"), sem("m_pow_ok"), sem("m_rms_ok")
    prep_mm, prep_read = sem("m_prep_mm"), sem("m_prep_read")
    ss_ok, qkm_ok, qkp_ok, scale_ok = sem("m_ss_ok"), sem("m_qkm_ok"), sem("m_qkp_ok"), sem("m_scale_ok")
    exp_ok, eq1_ok, yT_ok = sem("m_exp_ok"), sem("m_eq1_ok"), sem("m_yT_ok")
    dve_s, dve_p = sem("m_dve_s"), sem("m_dve_p")
    slots_ok, scattered, stand = sem("m_slots_ok"), [sem("m_scattered0"), sem("m_scattered1")], sem("m_stand")

    acc = [k.ps[0], k.ps[1]]
    stream = [[k.ps[2], k.ps[3]], [k.ps[4], k.ps[5]]]
    prep_a, prep_b = k.ps[6], k.ps[7]
    x_v = k.io["x"].rearrange("(c t p) d -> c p t d", p=P, t=TP)
    xn_v = k.dram["xn"].rearrange("(c t p) d -> c p t d", p=P, t=TP)
    r_v = k.dram["r"].rearrange("(c t p) d -> c p t d", p=P, t=TP)
    xnT_v = k.dram["xnT"].rearrange("(f p) (c n) -> c p f n", p=P, n=CH)
    QKV = {1: 0, 2: 1, 5: 2, 6: 3}
    CUM = {3: 0, 4: 1, 7: 2, 8: 3}
    ORDER = {1: 0, 2: 1, 3: 2, 4: 3, 5: 4, 6: 5, 7: 6, 8: 7, 10: 8}

    def chunks(eng, body, prologue):
        prologue()
        with eng.Fori(0, NCH // 2 - 1) as i:
            for u in range(2):
                body(2 * i + u, i, u, True)
        for u in range(2):
            body(NCH - 2 + u, NCH // 2 - 1, u, u == 0)

    with nc.Block() as block:

        @block.sync
        def _(sp):
            def load(c, u):
                sp.dma_start(xnT[:, u], xnT_v[c]).then_inc(xnT_in[u], 16)
                sp.dma_start(xn[:, u], xn_v[c]).then_inc(x_in[u], 16)
                sp.dma_start(x_t[:, u], x_v[c]).then_inc(x_in[u], 16)

            load(0, 0)
            sp.dma_start(w_qkv[:], k.io["w_qkv"].rearrange("(f p) n -> p f n", p=P)).then_inc(w_in, 16)
            sp.dma_start(w_ug[:], k.io["w_ug"].rearrange("(f p) n -> p f n", p=P)).then_inc(w_in, 16)
            sp.dma_start(w_out[:], k.io["w_out"].rearrange("(f p) n -> p f n", p=P)).then_inc(w_in, 16)
            load(1, 1)
            sp.dma_start(w_su[:], k.io["w_su"].rearrange("(f p) n -> p f n", p=P)).then_inc(w_in, 16)
            sp.dma_start(w_sd[:], k.io["w_sd"].rearrange("(f p) n -> p f n", p=P)).then_inc(w_in, 16)

            def body(c, i, u, more):
                sp.wait_ge(res_ok, 2 * c + 2)
                sp.dma_start(r_v[c], x_t[:, u]).then_inc(r_out[u], 16)

            with sp.Fori(0, NCH // 2 - 1) as i:
                for u in range(2):
                    c = 2 * i + u
                    body(c, i, u, True)
                    sp.wait_ge(r_out[u], 16 * i + 16)
                    sp.wait_ge(up_ok, NS * c + NS)
                    sp.wait_ge(scattered[u], 16 * TP * TOP0 * (i + 1))
                    load(c + 2, u)
                    if u == 0:
                        pass
            for u in range(2):
                body(NCH - 2 + u, 0, u, False)
            n_load = 0
            for e in range(0, E0, 8):
                sp.dma_start(k.wu[:, e:e + 8], k.io["wu"][:, e:e + 8]).then_inc(k.experts_in, 16)
                sp.dma_start(k.wd[:, e:e + 8], k.io["wd"][:, e:e + 8]).then_inc(k.experts_in, 16)
                n_load += 32
            assert n_load == k.NEXPERTS
            for u in range(2):
                sp.wait_ge(r_out[u], 16 * NCH // 2)
                sp.wait_ge(scattered[u], 16 * TP * TOP0 * NCH // 2)

        @block.gpsimd
        def _(pool):
            g = nc.gpsimd

            def norm(n, u, i):
                pool.wait_ge(mean_ok, n + 1)
                g.tensor_tensor(rms[:, u], rms[:, u], k.power[:, 0:TP], ALU.pow).then_inc(pow_ok, 1)

            def qkv(n, t, u):
                pool.wait_ge(qkm_ok, TP * n + t + 1)
                g.tensor_tensor(qk_pow[:], qk_mean[:], k.power[:, 0:2], ALU.pow).then_inc(qkp_ok, 1)
                pool.wait_ge(exp_ok, TP * n + t + 1)
                pool.sem_inc(stand, 1)
                g.tensor_scalar(eq[:, t], eq[:, t], 1.0, None, ALU.add).then_inc(eq1_ok, 1)

            def prologue():
                norm(0, 0, 0)
                for t in range(TP):
                    qkv(0, t, 0)
                pool.wait_ge(k.zero_out, k.NZERO)

            def body(c, i, u, more):
                pool.wait_ge(x_in[u], 32 * i + 32)
                g.tensor_copy(slots[:, u], k.slot_of[:, bass.ds(c * TP * TOP0, TP * TOP0)] if not isinstance(c, int)
                              else k.slot_of[:, c * TP * TOP0:(c + 1) * TP * TOP0]).then_inc(slots_ok, 1)
                g.tensor_tensor(x_t[:, u], x_t[:, u], xn[:, u], ALU.add).then_inc(xx_ok, 1)
                pool.wait_ge(slots_ok, c + 1)
                pool.sem_inc(stand, 1)
                if more:
                    norm(c + 1, 1 - u, i)
                done = 0
                for s in range(NS):
                    if more and s in QKV:
                        qkv(c + 1, QKV[s], 1 - u)
                        pool.sem_inc(stand, 1)
                    for _ in range(2):
                        if done < TP * TOP0:
                            t, j = divmod(done, TOP0)
                            g.indirect_dma_start(k.dram["xg"], bass.IndirectOffsetOnAxis(ap=slots[:, u, done:done + 1], axis=0),
                                                 xn[:, u, t], None).then_inc(scattered[u], 16)
                            done += 1
                assert done == TP * TOP0

            chunks(pool, body, prologue)

        @block.scalar
        def _(act):
            a = nc.scalar

            def norm(n, u, i, load):
                act.wait_ge(x_in[u], load)
                act.wait_ge(mean_ok, n)
                for t in range(TP):
                    ins = a.activation(squares[:, t], xn[:, u, t], ACT.Square, accum_out=ssx[:, t:t + 1])
                ins.then_inc(ssx_ok, 1)

            def qkv(n, t):
                act.wait_ge(prep_mm, 9 * n + {0: 1, 1: 2, 2: 5, 3: 6}[t])
                act.wait_ge(qkm_ok, TP * n + t)
                a.activation(squares_qk[:, 0], prep_a[:, 0:D], ACT.Square, accum_out=ssqk[:, 0:1])
                a.activation(squares_qk[:, 1], prep_a[:, D:2 * D], ACT.Square, accum_out=ssqk[:, 1:2]).then_inc(ss_ok, 1)
                act.wait_ge(scale_ok, TP * n + t + 1)
                act.wait_ge(prep_read, 8 * n)
                a.activation(eq[:, t], prep_a[:, 0:D], ACT.Exp, scale=qk_scale[:, 0:1])
                a.activation(wv[:, t, D:2 * D], prep_a[:, D:2 * D], ACT.Exp, scale=qk_scale[:, 1:2]).then_inc(exp_ok, 1)

            def turn(n):
                act.wait_ge(prep_mm, 9 * n + 9)
                for f in range(KT):
                    a.activation(yT[:, f], (prep_a, prep_b)[f][:], ACT.Copy).then_inc(yT_ok, 1)

            def prologue():
                norm(0, 0, 0, 32)
                for t in range(TP):
                    qkv(0, t)
                turn(0)

            def body(c, i, u, more):
                for s in range(NS):
                    act.wait_ge(up_ok, NS * c + s + 1)
                    if s < SW:
                        a.activation(gate[:, s % 2], stream[s % 2][1][:], ACT.Tanh, scale=0.5).then_inc(gate_ok, 1)
                    else:
                        a.activation(gate[:, s % 2], stream[s % 2][0][:], ACT.Relu).then_inc(gate_ok, 1)
                    if more and s == 0:
                        norm(c + 1, 1 - u, i, 32 * (i + 1 + u))
                    if more and s in QKV:
                        qkv(c + 1, QKV[s])
                    if more and s == 10:
                        turn(c + 1)

            chunks(act, body, prologue)

        @block.tensor
        def _(pe):
            t_ = nc.tensor

            def qkv(n, t, u, j):
                pe.wait_ge(prep_read, 8 * n + j)
                if j == 0:
                    pe.wait_ge(yT_ok, 2 * n)
                for f in range(KT):
                    t_.matmul(prep_a[:, 0:2 * D], xnT[:, u, f, t * P:(t + 1) * P], w_qkv[:, f, 0:2 * D], start=(f == 0), stop=(f == KT - 1))
                for f in range(KT):
                    m = t_.matmul(prep_b[:, 0:D], xnT[:, u, f, t * P:(t + 1) * P], w_qkv[:, f, 2 * D:3 * D], start=(f == 0), stop=(f == KT - 1))
                m.then_inc(prep_mm, 1)

            def cum(n, t, j):
                pe.wait_ge(prep_read, 8 * n + j)
                m = t_.matmul(prep_a[:], k.upto[:], wv[:, t], start=True, stop=(t % 2 == 0))
                if t % 2:
                    m = t_.matmul(prep_a[:], k.ones[:], wv[:, t - 1], start=False, stop=True)
                m.then_inc(prep_mm, 1)

            def turn(n):
                pe.wait_ge(prep_read, 8 * n + 8)
                for f in range(KT):
                    for t in range(TP):
                        m = t_.transpose((prep_a, prep_b)[f][:, t * P:(t + 1) * P], y[:, t, f * P:(f + 1) * P], k.ident[:])
                m.then_inc(prep_mm, 1)

            def prep(n, u, s):
                if s in QKV:
                    qkv(n, QKV[s], u, ORDER[s])
                if s in CUM:
                    cum(n, CUM[s], ORDER[s])
                if s == 10:
                    turn(n)

            def prologue():
                pe.wait_ge(w_in, 16 * 5)
                pe.wait_ge(xnT_in[0], 16)
                for s in sorted(ORDER):
                    prep(0, 0, s)

            def up(c, u, s):
                pe.wait_ge(h_ok, NS * c + max(s - 1, 0))
                if s == 0:
                    pe.wait_ge(yT_ok, 2 * c + 2)
                if s < SW:
                    for half in range(2):
                        for f in range(KT):
                            m = t_.matmul(stream[s % 2][half][:], w_ug[:, f, half * UG + s * P:half * UG + (s + 1) * P],
                                          yT[:, f], start=(f == 0), stop=(f == KT - 1))
                else:
                    for f in range(KT):
                        m = t_.matmul(stream[s % 2][0][:], w_su[:, f, (s - SW) * P:(s - SW + 1) * P], xnT[:, u, f],
                                      start=(f == 0), stop=(f == KT - 1))
                m.then_inc(up_ok, 1)

            def down(c, s):
                pe.wait_ge(h_ok, NS * c + s + 1)
                if s == 0:
                    pe.wait_ge(res_ok, 2 * c)
                w = w_out[:, s] if s < SW else w_sd[:, s - SW]
                for t in range(TP):
                    m = t_.matmul(acc[t // 2][:, (t % 2) * D:(t % 2 + 1) * D], h[:, s % 3, t * P:(t + 1) * P], w,
                                  start=(s == 0 and t % 2 == 0), stop=(s == NS - 1), skip_group_check=True)
                m.then_inc(down_ok, 1)

            def body(c, i, u, more):
                up(c, u, 0)
                if more:
                    pe.wait_ge(xnT_in[1 - u], 16 * (i + 1 + u))
                for s in range(1, NS):
                    up(c, u, s)
                    if more:
                        prep(c + 1, 1 - u, s)
                    down(c, s - 1)
                down(c, NS - 1)

            chunks(pe, body, prologue)

        @block.vector
        def _(dve):
            v = nc.vector
            own_s = Chain(dve, dve_s, SW)
            own_p = Chain(dve, dve_p, 1 + 2 * TP)

            def norm(n, u):
                own_p.begin(n)
                dve.wait_ge(ssx_ok, n + 1)
                v.tensor_scalar(rms[:, u], ssx[:], 1.0 / D, RMS_EPS, ALU.mult, ALU.add).then_inc(mean_ok, 1)
                dve.wait_ge(pow_ok, n + 1)
                own_p.link(v.tensor_tensor(rms_sq[:, u], rms[:, u], rms[:, u], ALU.mult))
                v.tensor_scalar(rms_sq[:, u], rms_sq[:, u], 1.0 / D, None, ALU.mult)
                v.tensor_scalar(rms_pm[:, u, :, 0], rms[:, u], -1.0, None, ALU.mult)
                v.tensor_copy(rms_pm[:, u, :, 1], rms[:, u]).then_inc(rms_ok, 1)

            def qkv(n, t, u):
                dve.wait_ge(ss_ok, TP * n + t + 1)
                dve.wait_ge(rms_ok, n + 1)
                v.tensor_scalar(qk_mean[:], ssqk[:], rms_sq[:, u, t:t + 1], RMS_EPS, ALU.mult, ALU.add).then_inc(qkm_ok, 1)
                dve.wait_ge(qkp_ok, TP * n + t + 1)
                v.tensor_tensor(qk_scale[:], qk_pow[:], rms_pm[:, u, t], ALU.mult).then_inc(scale_ok, 1)
                dve.wait_ge(exp_ok, TP * n + t + 1)
                v.scalar_tensor_tensor(wv[:, t, 0:D], prep_b[:, 0:D], rms[:, u, t:t + 1], wv[:, t, D:2 * D],
                                       ALU.mult, ALU.mult).then_inc(prep_read, 1)

            def cum(n, t):
                dve.wait_ge(prep_mm, 9 * n + {0: 3, 1: 4, 2: 7, 3: 8}[t])
                dve.wait_ge(eq1_ok, TP * n + t + 1)
                own_p.link(v.scalar_tensor_tensor(den[:], prep_a[:, D:2 * D], 1e-6, eq[:, t], ALU.add, ALU.mult))
                own_p.link(v.reciprocal(den[:], den[:]))
                if t == 0:
                    dve.wait_ge(yT_ok, 2 * n)
                v.tensor_tensor(y[:, t], prep_a[:, 0:D], den[:], ALU.mult).then_inc(prep_read, 1)

            def prologue():
                norm(0, 0)
                for s in sorted(ORDER):
                    if s in QKV:
                        qkv(0, QKV[s], 0)
                    if s in CUM:
                        cum(0, CUM[s])
                own_p.end()

            def body(c, i, u, more):
                own_s.begin(c)
                for s in range(NS):
                    dve.wait_ge(gate_ok, NS * c + s + 1)
                    if s < SW:
                        own_s.link(v.scalar_tensor_tensor(gated[:, s % 2], gate[:, s % 2], 1.0, stream[s % 2][1][:], ALU.add, ALU.mult))
                        dve.wait_ge(down_ok, NS * c + max(s - 2, 0))
                        v.scalar_tensor_tensor(h[:, s % 3], gated[:, s % 2], 0.5, stream[s % 2][0][:], ALU.mult, ALU.mult).then_inc(h_ok, 1)
                    else:
                        dve.wait_ge(down_ok, NS * c + s - 2)
                        v.tensor_tensor(h[:, s % 3], gate[:, s % 2], gate[:, s % 2], ALU.mult).then_inc(h_ok, 1)
                    if more and s == 0:
                        norm(c + 1, 1 - u)
                    if more and s in QKV:
                        qkv(c + 1, QKV[s], 1 - u)
                    if more and s in CUM:
                        cum(c + 1, CUM[s])
                own_s.end()
                dve.wait_ge(down_ok, NS * c + NS)
                dve.wait_ge(xx_ok, c + 1)
                for b in range(2):
                    x2 = x_t[:, u, 2 * b:2 * b + 2].rearrange("p t d -> p (t d)")
                    v.tensor_tensor(x2, x2, acc[b][:], ALU.add).then_inc(res_ok, 1)

            chunks(dve, body, prologue)


def expert_blocks(nc, k, st):
    sem, sb = k.sem, lambda name, shape, dt=F32: k.sb(st, name, shape, dt)
    RING = 3
    xg = sb("e_xg", [P, RING, 2, D])
    xgT = sb("e_xgT", [P, 2, 2, KT, P])
    r = sb("e_r", [P, 2, 2, I0])
    actT = sb("e_actT", [P, 2, 2, P])
    ys = sb("e_ys", [P, RING, 2, D])
    x_in = [sem(f"e_x_in{n}") for n in range(RING)]
    y_out = [sem(f"e_y_out{n}") for n in range(RING)]
    turned, xgT_ok, up_ok, r_ok = sem("e_turned"), sem("e_xgT_ok"), sem("e_up_ok"), sem("e_r_ok")
    back, actT_ok, down_ok, y_ok = sem("e_back"), sem("e_actT_ok"), sem("e_down_ok"), sem("e_y_ok")
    xg_v = k.dram["xg"].rearrange("(q b p) d -> q p b d", p=P, b=2)
    y_v = k.dram["y"].rearrange("(q b p) d -> q p b d", p=P, b=2)
    NQ = NB // 2
    STEPS = 6
    LOOPS = (NQ - 5) // STEPS

    def steps(eng, step):
        def one(q):
            step(q, q % STEPS, q // STEPS)
        one(0)
        one(1)
        with eng.Fori(0, LOOPS) as i:
            for j in range(2, STEPS + 2):
                step(STEPS * i + j, j % STEPS, i + j // STEPS)
        for q in range(LOOPS * STEPS + 2, NQ):
            one(q)

    def ring(rem, i, n):
        return i * (STEPS // RING) + (rem + n) // RING

    def wait(eng, s, value):
        if not isinstance(value, int) or value > 0:
            eng.wait_ge(s, value)

    def known(q, n):
        return not isinstance(q, int) or 0 <= q + n < NQ

    with nc.Block() as block:

        @block.sync
        def _(sp):
            def load(q, rem, i, n):
                b = (rem + n) % RING
                sp.dma_start(xg[:, b], xg_v[q + n]).then_inc(x_in[b], 16)

            def step(q, rem, i):
                if known(q, RING):
                    sp.wait_ge(turned, q + 1)
                    load(q, rem, i, RING)
                sp.wait_ge(y_ok, q + 1)
                sp.dma_start(y_v[q], ys[:, rem % RING]).then_inc(y_out[rem % RING], 16)

            for n in range(RING):
                load(0, 0, 0, n)
            steps(sp, step)
            for b in range(RING):
                sp.wait_ge(y_out[b], 16 * len(range(b, NQ, RING)))

        @block.tensor
        def _(pe):
            t_ = nc.tensor

            def turn(q, rem, i, n):
                b, two = (rem + n) % RING, (rem + n) % 2
                pe.wait_ge(x_in[b], 16 * ring(rem, i, n) + 16)
                wait(pe, xgT_ok, q + n - 1)
                for blk in range(2):
                    for f in range(KT):
                        o = (blk * KT + f) * P
                        m = t_.transpose(k.ps[two][:, o:o + P], xg[:, b, blk, f * P:(f + 1) * P], k.ident[:])
                m.then_inc(turned, 1)

            def expert(q, n, blk):
                at = 2 * (q + n) + blk
                here = k.block_expert[0:1, bass.ds(at, 1)] if not isinstance(at, int) else k.block_expert[0:1, at:at + 1]
                return pe.value_load(here, min_val=0, max_val=E0 - 1)

            def up(q, rem, i, n, experts):
                two = (rem + n) % 2
                pe.wait_ge(xgT_ok, q + n + 1)
                wait(pe, r_ok, q + n - 1)
                for blk in range(2):
                    e = experts[blk]
                    for f in range(KT):
                        m = t_.matmul(k.ps[2 + two][:, blk * I0:(blk + 1) * I0], xgT[:, two, blk, f],
                                      k.wu[:, bass.ds(e, 1), f].rearrange("p a i -> p (a i)"), start=(f == 0), stop=(f == KT - 1))
                m.then_inc(up_ok, 1)

            def turn_back(q, rem, i):
                two = rem % 2
                pe.wait_ge(r_ok, q + 1)
                wait(pe, actT_ok, q - 1)
                for blk in range(2):
                    m = t_.transpose(k.ps[4 + two][:, blk * P:(blk + 1) * P], r[:, two, blk], k.ident[:])
                m.then_inc(back, 1)

            def down(q, rem, i, n, experts):
                two = (rem + n) % 2
                pe.wait_ge(actT_ok, q + n + 1)
                wait(pe, y_ok, q + n - 1)
                for blk in range(2):
                    e = experts[blk]
                    m = t_.matmul(k.ps[6 + two][:, blk * D:(blk + 1) * D], actT[:, two, blk],
                                  k.wd[:, bass.ds(e, 1)].rearrange("p a d -> p (a d)"), start=True, stop=True)
                m.then_inc(down_ok, 1)

            def step(q, rem, i):
                before = [expert(q, -1, blk) for blk in range(2)] if known(q, -1) else None
                behind = [expert(q, 1, blk) for blk in range(2)] if known(q, 1) else None
                if before:
                    down(q, rem, i, -1, before)
                if known(q, 2):
                    turn(q, rem, i, 2)
                turn_back(q, rem, i)
                if behind:
                    up(q, rem, i, 1, behind)

            pe.wait_ge(k.experts_in, k.NEXPERTS)
            turn(0, 0, 0, 0)
            turn(0, 0, 0, 1)
            up(0, 0, 0, 0, [expert(0, 0, blk) for blk in range(2)])
            steps(pe, step)
            down(NQ - 1, (NQ - 1) % STEPS, (NQ - 1) // STEPS, 0, [expert(NQ - 1, 0, blk) for blk in range(2)])

        @block.vector
        def _(dve):
            v = nc.vector

            def turned_out(q, rem, i, n):
                two = (rem + n) % 2
                dve.wait_ge(turned, q + n + 1)
                wait(dve, up_ok, q + n - 1)
                v.tensor_copy(xgT[:, two].rearrange("p b f n -> p (b f n)"), k.ps[two][:]).then_inc(xgT_ok, 1)

            def result(q, rem, i, n):
                b, two = (rem + n) % RING, (rem + n) % 2
                dve.wait_ge(down_ok, q + n + 1)
                wait(dve, y_out[b], 16 * ring(rem, i, n))
                v.tensor_copy(ys[:, b].rearrange("p b d -> p (b d)"), k.ps[6 + two][:]).then_inc(y_ok, 1)

            def step(q, rem, i):
                if known(q, -1):
                    result(q, rem, i, -1)
                if known(q, 2):
                    turned_out(q, rem, i, 2)

            turned_out(0, 0, 0, 0)
            turned_out(0, 0, 0, 1)
            steps(dve, step)
            result(NQ - 1, (NQ - 1) % STEPS, (NQ - 1) // STEPS, 0)

        @block.scalar
        def _(act):
            a = nc.scalar

            def relu(q, rem, i, n):
                two = (rem + n) % 2
                act.wait_ge(up_ok, q + n + 1)
                wait(act, back, q + n - 1)
                a.activation(r[:, two].rearrange("p b i -> p (b i)"), k.ps[2 + two][:, 0:2 * I0], ACT.Relu).then_inc(r_ok, 1)

            def square(q, rem, i):
                two = rem % 2
                act.wait_ge(back, q + 1)
                wait(act, down_ok, q - 1)
                a.activation(actT[:, two].rearrange("p b n -> p (b n)"), k.ps[4 + two][:, 0:2 * P], ACT.Square).then_inc(actT_ok, 1)

            def step(q, rem, i):
                square(q, rem, i)
                if known(q, 1):
                    relu(q, rem, i, 1)

            relu(0, 0, 0, 0)
            steps(act, step)


class Banks:

    def __init__(self, sem, tag, plan):
        self.at, self.per_round = {}, [0] * 8
        for name, bank in plan:
            assert name not in self.at, name
            self.at[name] = bank, self.per_round[bank]
            self.per_round[bank] += 1
        self.filled = [sem(f"{tag}_filled{b}") for b in range(8)]
        self.drained = [sem(f"{tag}_drained{b}") for b in range(8)]

    def fill(self, eng, name, c):
        bank, nth = self.at[name]
        eng.wait_ge(self.drained[bank], c * self.per_round[bank] + nth)
        return bank

    def full(self, ins, name):
        ins.then_inc(self.filled[self.at[name][0]], 1)

    def read(self, eng, name, c):
        bank, nth = self.at[name]
        eng.wait_ge(self.filled[bank], c * self.per_round[bank] + nth + 1)
        return bank

    def drain(self, ins, name):
        ins.then_inc(self.drained[self.at[name][0]], 1)

    def passed(self, eng, name, c):
        bank, nth = self.at[name]
        eng.wait_ge(self.drained[bank], c * self.per_round[bank] + nth + 1)

    def rounds(self, eng, name, c):
        bank, _ = self.at[name]
        eng.wait_ge(self.filled[bank], c * self.per_round[bank])


def load_layer1(nc, k, pool):
    g = nc.gpsimd
    n = 0
    for f in range(KT):
        for tile in (k.w1, k.w3):
            g.memset(tile[:, f, ROWS1:SLOTS1 * P].bitcast(F32), 0.0)
    g.memset(k.w2[:, SLOTS1 - 1].bitcast(F32), 0.0).then_inc(k.padded, 1)
    pool.wait_ge(k.padded, 1)
    for f in range(KT):
        for tile, name in ((k.w1, "w1"), (k.w3, "w3")):
            g.dma_start(tile[:, f, 0:ROWS1], k.io[name][f * P:(f + 1) * P]).then_inc(k.layer1_in, 16)
            n += 16
    full = ROWS1 // P
    g.dma_start(k.w2[:, 0:full], k.io["w2"][0:full * P].rearrange("(s p) d -> p s d", p=P)).then_inc(k.layer1_in, 16)
    g.dma_start(k.w2[0:ROWS1 - full * P, full], k.io["w2"][full * P:ROWS1]).then_inc(k.layer1_in, 16)
    assert n + 32 == k.NLAYER1


def layer1(nc, k, st):
    sem, sb = k.sem, lambda name, shape, dt=F32: k.sb(st, name, shape, dt)
    K = TOP0
    yk = sb("l_yk", [P, TP, K, D])
    x1 = sb("l_x1", [P, TP, D])
    xn = sb("l_xn", [P, TP, D])
    slots = sb("l_slots", [P, TP * K], I32)
    w4 = sb("l_w4", [P, TP * K])
    stats = sb("l_stats", [P, TP, 6])
    mv = sb("l_mv", [P, TP, 2])
    var = sb("l_var", [P, TP])
    rstd = sb("l_rstd", [P, TP])
    ssx = sb("l_ssx", [P, TP])
    ms = sb("l_ms", [P, TP])
    rms = sb("l_rms", [P, TP])
    xh = sb("l_xh", [P, KT, CH], F32R)
    xl = sb("l_xl", [P, KT, CH], F32R)
    wqh, wql = sb("l_wqh", [P, KT, D], F32R), sb("l_wql", [P, KT, D], F32R)
    woh, wol = sb("l_woh", [P, KT, D], F32R), sb("l_wol", [P, KT, D], F32R)
    rms_w = sb("l_rms_w", [P, KT])
    bq, bo = sb("l_bq", [P, D]), sb("l_bo", [P, D])
    gate_w = sb("l_gate_w", [P, KT, E1])
    gate_b = sb("l_gate_b", [P, E1])
    root = sb("l_root", [P, TP * E1])
    absx, expx, wplus, lnw, zero, dif, score, biased = (sb(f"l_g{n}", [P, TP, E1]) for n in range(8))
    spos = sb("l_spos", [P, TP, E1])
    top8 = sb("l_top8", [P, TP, 8])
    index8 = sb("l_index8", [P, TP, 8], U32)
    chosen = sb("l_chosen", [P, TP, TOP1])
    onehot = sb("l_onehot", [P, TP, E1])
    onehot2 = sb("l_onehot2", [P, TP, E1])
    cw = sb("l_cw", [P, TP, E1])
    cwT = sb("l_cwT", [E1, CH])
    cb = sb("l_cb", [P, ROUTED1, CH])
    v_aug = sb("l_v", [P, TP, H1, DK + 1])
    cos, sin = sb("l_cos", [P, TP, DK]), sb("l_sin", [P, TP, DK])
    qr = sb("l_qr", [P, TP, H1, DK])
    rot = sb("l_rot", [P, TP, H1, DK])
    squares = rot[:].rearrange("p t h d -> p t (h d)")
    qa = sb("l_qa", [P, 2, H1, 64], F32R)
    kb = sb("l_kb", [P, 2, H1, 64], F32R)
    qaT = sb("l_qaT", [P, H1 // 2, S1], F32R)
    kbT = sb("l_kbT", [P, H1 // 2, S1], F32R)
    mx = sb("l_mx", [P, 2, 2, H1 // 2])
    pt0 = sb("l_pt0", [P, 2, 4, S1])
    wq = pt0[:, 0].rearrange("p (f a) n -> p f (a n)", f=KT)[:, :, 0:D]
    wo = pt0[:, 1].rearrange("p (f a) n -> p f (a n)", f=KT)[:, :, 0:D]
    pt1 = sb("l_pt1", [P, 2, 4, P])
    rsum = sb("l_rsum", [P, 2, H1])
    on = sb("l_on", [P, 2, D])
    oh, ol = sb("l_oh", [P, KT, CH], F32R), sb("l_ol", [P, KT, CH], F32R)
    mask1, mask2, ident_bf = sb("l_mask1", [P, P], BF16), sb("l_mask2", [P, P], BF16), sb("l_ident_bf", [P, P], BF16)
    gate, gated = sb("l_gate", [P, 2, CH]), sb("l_gated", [P, 2, CH])
    h1, hc = sb("l_h1", [P, CH]), sb("l_hc", [P, 2, CH])
    hh, hl = sb("l_hh", [P, 2, CH], F32R), sb("l_hl", [P, 2, CH], F32R)

    plan, turn = [], [0]

    def put(name):
        plan.append((name, 2 + turn[0] % 6))
        turn[0] += 1

    for f in range(KT):
        put(f"x{f}")
    put("logits")
    for t in range(TP):
        put(f"q{t}")
    put("cw")
    GROUPS = [(g, kind, hh_, pp) for g in range(2) for kind, hh_, pp in
              [("two", 0, 0), ("two", 1, 0), ("two", 0, 1), ("two", 1, 1), ("four", 0, None), ("four", 1, None)]]
    for b in range(2):
        for side in ("kb", "qa"):
            for n in range(4):
                put(f"{side}{b}{n}")
        for n in range(12):
            put(f"s{b}{n}")
        for n in range(4):
            put(f"qm{b}{n}")
        for n in range(12):
            put(f"p{b}{n}")
        plan += [(f"o{b}0", 0), (f"o{b}1", 1)]
        put(f"oT{b}")
    for s in range(SLOTS1):
        put(f"a{s}")
        put(f"b{s}")
    plan += [("acc0", 0), ("acc1", 1)]
    banks = Banks(sem, "l", plan)

    consts, NCL = sem("l_consts"), 16 * 13
    r_in, y_in, slots_ok, out_st = sem("l_r_in"), sem("l_y_in"), sem("l_slots_ok"), sem("l_out")
    comb_ok, var_ok, rstd_ok, xn_ok = sem("l_comb_ok"), sem("l_var_ok"), sem("l_rstd_ok"), sem("l_xn_ok")
    ssx_ok, ms_ok, rms_ok, xh_ok = sem("l_ssx_ok"), sem("l_ms_ok"), sem("l_rms_ok"), sem("l_xh_ok")
    abs_ok, exp_ok, wplus_ok, ln_ok = sem("l_abs_ok"), sem("l_exp_ok"), sem("l_wplus_ok"), sem("l_ln_ok")
    sp_ok, score_ok, cw_ok = sem("l_sp_ok"), sem("l_score_ok"), sem("l_cw_ok")
    c_out, cb_in = sem("l_c_out"), sem("l_cb_in")
    rope_ok, hi_ok, lo_ok, mrow_ok = sem("l_rope_ok"), sem("l_hi_ok"), sem("l_lo_ok"), sem("l_mrow_ok")
    oh_ok = sem("l_oh_ok")
    prep_w, xx_ok = sem("l_prep_w"), sem("l_xx_ok")
    tanh_ok, h_ok, hh_ok, hl_ok, down_ok = sem("l_tanh_ok"), sem("l_h_ok"), sem("l_hh_ok"), sem("l_hl_ok"), sem("l_down_ok")
    dve_own, pool_own, dve_once, stand = sem("l_dve"), sem("l_pool"), sem("l_dve_once"), sem("l_stand")

    x_v = k.dram["r"].rearrange("(c t p) d -> c p t d", p=P, t=TP)
    out_v = k.out.rearrange("(c t p) d -> c p t d", p=P, t=TP)
    c_v = k.dram["cw"]
    ROWS = []
    for s in range(ROUTED1):
        p = 0
        while p < P:
            e = (s * P + p) // I1
            end = min(P, (e + 1) * I1 - s * P)
            ROWS.append((s, p, end, e))
            p = end

    with nc.Block() as block:

        @block.sync
        def _(sp):
            for tile, name in ((wq, "wq"), (wo, "wo"), (gate_w, "gate_w1")):
                sp.dma_start(tile if name != "gate_w1" else tile[:], k.io[name].rearrange("(f p) n -> p f n", p=P)).then_inc(consts, 16)
            for tile, name in ((rms_w, "rms_w"), (bq, "bq"), (bo, "bo"), (gate_b, "gate_b1"), (cos, "cos"), (sin, "sin"),
                               (mask1, "mask1"), (mask2, "mask2"), (ident_bf, "ident_bf")):
                sp.dma_start(tile[:], k.io[name]).then_inc(consts, 16)
            sp.dma_start(root[:], k.io["root"]).then_inc(consts, 16)
            with sp.Fori(0, NCH) as c:
                sp.wait_ge(out_st, 16 * c)
                sp.dma_start(x1[:], x_v[c]).then_inc(r_in, 16)
                banks.passed(sp, "cw", c)
                sp.dma_start(c_v[c], cwT[:]).then_inc(c_out, 16)
                sp.wait_ge(c_out, 16 * c + 16)
                sp.sem_inc(stand, 1)
                sp.wait_ge(h_ok, SLOTS1 * c)
                sp.sem_inc(stand, 1)
                for s, p, end, e in ROWS:
                    sp.dma_start(cb[p:end, s], c_v[c, e:e + 1].to_broadcast([end - p, CH])).then_inc(cb_in, 16)
                for n in range(2):
                    banks.passed(sp, f"acc{n}", c)
                sp.dma_start(out_v[c], x1[:]).then_inc(out_st, 16)
            sp.wait_ge(out_st, 16 * NCH)

        @block.gpsimd
        def _(pool):
            g = nc.gpsimd
            own = Chain(pool, pool_own, 3)
            load_layer1(nc, k, pool)

            def gather(c):
                at = k.slot_of[:, bass.ds(c * TP * K, TP * K)] if not isinstance(c, int) else k.slot_of[:, c * TP * K:(c + 1) * TP * K]
                pool.wait_ge(comb_ok, c)
                pool.sem_inc(stand, 1)
                g.tensor_copy(slots[:], at).then_inc(slots_ok, 1)
                pool.wait_ge(slots_ok, c + 1)
                pool.sem_inc(stand, 1)
                for t in range(TP):
                    for j in range(K):
                        n = t * K + j
                        g.indirect_dma_start(yk[:, t, j], None, k.dram["y"],
                                             bass.IndirectOffsetOnAxis(ap=slots[:, n:n + 1], axis=0)).then_inc(y_in, 16)

            def body(c, more):
                own.begin(c)
                pool.wait_ge(var_ok, c + 1)
                g.tensor_tensor(rstd[:], var[:], k.power[:, 0:TP], ALU.pow).then_inc(rstd_ok, 1)
                pool.wait_ge(ms_ok, c + 1)
                g.tensor_tensor(rms[:], ms[:], k.power[:, 0:TP], ALU.pow).then_inc(rms_ok, 1)
                own.link(g.tensor_tensor(x1[:], x1[:], xn[:], ALU.add))
                g.tensor_tensor(x1[:], x1[:], bo[:].unsqueeze(1).to_broadcast([P, TP, D]), ALU.add).then_inc(xx_ok, 1)
                pool.wait_ge(sp_ok, c + 1)
                g.tensor_tensor(score[:].rearrange("p t e -> p (t e)"), spos[:].rearrange("p t e -> p (t e)"),
                                root[:], ALU.pow).then_inc(score_ok, 1)
                banks.passed(pool, f"q{TP - 1}", c)
                vq = v_aug[:, :, :, 0:DK]
                half = DK // 2
                g.tensor_tensor(qr[:], vq, cos[:].unsqueeze(2).to_broadcast([P, TP, H1, DK]), ALU.mult)
                g.tensor_tensor(rot[:, :, :, 0:half], vq[:, :, :, half:DK], sin[:, :, 0:half].unsqueeze(2).to_broadcast([P, TP, H1, half]), ALU.mult)
                own.link(g.tensor_tensor(rot[:, :, :, half:DK], vq[:, :, :, 0:half], sin[:, :, half:DK].unsqueeze(2).to_broadcast([P, TP, H1, half]), ALU.mult))
                own.link(g.tensor_tensor(qr[:], qr[:], rot[:], ALU.add))
                pool.sem_inc(rope_ok, 1)
                own.end()
                if more:
                    gather(c + 1)
                for s in range(SLOTS1):
                    pool.wait_ge(hh_ok, SLOTS1 * c + s + 1)
                    pool.wait_ge(down_ok, (SLOTS1 - 1) * c + max(s - 1, 0))
                    g.tensor_tensor(hl[:, s % 2], hc[:, s % 2], hh[:, s % 2].bitcast(F32), ALU.subtract).then_inc(hl_ok, 1)

            gather(0)
            with pool.Fori(0, NCH - 1) as c:
                body(c, True)
            body(NCH - 1, False)

        @block.scalar
        def _(act):
            a = nc.scalar
            act.wait_ge(consts, NCL)
            with act.Fori(0, NCH) as c:
                act.wait_ge(xn_ok, TP * c + TP)
                act.wait_ge(ms_ok, c)
                for t in range(TP):
                    ins = a.activation(squares[:, t], xn[:, t], ACT.Square, accum_out=ssx[:, t:t + 1])
                ins.then_inc(ssx_ok, 1)
                for f in range(KT):
                    bank = banks.read(act, f"x{f}", c)
                    a.activation(xh[:, f], k.ps[bank][:], ACT.Copy).then_inc(xh_ok, 1)
                banks.passed(act, "logits", c)
                a.activation(expx[:], absx[:], ACT.Exp, scale=-1.0).then_inc(exp_ok, 1)
                act.wait_ge(wplus_ok, c + 1)
                a.activation(lnw[:], wplus[:], ACT.Ln).then_inc(ln_ok, 1)
                bank = banks.read(act, "cw", c)
                act.wait_ge(c_out, 16 * c)
                banks.drain(a.activation(cwT[:], k.ps[bank][0:E1, :], ACT.Copy), "cw")
                for b in range(2):
                    act.wait_ge(rope_ok, c + 1)
                    if b:
                        banks.read(act, f"qm{b - 1}3", c)
                    src = qr[:, 2 * b:2 * b + 2].rearrange("p t h d -> p (t h) d")
                    kbv = kb[:].rearrange("p t h d -> p (t h) d")
                    qav = qa[:].rearrange("p t h d -> p (t h) d")
                    for dst, lo in ((kbv, 0), (kbv, DK), (qav, 0), (qav, 2 * DK)):
                        a.activation(dst[:, :, lo:lo + DK], src, ACT.Copy).then_inc(hi_ok, 1)
                    for n in range(4):
                        bank = banks.read(act, f"kb{b}{n}", c)
                        banks.drain(a.activation(kbT[:, 2 * n:2 * n + 2].rearrange("p a n -> p (a n)"), k.ps[bank][:], ACT.Copy), f"kb{b}{n}")
                    for n, (g, kind, par, pp) in enumerate(GROUPS):
                        bank = banks.read(act, f"p{b}{n}", c)
                        dst = pt0[:, par, 2 * pp:2 * pp + 2] if kind == "two" else pt1[:, par]
                        banks.drain(a.activation(dst.rearrange("p a n -> p (a n)"), k.ps[bank][:], ACT.Exp, scale=DK ** -0.5), f"p{b}{n}")
                    bank = banks.read(act, f"oT{b}", c)
                    a.activation(oh[:, :, b * S1:(b + 1) * S1], k.ps[bank][:].rearrange("p (f n) -> p f n", f=KT), ACT.Copy).then_inc(oh_ok, 1)
                for s in range(SLOTS1):
                    bank = banks.read(act, f"a{s}", c)
                    a.activation(gate[:, s % 2], k.ps[bank][:], ACT.Tanh, scale=0.5).then_inc(tanh_ok, 1)
                    act.wait_ge(h_ok, SLOTS1 * c + s + 1)
                    act.wait_ge(down_ok, (SLOTS1 - 1) * c + max(s - 1, 0))
                    a.activation(hh[:, s % 2], hc[:, s % 2], ACT.Copy).then_inc(hh_ok, 1)

        @block.tensor
        def _(pe):
            t_ = nc.tensor
            pe.wait_ge(consts, NCL)
            pe.wait_ge(k.layer1_in, k.NLAYER1)
            pe.wait_ge(prep_w, 4)
            with pe.Fori(0, NCH) as c:
                pe.wait_ge(xn_ok, TP * c + TP)
                for f in range(KT):
                    bank = banks.fill(pe, f"x{f}", c)
                    for t in range(TP):
                        m = t_.transpose(k.ps[bank][:, t * P:(t + 1) * P], xn[:, t, f * P:(f + 1) * P], k.ident[:])
                    banks.full(m, f"x{f}")
                for f in range(KT):
                    banks.passed(pe, f"x{f}", c)
                bank = banks.fill(pe, "logits", c)
                for t in range(TP):
                    parts = [(x, f) for x in (xh, xl) for f in range(KT)]
                    for n, (x, f) in enumerate(parts):
                        m = t_.matmul(k.ps[bank][:, t * E1:(t + 1) * E1], x[:, f, t * P:(t + 1) * P].bitcast(F32), gate_w[:, f],
                                      start=(n == 0), stop=(n == len(parts) - 1))
                banks.full(m, "logits")

                def three(out, left, right, start, stop, **kw):
                    parts = [(l, r, f) for l, r in ((0, 0), (1, 0), (0, 1)) for f in range(KT)]
                    for n, (l, r, f) in enumerate(parts):
                        m = t_.matmul(out, left(l, f), right(r, f), start=(start and n == 0), stop=(stop and n == len(parts) - 1), **kw)
                    return m

                for t in range(TP):
                    bank = banks.fill(pe, f"q{t}", c)
                    m = three(k.ps[bank][:, 0:D], lambda l, f: (xh, xl)[l][:, f, t * P:(t + 1) * P],
                              lambda r, f: (wqh, wql)[r][:, f], True, True)
                    banks.full(m, f"q{t}")
                bank = banks.fill(pe, "cw", c)
                pe.wait_ge(cw_ok, c + 1)
                for t in range(TP):
                    m = t_.transpose(k.ps[bank][0:E1, t * P:(t + 1) * P], cw[:, t], k.ident[:])
                banks.full(m, "cw")
                for b in range(2):
                    cb_ = 2 * c + b

                    def sides(name, tile):
                        for n in range(4):
                            bank = banks.fill(pe, f"{name}{b}{n}", c)
                            for a in range(2):
                                for t in range(2):
                                    o = (a * 2 + t) * P
                                    pair = 2 * n + a
                                    m = t_.transpose(k.ps[bank][:, o:o + P], tile[:, t].bitcast(F32).rearrange("p h d -> p (h d)")[:, pair * P:(pair + 1) * P], k.ident[:])
                            banks.full(m, f"{name}{b}{n}")

                    def scores(name, first, K_, left, right, mask):
                        for n, (g, kind, par, pp) in enumerate(GROUPS):
                            bank = banks.fill(pe, f"{name}{b}{n}", c)
                            rows = slice(64 * par, 64 * par + K_)
                            if kind == "two":
                                for a in range(2):
                                    pair = 4 * g + 2 * pp + a
                                    lt, rt = first
                                    t_.matmul(k.ps[bank][:, a * S1:(a + 1) * S1], left[rows, pair, lt * P:(lt + 1) * P], right[rows, pair, rt:rt + S1],
                                              start=(a == 0), stop=False, skip_group_check=True)
                                o = 0 if lt == 0 else P
                                m = t_.matmul(k.ps[bank][:].rearrange("p (a n) -> p a n", a=2)[:, :, o:o + P], ident_bf[:],
                                              mask[:].unsqueeze(1).to_broadcast([P, 2, P]), start=False, stop=True, skip_group_check=True)
                            else:
                                t = 1 - lt
                                for a in range(4):
                                    pair = 4 * g + a
                                    t_.matmul(k.ps[bank][:, a * P:(a + 1) * P], left[rows, pair, t * P:(t + 1) * P], right[rows, pair, t * P:(t + 1) * P],
                                              start=(a == 0), stop=False, skip_group_check=True)
                                m = t_.matmul(k.ps[bank][:].rearrange("p (a n) -> p a n", a=4), ident_bf[:],
                                              mask[:].unsqueeze(1).to_broadcast([P, 4, P]), start=False, stop=True, skip_group_check=True)
                            banks.full(m, f"{name}{b}{n}")
                            if name == "p" and n % 6 == 5:
                                values(g)

                    def values(g):
                        for n in range(6):
                            banks.passed(pe, f"p{b}{6 * g + n}", c)
                        if g == 0:
                            for t in range(2):
                                banks.fill(pe, f"o{b}{t}", c)
                        for a in range(4):
                            for par in range(2):
                                head = 2 * (4 * g + a) + par
                                o = slice(head * (DK + 1), (head + 1) * (DK + 1))
                                v0, v1 = v_aug[:, 2 * b, head], v_aug[:, 2 * b + 1, head]
                                m0 = t_.matmul(k.ps[0][:, o], pt0[:, par, a, 0:P], v0, start=True, stop=True)
                                t_.matmul(k.ps[1][:, o], pt0[:, par, a, P:S1], v0, start=True, stop=False)
                                m1 = t_.matmul(k.ps[1][:, o], pt1[:, par, a], v1, start=False, stop=True)
                        if g == 1:
                            banks.full(m0, f"o{b}0")
                            banks.full(m1, f"o{b}1")

                    pe.wait_ge(hi_ok, 4 * cb_ + 4)
                    pe.wait_ge(lo_ok, 2 * cb_ + 2)
                    sides("kb", kb)
                    sides("qa", qa)
                    for n in range(4):
                        banks.passed(pe, f"kb{b}{n}", c)
                        banks.passed(pe, f"qa{b}{n}", c)
                    scores("s", (1, 0), 3 * DK, qaT, kbT, mask1)
                    pe.wait_ge(mrow_ok, cb_ + 1)
                    sides("qm", qa)
                    for n in range(4):
                        banks.passed(pe, f"qm{b}{n}", c)
                    scores("p", (0, 0), 3 * DK + 2, kbT, qaT, mask2)
                    bank = banks.fill(pe, f"oT{b}", c)
                    for t in range(2):
                        banks.passed(pe, f"o{b}{t}", c)
                    for f in range(KT):
                        for t in range(2):
                            m = t_.transpose(k.ps[bank][:, (f * 2 + t) * P:(f * 2 + t + 1) * P], on[:, t, f * P:(f + 1) * P], k.ident[:])
                    banks.full(m, f"oT{b}")

                def up(s):
                    for name, w in (("a", k.w1), ("b", k.w3)):
                        bank = banks.fill(pe, f"{name}{s}", c)
                        parts = [(x, f) for x in (xh, xl) for f in range(KT)]
                        for n, (x, f) in enumerate(parts):
                            m = t_.matmul(k.ps[bank][:], w[:, f, s * P:(s + 1) * P], x[:, f], start=(n == 0), stop=(n == len(parts) - 1))
                        banks.full(m, f"{name}{s}")

                def down(s):
                    pe.wait_ge(hh_ok, SLOTS1 * c + s + 1)
                    pe.wait_ge(hl_ok, SLOTS1 * c + s + 1)
                    for n, x in enumerate((hh, hl)):
                        for t in range(TP):
                            m = t_.matmul(k.ps[t // 2][:, (t % 2) * D:(t % 2 + 1) * D], x[:, s % 2, t * P:(t + 1) * P], k.w2[:, s],
                                          start=False, stop=(n == 1 and s == SLOTS1 - 1), skip_group_check=True)
                            if s == SLOTS1 - 1 and n == 1 and t % 2:
                                banks.full(m, f"acc{t // 2}")
                    if s < SLOTS1 - 1:
                        m.then_inc(down_ok, 1)

                up(0)
                for b in range(2):
                    banks.passed(pe, f"oT{b}", c)
                for n in range(2):
                    banks.fill(pe, f"acc{n}", c)
                for t in range(TP):
                    three(k.ps[t // 2][:, (t % 2) * D:(t % 2 + 1) * D], lambda l, f: (oh, ol)[l][:, f, t * P:(t + 1) * P],
                          lambda r, f: (woh, wol)[r][:, f], t % 2 == 0, False, skip_group_check=True)
                for s in range(1, SLOTS1):
                    up(s)
                    down(s - 1)
                down(SLOTS1 - 1)

        @block.vector
        def _(dve):
            v = nc.vector
            own = Chain(dve, dve_own, k.DVE_L, stand)
            once = Chain(dve, dve_once, 0)
            dve.wait_ge(consts, NCL)
            v.memset(qa[:].bitcast(U32), 0)
            v.memset(v_aug[:], 1.0)
            once.link(v.memset(kb[:].bitcast(U32), 0))
            v.tensor_copy(kb[:, :, :, 3 * DK:3 * DK + 2], k.ones[:, 0:2 * H1 * 2].rearrange("p (t h a) -> p t h a", t=2, a=2))
            for f in range(KT):
                ins = v.tensor_scalar(wq[:, f], wq[:, f], rms_w[:, f:f + 1], None, ALU.mult)
            once.link(ins)
            v.tensor_copy(wqh[:], wq).then_inc(prep_w, 1)
            once.link(v.tensor_copy(woh[:], wo))
            dve.wait_ge(prep_w, 1)
            v.tensor_tensor(wql[:], wq, wqh[:].bitcast(F32), ALU.subtract).then_inc(prep_w, 1)
            v.tensor_tensor(wol[:], wo, woh[:].bitcast(F32), ALU.subtract).then_inc(prep_w, 2)
            with dve.Fori(0, NCH) as c:
                own.begin(c)
                own.link(v.tensor_copy(w4[:], k.weight_of[:, bass.ds(c * TP * K, TP * K)]))
                dve.wait_ge(r_in, 16 * c + 16)
                dve.wait_ge(y_in, 16 * TP * K * (c + 1))
                for j in range(K):
                    for t in range(TP):
                        n = t * K + j
                        ins = v.scalar_tensor_tensor(x1[:, t], yk[:, t, j], w4[:, n:n + 1], x1[:, t], ALU.mult, ALU.add)
                    own.link(ins)
                dve.sem_inc(comb_ok, 1)
                for t in range(TP):
                    ins = v.bn_stats(stats[:, t], x1[:, t])
                own.link(ins, apart=True)
                for t in range(TP):
                    ins = v.bn_aggr(mv[:, t], stats[:, t])
                own.link(ins)
                v.tensor_scalar(var[:], mv[:, :, 1], LN_EPS, None, ALU.add).then_inc(var_ok, 1)
                dve.wait_ge(rstd_ok, c + 1)
                for t in range(TP):
                    v.tensor_scalar(xn[:, t], x1[:, t], mv[:, t, 0:1], rstd[:, t:t + 1], ALU.subtract, ALU.mult).then_inc(xn_ok, 1)
                dve.wait_ge(ssx_ok, c + 1)
                v.tensor_scalar(ms[:], ssx[:], 1.0 / D, RMS_EPS, ALU.mult, ALU.add).then_inc(ms_ok, 1)
                for f in range(KT):
                    bank = banks.read(dve, f"x{f}", c)
                    dve.wait_ge(xh_ok, KT * c + f + 1)
                    banks.drain(v.tensor_tensor(xl[:, f], k.ps[bank][:], xh[:, f].bitcast(F32), ALU.subtract), f"x{f}")
                bank = banks.read(dve, "logits", c)
                logits = k.ps[bank][:, 0:TP * E1].rearrange("p (t e) -> p t e", e=E1)
                own.link(v.tensor_scalar(spos[:], logits, 0.0, None, ALU.max))
                banks.drain(v.scalar_tensor_tensor(absx[:], spos[:], 2.0, logits, ALU.mult, ALU.subtract), "logits")
                dve.wait_ge(exp_ok, c + 1)
                v.tensor_scalar(wplus[:], expx[:], 1.0, None, ALU.add).then_inc(wplus_ok, 1)
                dve.wait_ge(wplus_ok, c + 1)
                own.link(v.tensor_scalar(dif[:], wplus[:], -1.0, None, ALU.add))
                own.link(v.tensor_scalar(zero[:], dif[:], 0.0, None, ALU.is_equal))
                own.link(v.tensor_tensor(dif[:], dif[:], zero[:], ALU.add))
                own.link(v.reciprocal(dif[:], dif[:]))
                dve.wait_ge(ln_ok, c + 1)
                own.link(v.tensor_tensor(lnw[:], lnw[:], zero[:], ALU.add))
                own.link(v.tensor_tensor(lnw[:], lnw[:], expx[:], ALU.mult))
                own.link(v.tensor_tensor(lnw[:], lnw[:], dif[:], ALU.mult))
                v.tensor_tensor(spos[:], spos[:], lnw[:], ALU.add).then_inc(sp_ok, 1)
                dve.wait_ge(rms_ok, c + 1)
                for t in range(TP):
                    bank = banks.read(dve, f"q{t}", c)
                    banks.drain(v.scalar_tensor_tensor(v_aug[:, t, :, 0:DK], k.ps[bank][:, 0:D].rearrange("p (h d) -> p h d", h=H1), rms[:, t:t + 1],
                                                       bq[:].rearrange("p (h d) -> p h d", h=H1), ALU.mult, ALU.add), f"q{t}")
                dve.wait_ge(score_ok, c + 1)
                own.link(v.tensor_tensor(biased[:], score[:], gate_b[:].unsqueeze(1).to_broadcast([P, TP, E1]), ALU.add), apart=True)
                for t in range(TP):
                    ins = v.max(top8[:, t], biased[:, t])
                own.link(ins, apart=True)
                for t in range(TP):
                    ins = v.max_index(index8[:, t], top8[:, t], biased[:, t])
                own.link(ins)
                own.link(v.tensor_copy(chosen[:], index8[:, :, 0:TOP1]))
                experts = k.iota[:, 0:E1].unsqueeze(1).to_broadcast([P, TP, E1])
                v.tensor_tensor(onehot[:], experts, chosen[:, :, 0:1].to_broadcast([P, TP, E1]), ALU.is_equal)
                own.link(v.tensor_tensor(onehot2[:], experts, chosen[:, :, 1:2].to_broadcast([P, TP, E1]), ALU.is_equal))
                own.link(v.tensor_tensor(onehot[:], onehot[:], onehot2[:], ALU.add))
                v.tensor_tensor(cw[:], onehot[:], score[:], ALU.mult).then_inc(cw_ok, 1)
                for b in range(2):
                    dve.wait_ge(hi_ok, 4 * (2 * c + b) + 4)
                    q2 = qr[:, 2 * b:2 * b + 2].rearrange("p t h d -> p (t h) d")
                    kbv, qav = kb[:].rearrange("p t h d -> p (t h) d"), qa[:].rearrange("p t h d -> p (t h) d")
                    hi = kbv[:, :, 0:DK].bitcast(F32)
                    v.tensor_tensor(kbv[:, :, 2 * DK:3 * DK], q2, hi, ALU.subtract).then_inc(lo_ok, 1)
                    v.tensor_tensor(qav[:, :, DK:2 * DK], q2, hi, ALU.subtract).then_inc(lo_ok, 1)

                    def queries(name):
                        for n in range(4):
                            bank = banks.read(dve, f"{name}{b}{n}", c)
                            banks.drain(v.tensor_copy(qaT[:, 2 * n:2 * n + 2].rearrange("p a n -> p (a n)"), k.ps[bank][:]), f"{name}{b}{n}")

                    queries("qa")
                    for n, (g, kind, par, pp) in enumerate(GROUPS):
                        bank = banks.read(dve, f"s{b}{n}", c)
                        if kind == "two":
                            o, a = mx[:, 1, par, 4 * g + 2 * pp:4 * g + 2 * pp + 2], 2
                        else:
                            o, a = mx[:, 0, par, 4 * g:4 * g + 4], 4
                        banks.drain(v.tensor_reduce(o, k.ps[bank][:].rearrange("p (a n) -> p a n", a=a), AX, ALU.max), f"s{b}{n}")
                    for n in (5, 11, 10, 9, 8, 7):
                        banks.passed(dve, f"s{b}{n}", c)
                    own.link(v.tensor_scalar(mx[:], mx[:], -1.0, None, ALU.mult))
                    top = qa[:].rearrange("p t (q r) d -> p t r q d", r=2)
                    for t in range(2):
                        ins = v.tensor_copy(top[:, t, :, :, 3 * DK], mx[:, t])
                    own.link(ins)
                    for t in range(2):
                        ins = v.tensor_tensor(top[:, t, :, :, 3 * DK + 1], mx[:, t], top[:, t, :, :, 3 * DK].bitcast(F32), ALU.subtract)
                    ins.then_inc(mrow_ok, 1)
                    queries("qm")
                    for t in range(2):
                        bank = banks.read(dve, f"o{b}{t}", c)
                        o = k.ps[bank][:, 0:H1 * (DK + 1)].rearrange("p (h d) -> p h d", h=H1)
                        own.link(v.reciprocal(rsum[:, t], o[:, :, DK]))
                        i = v.tensor_tensor(on[:, t].rearrange("p (h d) -> p h d", h=H1), o[:, :, 0:DK],
                                            rsum[:, t].unsqueeze(2).to_broadcast([P, H1, DK]), ALU.mult)
                        banks.drain(i, f"o{b}{t}")
                    bank = banks.read(dve, f"oT{b}", c)
                    dve.wait_ge(oh_ok, 2 * c + b + 1)
                    part = slice(b * S1, (b + 1) * S1)
                    banks.drain(v.tensor_tensor(ol[:, :, part], k.ps[bank][:].rearrange("p (f n) -> p f n", f=KT), oh[:, :, part].bitcast(F32), ALU.subtract), f"oT{b}")
                dve.wait_ge(cb_in, 16 * len(ROWS) * (c + 1))
                for s in range(SLOTS1):
                    dve.wait_ge(tanh_ok, SLOTS1 * c + s + 1)
                    bank = banks.read(dve, f"a{s}", c)
                    banks.drain(v.scalar_tensor_tensor(gated[:, s % 2], gate[:, s % 2], 1.0, k.ps[bank][:], ALU.add, ALU.mult), f"a{s}")
                    banks.passed(dve, f"a{s}", c)
                    bank = banks.read(dve, f"b{s}", c)
                    banks.drain(v.tensor_tensor(h1[:], gated[:, s % 2], k.ps[bank][:], ALU.mult), f"b{s}")
                    banks.passed(dve, f"b{s}", c)
                    dve.wait_ge(down_ok, (SLOTS1 - 1) * c + max(s - 1, 0))
                    if s < ROUTED1:
                        v.scalar_tensor_tensor(hc[:, s % 2], h1[:], 0.5, cb[:, s], ALU.mult, ALU.mult).then_inc(h_ok, 1)
                    else:
                        v.tensor_scalar(hc[:, s % 2], h1[:], 0.5, None, ALU.mult).then_inc(h_ok, 1)
                dve.wait_ge(xx_ok, c + 1)
                for n in range(2):
                    x2 = x1[:, 2 * n:2 * n + 2].rearrange("p t d -> p (t d)")
                    banks.read(dve, f"acc{n}", c)
                    banks.drain(v.tensor_tensor(x2, x2, k.ps[n][:], ALU.add), f"acc{n}")
                own.end()


def program(nc, io, dram, out):
    with ExitStack() as top:
        def sem(name):
            return top.enter_context(nc.semaphore(name))

        def sb(stack, name, shape, dt=F32):
            return stack.enter_context(nc.sbuf_tensor(name, shape, dt))

        k = Shared()
        k.io, k.dram, k.out, k.sem, k.sb = io, dram, out, sem, sb
        k.ps = [top.enter_context(nc.psum_tensor(f"bank{i}", [P, 512], F32)) for i in range(8)]
        k.ident = sb(top, "ident", [P, P])
        k.upto = sb(top, "upto", [P, P])
        k.ones = sb(top, "ones", [P, P])
        k.before_bf = sb(top, "before_bf", [P, P], BF16)
        k.ones_bf = sb(top, "ones_bf", [P, P], BF16)
        k.iota = sb(top, "iota", [P, NB])
        k.power = sb(top, "power", [P, 32])
        k.slot_of = sb(top, "slot_of", [P, NT * TOP0], I32)
        k.weight_of = sb(top, "weight_of", [P, NT * TOP0])
        k.expert_of = sb(top, "expert_of", [P, NT * TOP0])
        k.rank_of = sb(top, "rank_of", [P, NT * TOP0])
        k.block_f = sb(top, "block_f", [P, NB])
        k.block_expert = sb(top, "block_expert", [P, NB], I32)
        k.consts_in, k.NCONST = sem("consts_in"), 7 * 16
        k.zero_out = sem("zero_out")
        k.DVE_A = 25
        k.DVE_L = 29

        k.NZERO = 16 * (SLOTS // (8 * P))
        k.experts_in, k.NEXPERTS = sem("experts_in"), 16 * 2 * (E0 // 8)
        with ExitStack() as experts:
            k.wu = sb(experts, "wu", [P, E0, KT, I0])
            k.wd = sb(experts, "wd", [P, E0, D])
            with ExitStack() as st:
                route_tokens(nc, k, st)
            with ExitStack() as st:
                mix_tokens(nc, k, st)
            with ExitStack() as st:
                expert_blocks(nc, k, st)
        with ExitStack() as st:
            k.w1 = sb(st, "w1", [P, KT, SLOTS1 * P], F32R)
            k.w3 = sb(st, "w3", [P, KT, SLOTS1 * P], F32R)
            k.w2 = sb(st, "w2", [P, SLOTS1, D], F32R)
            k.layer1_in, k.NLAYER1, k.padded = sem("layer1_in"), 16 * 6, sem("padded")
            layer1(nc, k, st)


def constants():
    import numpy as np
    p = np.arange(P)
    inv = (1.0 / 10000.0 ** (np.arange(0, DK, 2, dtype=np.float32) / DK)).astype(np.float32)
    angle = np.arange(S1, dtype=np.float32)[:, None] * inv[None, :]

    def table(first, second):
        one = np.concatenate([first, second], axis=-1).astype(np.float32)
        return np.ascontiguousarray(np.concatenate([one] * (CH // S1)).reshape(TP, P, DK).transpose(1, 0, 2))

    return {
        "ident": np.eye(P, dtype=np.float32),
        "upto": (p[:, None] <= p[None, :]).astype(np.float32),
        "ones": np.ones((P, P), np.float32),
        "iota": np.ascontiguousarray(np.broadcast_to(np.arange(NB, dtype=np.float32), (P, NB))),
        "before_bf": (p[:, None] < p[None, :]).astype(mybir.dt.np(BF16)),
        "ones_bf": np.ones((P, P), mybir.dt.np(BF16)),
        "power": np.full((P, 32), -0.5, np.float32),
        "root": np.full((P, 32), 0.5, np.float32),
        "cos": table(np.cos(angle), np.cos(angle)),
        "sin": table(-np.sin(angle), np.sin(angle)),
        "mask1": np.where(p[None, :] > p[:, None], np.float32(-1e30), np.float32(0)).astype(mybir.dt.np(BF16)),
        "mask2": np.where(p[:, None] > p[None, :], np.float32(-1e30), np.float32(0)).astype(mybir.dt.np(BF16)),
        "ident_bf": np.eye(P, dtype=np.float32).astype(mybir.dt.np(BF16)),
    }


def scratch(nc, kind="Internal"):
    def d(name, *shape):
        return nc.dram_tensor("s_" + name, shape, F32, kind=kind).ap()

    return {"xn": d("xn", T, D), "xnT": d("xnT", D, T), "xg": d("xg", SLOTS, D), "y": d("y", SLOTS, D),
            "r": d("r", T, D), "cw": d("cw", NCH, E1, CH)}


def lay_out(inp):
    import numpy as np
    a = dict(constants())
    n = {name: np.asarray(v) for name, v in inp.items()}
    c = np.ascontiguousarray

    def rows(v):
        return c(np.broadcast_to(v, (P, v.shape[-1])))

    a["x"] = c(n["L0_attn_x"].reshape(T, D))
    a["gate_w0"] = c(n["L0_ffn_gate_w"])
    a["w_qkv"] = c(n["L0_attn_w_qkv"].T)
    a["w_ug"] = c(n["L0_attn_w_swiglu"].T)
    a["w_out"] = c(n["L0_attn_w_out"].T)
    a["w_su"] = c(n["L0_ffn_Wsu"])
    a["w_sd"] = c(n["L0_ffn_Wsd"])
    a["wu"] = c(n["L0_ffn_Wu"].reshape(E0, KT, P, I0).transpose(2, 0, 1, 3))
    a["wd"] = c(n["L0_ffn_Wd"].transpose(1, 0, 2))
    cat = np.concatenate
    a["w1"] = c(cat([n["L1_ffn_w1"].reshape(-1, D), n["L1_ffn_sw1"]]).T)
    a["w3"] = c(cat([n["L1_ffn_w3"].reshape(-1, D), n["L1_ffn_sw3"]]).T)
    a["w2"] = c(cat([n["L1_ffn_w2"].transpose(0, 2, 1).reshape(-1, D), n["L1_ffn_sw2"].T]))
    a["wq"] = c(n["L1_attn_Wq_w"].T)
    a["wo"] = c(n["L1_attn_Wo_w"].T)
    a["bq"] = rows(n["L1_attn_Wq_b"])
    a["bo"] = rows(n["L1_attn_Wo_b"])
    a["rms_w"] = c(n["L1_attn_rms_w"].reshape(KT, P).T)
    a["gate_w1"] = c(n["L1_ffn_gate_w"].T)
    a["gate_b1"] = rows(n["L1_ffn_gate_b"])
    a["bias0"] = rows(n["L0_ffn_e_bias"])
    return a


def kernel(**inputs):
    import concourse.bacc as bacc
    import numpy as np
    from concourse.bass_utils import run_bass_kernel_spmd

    arrays = lay_out(inputs)
    nc = bacc.Bacc("TRN2", target_bir_lowering=False, num_devices=1)
    io = {name: nc.dram_tensor("in_" + name, v.shape, mybir.dt.from_np(v.dtype), kind="ExternalInput").ap()
          for name, v in arrays.items()}
    out = nc.dram_tensor("out", (T, D), F32, kind="ExternalOutput").ap()
    program(nc, io, scratch(nc), out)
    result = run_bass_kernel_spmd(nc, [{"in_" + name: v for name, v in arrays.items()}], core_ids=[0]).results[0]
    return np.asarray(result["out"]).reshape(T // S1, S1, D)
```

```python
from contextlib import ExitStack

import concourse.bass as bass
from concourse import mybir

F32 = mybir.dt.float32
F32R = mybir.dt.float32r
BF16 = mybir.dt.bfloat16
I32 = mybir.dt.int32
U32 = mybir.dt.uint32
ALU = mybir.AluOpType
ACT = mybir.ActivationFunctionType
AX = mybir.AxisListType.X

P = 128
D = 256
KT = D // P
T = 4096
CH = 512
NCH = T // CH
TP = CH // P
NT = T // P
E0, TOP0, I0 = 32, 4, 128
G0 = 4
EG = E0 // G0
SCALE0 = 2.5
NB = (T * TOP0 + E0 * (P - 1)) // P + 1
SLOTS = NB * P
UG = 1024
SI = 512
E1, TOP1, I1 = 8, 2, 176
ROWS1 = (E1 + 1) * I1
SLOTS1 = -(-ROWS1 // P)
ROUTED1 = E1 * I1 // P
H1, S1 = 16, 256
DK = D // H1
LN_EPS = 1e-5
RMS_EPS = 1.1920929e-07


class Shared:
    pass


class Chain:

    def __init__(self, eng, sem, per_round, done=None):
        self.eng, self.sem, self.per_round, self.done = eng, sem, per_round, done
        self.base, self.n = 0, 0

    def begin(self, rounds_before):
        self.base, self.n = rounds_before * self.per_round, 0

    def count(self, ins):
        self.n += 1
        ins.then_inc(self.sem, 1)

    def link(self, ins, apart=False):
        self.count(ins)
        self.eng.wait_ge(self.sem, self.base + self.n)
        if apart:
            self.eng.sem_inc(self.done, 1)

    def end(self):
        assert self.n == self.per_round, self.n


def route_tokens(nc, k, st):
    sem, sb = k.sem, lambda name, shape, dt=F32: k.sb(st, name, shape, dt)
    E, K = E0, TOP0
    x_t = sb("a_x", [P, 2, TP, D])
    xn = sb("a_xn", [P, 2, TP, D])
    xnT = sb("a_xnT", [P, 2, KT, CH])
    gate_w = sb("a_gate_w", [P, KT, E])
    bias = sb("a_bias", [P, E])
    stats = sb("a_stats", [P, TP, 6])
    mv = sb("a_mv", [P, TP, 2])
    var = sb("a_var", [P, 2, TP])
    rstd = sb("a_rstd", [P, 2, TP])
    expn = sb("a_expn", [P, TP * E])
    score = sb("a_score", [P, TP, E])
    biased = sb("a_biased", [P, TP, E])
    top8g = sb("a_top8g", [P, TP * G0, 8])
    gscore = sb("a_gscore", [P, TP, G0])
    beats = sb("a_beats", [P, TP, G0, G0])
    gmask = sb("a_gmask", [P, TP, G0])
    top8 = sb("a_top8", [P, TP, 8])
    index8 = sb("a_index8", [P, TP, 8], U32)
    chosen = sb("a_chosen", [P, TP, K])
    onehot = sb("a_onehot", [P, TP, K, E])
    picked = sb("a_picked", [P, TP, K, E])
    weight = sb("a_weight", [P, TP, K])
    wsum = sb("a_wsum", [P, TP])
    takes = sb("a_takes", [P, 2, TP, E], BF16)
    rank = sb("a_rank", [P, TP, E])
    count = sb("a_count", [P, E])
    blocks = sb("a_blocks", [P, E])
    blocks_i = sb("a_blocks_i", [P, E], I32)
    upto_blocks = sb("a_upto_blocks", [P, E])
    start = sb("a_start", [P, E])
    zeros = sb("a_zeros", [P, 2048])
    wide = sb("a_wide", [P, 40 * E])

    w_in, x_in = sem("a_w_in"), [sem("a_x_in0"), sem("a_x_in1")]
    var_ok, rstd_ok, xn_ok = sem("a_var_ok"), sem("a_rstd_ok"), sem("a_xn_ok")
    turned, xnT_ok, logits_ok, exp_ok = sem("a_turned"), sem("a_xnT_ok"), sem("a_logits_ok"), sem("a_exp_ok")
    takes_ok, ranks_ok, rank_read = sem("a_takes_ok"), sem("a_ranks_ok"), sem("a_rank_read")
    xn_out, xnT_out, zeros_ok, zero_out = [sem("a_xn_out0"), sem("a_xn_out1")], [sem("a_xnT_out0"), sem("a_xnT_out1")], sem("a_zeros_ok"), k.zero_out
    dve_own = sem("a_dve_own")

    turn_bank = [ [k.ps[0], k.ps[1]], [k.ps[2], k.ps[3]] ]
    logits = [k.ps[4], k.ps[5]]
    ranks = [k.ps[6], k.ps[7]]
    x_v = k.io["x"].rearrange("(c t p) d -> c p t d", p=P, t=TP)
    xn_v = k.dram["xn"].rearrange("(c t p) d -> c p t d", p=P, t=TP)
    xnT_v = k.dram["xnT"].rearrange("(f p) (c n) -> c p f n", p=P, n=CH)

    with nc.Block() as block:

        @block.sync
        def _(sp):
            consts = [(k.ident, "ident"), (k.upto, "upto"), (k.ones, "ones"), (k.iota, "iota"),
                      (k.before_bf, "before_bf"), (k.ones_bf, "ones_bf"), (k.power, "power")]
            for u in range(2):
                sp.dma_start(x_t[:, u], x_v[u]).then_inc(x_in[u], 16)
            for tile, name in consts:
                sp.dma_start(tile[:], k.io[name]).then_inc(k.consts_in, 16)
            sp.dma_start(gate_w[:], k.io["gate_w0"].rearrange("(f p) e -> p f e", p=P)).then_inc(w_in, 16)
            sp.dma_start(bias[:], k.io["bias0"]).then_inc(w_in, 16)
            sp.wait_ge(zeros_ok, 1)
            zv = k.dram["xg"].rearrange("(z p r) d -> z p (r d)", p=P, r=8)
            for z in range(SLOTS // (8 * P)):
                sp.dma_start(zv[z], zeros[:, 0:8 * D]).then_inc(zero_out, 16)

            def stores(c, u):
                sp.wait_ge(xn_ok, TP * c + TP)
                sp.dma_start(xn_v[c], xn[:, u]).then_inc(xn_out[u], 16)
                sp.wait_ge(xnT_ok, KT * c + KT)
                sp.dma_start(xnT_v[c], xnT[:, u]).then_inc(xnT_out[u], 16)

            with sp.Fori(0, NCH // 2 - 1) as i:
                for u in range(2):
                    c = 2 * i + u
                    sp.wait_ge(xn_ok, TP * c + TP)
                    sp.dma_start(x_t[:, u], x_v[c + 2]).then_inc(x_in[u], 16)
                    stores(c, u)
            for u in range(2):
                stores(NCH - 2 + u, u)
            for u in range(2):
                sp.wait_ge(xn_out[u], 16 * NCH // 2)
                sp.wait_ge(xnT_out[u], 16 * NCH // 2)

        @block.gpsimd
        def _(pool):
            nc.gpsimd.memset(zeros[:], 0.0).then_inc(zeros_ok, 1)
            pool.wait_ge(k.consts_in, k.NCONST)
            with pool.Fori(0, NCH // 2) as i:
                for u in range(2):
                    c = 2 * i + u
                    pool.wait_ge(var_ok, c + 1)
                    nc.gpsimd.tensor_tensor(rstd[:, u], var[:, u], k.power[:, 0:TP], ALU.pow).then_inc(rstd_ok, 1)

        @block.scalar
        def _(act):
            with act.Fori(0, NCH // 2) as i:
                for u in range(2):
                    c = 2 * i + u
                    for f in range(KT):
                        act.wait_ge(turned, KT * c + f + 1)
                        act.wait_ge(xnT_out[u], 16 * i)
                        nc.scalar.activation(xnT[:, u, f], turn_bank[u][f][:], ACT.Copy).then_inc(xnT_ok, 1)
                    act.wait_ge(logits_ok, c + 1)
                    act.wait_ge(dve_own, k.DVE_A * c)
                    nc.scalar.activation(expn[:], logits[u][:, 0:TP * E], ACT.Exp, scale=-1.0).then_inc(exp_ok, 1)

        @block.tensor
        def _(pe):
            pe.wait_ge(k.consts_in, k.NCONST)
            pe.wait_ge(w_in, 32)
            with pe.Fori(0, NCH // 2) as i:
                for u in range(2):
                    c = 2 * i + u
                    pe.wait_ge(xnT_ok, KT * c)
                    for f in range(KT):
                        for t in range(TP):
                            pe.wait_ge(xn_ok, TP * c + t + 1)
                            m = nc.tensor.transpose(turn_bank[u][f][:, t * P:(t + 1) * P],
                                                    xn[:, u, t, f * P:(f + 1) * P], k.ident[:])
                        m.then_inc(turned, 1)
                    pe.wait_ge(xnT_ok, KT * c + KT)
                    for t in range(TP):
                        for f in range(KT):
                            m = nc.tensor.matmul(logits[u][:, t * E:(t + 1) * E], xnT[:, u, f, t * P:(t + 1) * P],
                                                 gate_w[:, f], start=(f == 0), stop=(f == KT - 1))
                    m.then_inc(logits_ok, 1)
                    pe.wait_ge(takes_ok, c + 1)
                    for t in range(TP + 1):
                        o = ranks[u][:, t * E:(t + 1) * E]
                        for s in range(min(t + 1, TP)):
                            m = nc.tensor.matmul(o, (k.before_bf if s == t else k.ones_bf)[:], takes[:, u, s],
                                                 start=(s == 0), stop=(s == min(t, TP - 1)))
                    m.then_inc(ranks_ok, 1)

        @block.vector
        def _(dve):
            v = nc.vector
            own = Chain(dve, dve_own, k.DVE_A, sem("a_stand"))
            dve.wait_ge(k.consts_in, k.NCONST)
            dve.wait_ge(w_in, 32)
            with nc.allow_low_precision("0 and 1 are exact in bf16"):
                v.memset(count[:], 0.0)
                v.memset(beats[:], 0.0)
                with dve.Fori(0, NCH // 2) as i:
                    for u in range(2):
                        c = 2 * i + u
                        own.begin(c)
                        dve.wait_ge(x_in[u], 16 * i + 16)
                        for t in range(TP):
                            ins = v.bn_stats(stats[:, t], x_t[:, u, t])
                        own.link(ins, apart=True)
                        for t in range(TP - 1):
                            v.bn_aggr(mv[:, t], stats[:, t])
                        own.link(v.bn_aggr(mv[:, TP - 1], stats[:, TP - 1]))
                        v.tensor_scalar(var[:, u], mv[:, :, 1], LN_EPS, None, ALU.add).then_inc(var_ok, 1)
                        dve.wait_ge(rstd_ok, c + 1)
                        dve.wait_ge(xn_out[u], 16 * i)
                        dve.wait_ge(turned, KT * c)
                        for t in range(TP):
                            v.tensor_scalar(xn[:, u, t], x_t[:, u, t], mv[:, t, 0:1], rstd[:, u, t:t + 1],
                                            ALU.subtract, ALU.mult).then_inc(xn_ok, 1)
                        dve.wait_ge(exp_ok, c + 1)
                        own.link(v.tensor_scalar(biased[:].rearrange("p t e -> p (t e)"), expn[:], 1.0, None, ALU.add))
                        own.link(v.reciprocal(score[:], biased[:]))
                        own.link(v.tensor_tensor(biased[:], score[:], bias[:].unsqueeze(1).to_broadcast([P, TP, E]), ALU.add), apart=True)
                        grouped = biased[:].rearrange("p t (g e) -> p (t g) e", e=EG)
                        for g in range(TP * G0):
                            ins = v.max(top8g[:, g], grouped[:, g])
                        own.link(ins)
                        own.link(v.tensor_tensor(gscore[:].rearrange("p t g -> p (t g)"), top8g[:, :, 0], top8g[:, :, 1], ALU.add))
                        for g in range(G0):
                            for lo, hi, op in ((0, g, ALU.is_ge), (g + 1, G0, ALU.is_gt)):
                                if lo < hi:
                                    ins = v.tensor_tensor(beats[:, :, g, lo:hi], gscore[:, :, lo:hi],
                                                          gscore[:, :, g:g + 1].to_broadcast([P, TP, hi - lo]), op)
                        own.link(ins)
                        own.link(v.tensor_reduce(gmask[:], beats[:], AX, ALU.add))
                        own.link(v.tensor_scalar(gmask[:], gmask[:], 2.0, None, ALU.is_lt))
                        own.link(v.tensor_tensor(biased[:].rearrange("p t (g e) -> p (t g) e", e=EG), grouped,
                                                 gmask[:].rearrange("p t g -> p (t g)").unsqueeze(2).to_broadcast([P, TP * G0, EG]), ALU.mult), apart=True)
                        choose(nc, k, own, c, u, E, K, biased, score, top8, index8, chosen, onehot, picked, weight,
                               takes, takes_ok, ranks_ok, ranks, rank, count)
                        own.link(v.tensor_reduce(wsum[:], weight[:], AX, ALU.add))
                        own.link(v.tensor_scalar(wsum[:], wsum[:], 1e-20, None, ALU.add))
                        own.link(v.reciprocal(wsum[:], wsum[:]))
                        own.link(v.scalar_tensor_tensor(k.weight_of[:, bass.ds(c * TP * K, TP * K)].rearrange("p (t k) -> p t k", k=K),
                                                        weight[:], SCALE0, wsum[:].unsqueeze(2).to_broadcast([P, TP, K]), ALU.mult, ALU.mult))
                        own.end()
                last = Chain(dve, sem("a_dve_last"), 0)
                last.link(v.tensor_scalar(blocks_i[:], count[:], float(P - 1), None, ALU.add))
                last.link(v.tensor_scalar(blocks_i[:], blocks_i[:], 7, None, ALU.arith_shift_right))
                last.link(v.tensor_copy(blocks[:], blocks_i[:]))
                last.link(v.tensor_tensor_scan(upto_blocks[:], k.ones[:, 0:E], blocks[:], 0.0, ALU.mult, ALU.add))
                last.link(v.tensor_tensor(start[:], upto_blocks[:], blocks[:], ALU.subtract))
                last.link(v.tensor_scalar(start[:], start[:], float(P), None, ALU.mult))
                step = 40
                for j in range(0, NB, step):
                    w = wide[:].rearrange("p (j e) -> p j e", e=E)
                    last.link(v.tensor_tensor(w, upto_blocks[:].unsqueeze(1).to_broadcast([P, step, E]),
                                              k.iota[:, j:j + step].unsqueeze(2).to_broadcast([P, step, E]), ALU.is_le))
                    last.link(v.tensor_reduce(k.block_f[:, j:j + step], w, AX, ALU.add))
                last.link(v.tensor_scalar(k.block_expert[:], k.block_f[:], float(E - 1), None, ALU.min))
                for j in range(0, NT * K, 32):
                    w = wide[:, 0:32 * E].rearrange("p (j e) -> p j e", e=E)
                    last.link(v.tensor_tensor(w, k.iota[:, 0:E].unsqueeze(1).to_broadcast([P, 32, E]),
                                              k.expert_of[:, j:j + 32].unsqueeze(2).to_broadcast([P, 32, E]), ALU.is_equal))
                    last.link(v.tensor_tensor(w, w, start[:].unsqueeze(1).to_broadcast([P, 32, E]), ALU.mult))
                    last.link(v.tensor_reduce(k.block_f[:, 0:32], w, AX, ALU.add))
                    last.link(v.tensor_tensor(k.slot_of[:, j:j + 32], k.block_f[:, 0:32], k.rank_of[:, j:j + 32], ALU.add))


def choose(nc, k, own, c, u, E, K, biased, score, top8, index8, chosen, onehot, picked, weight, takes, takes_ok, ranks_ok, ranks, rank, count):
    v, dve = nc.vector, nc.vector
    for t in range(TP):
        ins = v.max(top8[:, t], biased[:, t])
    own.link(ins, apart=True)
    for t in range(TP):
        ins = v.max_index(index8[:, t], top8[:, t], biased[:, t])
    own.link(ins)
    own.link(v.tensor_copy(chosen[:], index8[:, :, 0:K]))
    v.tensor_copy(k.expert_of[:, bass.ds(c * TP * K, TP * K)].rearrange("p (t k) -> p t k", k=K), chosen[:])
    own.link(v.tensor_tensor(onehot[:], k.iota[:, 0:E].unsqueeze(1).unsqueeze(1).to_broadcast([P, TP, K, E]),
                             chosen[:].unsqueeze(3).to_broadcast([P, TP, K, E]), ALU.is_equal))
    v.tensor_reduce(takes[:, u], onehot[:].rearrange("p t k e -> p t e k"), AX, ALU.add).then_inc(takes_ok, 1)
    own.link(v.tensor_tensor(picked[:], onehot[:], score[:].unsqueeze(2).to_broadcast([P, TP, K, E]), ALU.mult))
    own.link(v.tensor_reduce(weight[:], picked[:], AX, ALU.add))
    dve.wait_ge(ranks_ok, c + 1)
    own.link(v.tensor_tensor(rank[:], ranks[u][:, 0:TP * E].rearrange("p (t e) -> p t e", e=E),
                             count[:].unsqueeze(1).to_broadcast([P, TP, E]), ALU.add))
    own.link(v.tensor_tensor(count[:], count[:], ranks[u][:, TP * E:TP * E + E], ALU.add))
    own.link(v.tensor_tensor(picked[:], onehot[:], rank[:].unsqueeze(2).to_broadcast([P, TP, K, E]), ALU.mult))
    own.link(v.tensor_reduce(k.rank_of[:, bass.ds(c * TP * K, TP * K)].rearrange("p (t k) -> p t k", k=K), picked[:], AX, ALU.add))


def mix_tokens(nc, k, st):
    sem, sb = k.sem, lambda name, shape, dt=F32: k.sb(st, name, shape, dt)
    x_t = sb("m_x", [P, 2, TP, D])
    xn = sb("m_xn", [P, 2, TP, D])
    xnT = sb("m_xnT", [P, 2, KT, CH])
    w_qkv = sb("m_w_qkv", [P, KT, 3 * D])
    w_ug = sb("m_w_ug", [P, KT, 2 * UG])
    w_out = sb("m_w_out", [P, UG // P, D])
    w_su = sb("m_w_su", [P, KT, SI])
    w_sd = sb("m_w_sd", [P, SI // P, D])
    squares = sb("m_squares", [P, TP, D])
    squares_qk = sb("m_squares_qk", [P, 2, D])
    ssx = sb("m_ssx", [P, TP])
    rms = sb("m_rms", [P, 2, TP])
    rms_sq = sb("m_rms_sq", [P, 2, TP])
    rms_pm = sb("m_rms_pm", [P, 2, TP, 2])
    ssqk = sb("m_ssqk", [P, 2])
    qk_mean = sb("m_qk_mean", [P, 2])
    qk_pow = sb("m_qk_pow", [P, 2])
    qk_scale = sb("m_qk_scale", [P, 2])
    eq = sb("m_eq", [P, TP, D])
    wv = sb("m_wv", [P, TP, 2 * D])
    den = sb("m_den", [P, D])
    y = sb("m_y", [P, TP, D])
    yT = sb("m_yT", [P, KT, CH])
    gate = sb("m_gate", [P, 2, CH])
    gated = sb("m_gated", [P, 2, CH])
    h = sb("m_h", [P, 3, CH])
    slots = sb("m_slots", [P, 2, TP * TOP0], I32)

    NS, SW = UG // P + SI // P, UG // P
    w_in = sem("m_w_in")
    x_in, xnT_in = [sem("m_x_in0"), sem("m_x_in1")], [sem("m_xnT_in0"), sem("m_xnT_in1")]
    up_ok, gate_ok, h_ok, down_ok = sem("m_up_ok"), sem("m_gate_ok"), sem("m_h_ok"), sem("m_down_ok")
    xx_ok, res_ok, r_out = sem("m_xx_ok"), sem("m_res_ok"), [sem("m_r_out0"), sem("m_r_out1")]
    ssx_ok, mean_ok, pow_ok, rms_ok = sem("m_ssx_ok"), sem("m_mean_ok"), sem("m_pow_ok"), sem("m_rms_ok")
    prep_mm, prep_read = sem("m_prep_mm"), sem("m_prep_read")
    ss_ok, qkm_ok, qkp_ok, scale_ok = sem("m_ss_ok"), sem("m_qkm_ok"), sem("m_qkp_ok"), sem("m_scale_ok")
    exp_ok, eq1_ok, yT_ok = sem("m_exp_ok"), sem("m_eq1_ok"), sem("m_yT_ok")
    dve_s, dve_p = sem("m_dve_s"), sem("m_dve_p")
    slots_ok, scattered, stand = sem("m_slots_ok"), [sem("m_scattered0"), sem("m_scattered1")], sem("m_stand")

    acc = [k.ps[0], k.ps[1]]
    stream = [[k.ps[2], k.ps[3]], [k.ps[4], k.ps[5]]]
    prep_a, prep_b = k.ps[6], k.ps[7]
    x_v = k.io["x"].rearrange("(c t p) d -> c p t d", p=P, t=TP)
    xn_v = k.dram["xn"].rearrange("(c t p) d -> c p t d", p=P, t=TP)
    r_v = k.dram["r"].rearrange("(c t p) d -> c p t d", p=P, t=TP)
    xnT_v = k.dram["xnT"].rearrange("(f p) (c n) -> c p f n", p=P, n=CH)
    QKV = {1: 0, 2: 1, 5: 2, 6: 3}
    CUM = {3: 0, 4: 1, 7: 2, 8: 3}
    ORDER = {1: 0, 2: 1, 3: 2, 4: 3, 5: 4, 6: 5, 7: 6, 8: 7, 10: 8}

    def chunks(eng, body, prologue):
        prologue()
        with eng.Fori(0, NCH // 2 - 1) as i:
            for u in range(2):
                body(2 * i + u, i, u, True)
        for u in range(2):
            body(NCH - 2 + u, NCH // 2 - 1, u, u == 0)

    with nc.Block() as block:

        @block.sync
        def _(sp):
            def load(c, u):
                sp.dma_start(xnT[:, u], xnT_v[c]).then_inc(xnT_in[u], 16)
                sp.dma_start(xn[:, u], xn_v[c]).then_inc(x_in[u], 16)
                sp.dma_start(x_t[:, u], x_v[c]).then_inc(x_in[u], 16)

            load(0, 0)
            sp.dma_start(w_qkv[:], k.io["w_qkv"].rearrange("(f p) n -> p f n", p=P)).then_inc(w_in, 16)
            sp.dma_start(w_ug[:], k.io["w_ug"].rearrange("(f p) n -> p f n", p=P)).then_inc(w_in, 16)
            sp.dma_start(w_out[:], k.io["w_out"].rearrange("(f p) n -> p f n", p=P)).then_inc(w_in, 16)
            load(1, 1)
            sp.dma_start(w_su[:], k.io["w_su"].rearrange("(f p) n -> p f n", p=P)).then_inc(w_in, 16)
            sp.dma_start(w_sd[:], k.io["w_sd"].rearrange("(f p) n -> p f n", p=P)).then_inc(w_in, 16)

            def body(c, i, u, more):
                sp.wait_ge(res_ok, 2 * c + 2)
                sp.dma_start(r_v[c], x_t[:, u]).then_inc(r_out[u], 16)

            with sp.Fori(0, NCH // 2 - 1) as i:
                for u in range(2):
                    c = 2 * i + u
                    body(c, i, u, True)
                    sp.wait_ge(r_out[u], 16 * i + 16)
                    sp.wait_ge(up_ok, NS * c + NS)
                    sp.wait_ge(scattered[u], 16 * TP * TOP0 * (i + 1))
                    load(c + 2, u)
                    if u == 0:
                        pass
            for u in range(2):
                body(NCH - 2 + u, 0, u, False)
            n_load = 0
            for e in range(0, E0, 8):
                sp.dma_start(k.wu[:, e:e + 8], k.io["wu"][:, e:e + 8]).then_inc(k.experts_in, 16)
                sp.dma_start(k.wd[:, e:e + 8], k.io["wd"][:, e:e + 8]).then_inc(k.experts_in, 16)
                n_load += 32
            assert n_load == k.NEXPERTS
            for u in range(2):
                sp.wait_ge(r_out[u], 16 * NCH // 2)
                sp.wait_ge(scattered[u], 16 * TP * TOP0 * NCH // 2)

        @block.gpsimd
        def _(pool):
            g = nc.gpsimd

            def norm(n, u, i):
                pool.wait_ge(mean_ok, n + 1)
                g.tensor_tensor(rms[:, u], rms[:, u], k.power[:, 0:TP], ALU.pow).then_inc(pow_ok, 1)

            def qkv(n, t, u):
                pool.wait_ge(qkm_ok, TP * n + t + 1)
                g.tensor_tensor(qk_pow[:], qk_mean[:], k.power[:, 0:2], ALU.pow).then_inc(qkp_ok, 1)
                pool.wait_ge(exp_ok, TP * n + t + 1)
                pool.sem_inc(stand, 1)
                g.tensor_scalar(eq[:, t], eq[:, t], 1.0, None, ALU.add).then_inc(eq1_ok, 1)

            def prologue():
                norm(0, 0, 0)
                for t in range(TP):
                    qkv(0, t, 0)
                pool.wait_ge(k.zero_out, k.NZERO)

            def body(c, i, u, more):
                pool.wait_ge(x_in[u], 32 * i + 32)
                g.tensor_copy(slots[:, u], k.slot_of[:, bass.ds(c * TP * TOP0, TP * TOP0)] if not isinstance(c, int)
                              else k.slot_of[:, c * TP * TOP0:(c + 1) * TP * TOP0]).then_inc(slots_ok, 1)
                g.tensor_tensor(x_t[:, u], x_t[:, u], xn[:, u], ALU.add).then_inc(xx_ok, 1)
                pool.wait_ge(slots_ok, c + 1)
                pool.sem_inc(stand, 1)
                if more:
                    norm(c + 1, 1 - u, i)
                done = 0
                for s in range(NS):
                    if more and s in QKV:
                        qkv(c + 1, QKV[s], 1 - u)
                        pool.sem_inc(stand, 1)
                    for _ in range(2):
                        if done < TP * TOP0:
                            t, j = divmod(done, TOP0)
                            g.indirect_dma_start(k.dram["xg"], bass.IndirectOffsetOnAxis(ap=slots[:, u, done:done + 1], axis=0),
                                                 xn[:, u, t], None).then_inc(scattered[u], 16)
                            done += 1
                assert done == TP * TOP0

            chunks(pool, body, prologue)

        @block.scalar
        def _(act):
            a = nc.scalar

            def norm(n, u, i, load):
                act.wait_ge(x_in[u], load)
                act.wait_ge(mean_ok, n)
                for t in range(TP):
                    ins = a.activation(squares[:, t], xn[:, u, t], ACT.Square, accum_out=ssx[:, t:t + 1])
                ins.then_inc(ssx_ok, 1)

            def qkv(n, t):
                act.wait_ge(prep_mm, 9 * n + {0: 1, 1: 2, 2: 5, 3: 6}[t])
                act.wait_ge(qkm_ok, TP * n + t)
                a.activation(squares_qk[:, 0], prep_a[:, 0:D], ACT.Square, accum_out=ssqk[:, 0:1])
                a.activation(squares_qk[:, 1], prep_a[:, D:2 * D], ACT.Square, accum_out=ssqk[:, 1:2]).then_inc(ss_ok, 1)
                act.wait_ge(scale_ok, TP * n + t + 1)
                act.wait_ge(prep_read, 8 * n)
                a.activation(eq[:, t], prep_a[:, 0:D], ACT.Exp, scale=qk_scale[:, 0:1])
                a.activation(wv[:, t, D:2 * D], prep_a[:, D:2 * D], ACT.Exp, scale=qk_scale[:, 1:2]).then_inc(exp_ok, 1)

            def turn(n):
                act.wait_ge(prep_mm, 9 * n + 9)
                for f in range(KT):
                    a.activation(yT[:, f], (prep_a, prep_b)[f][:], ACT.Copy).then_inc(yT_ok, 1)

            def prologue():
                norm(0, 0, 0, 32)
                for t in range(TP):
                    qkv(0, t)
                turn(0)

            def body(c, i, u, more):
                for s in range(NS):
                    act.wait_ge(up_ok, NS * c + s + 1)
                    if s < SW:
                        a.activation(gate[:, s % 2], stream[s % 2][1][:], ACT.Tanh, scale=0.5).then_inc(gate_ok, 1)
                    else:
                        a.activation(gate[:, s % 2], stream[s % 2][0][:], ACT.Relu).then_inc(gate_ok, 1)
                    if more and s == 0:
                        norm(c + 1, 1 - u, i, 32 * (i + 1 + u))
                    if more and s in QKV:
                        qkv(c + 1, QKV[s])
                    if more and s == 10:
                        turn(c + 1)

            chunks(act, body, prologue)

        @block.tensor
        def _(pe):
            t_ = nc.tensor

            def qkv(n, t, u, j):
                pe.wait_ge(prep_read, 8 * n + j)
                if j == 0:
                    pe.wait_ge(yT_ok, 2 * n)
                for f in range(KT):
                    t_.matmul(prep_a[:, 0:2 * D], xnT[:, u, f, t * P:(t + 1) * P], w_qkv[:, f, 0:2 * D], start=(f == 0), stop=(f == KT - 1))
                for f in range(KT):
                    m = t_.matmul(prep_b[:, 0:D], xnT[:, u, f, t * P:(t + 1) * P], w_qkv[:, f, 2 * D:3 * D], start=(f == 0), stop=(f == KT - 1))
                m.then_inc(prep_mm, 1)

            def cum(n, t, j):
                pe.wait_ge(prep_read, 8 * n + j)
                m = t_.matmul(prep_a[:], k.upto[:], wv[:, t], start=True, stop=(t % 2 == 0))
                if t % 2:
                    m = t_.matmul(prep_a[:], k.ones[:], wv[:, t - 1], start=False, stop=True)
                m.then_inc(prep_mm, 1)

            def turn(n):
                pe.wait_ge(prep_read, 8 * n + 8)
                for f in range(KT):
                    for t in range(TP):
                        m = t_.transpose((prep_a, prep_b)[f][:, t * P:(t + 1) * P], y[:, t, f * P:(f + 1) * P], k.ident[:])
                m.then_inc(prep_mm, 1)

            def prep(n, u, s):
                if s in QKV:
                    qkv(n, QKV[s], u, ORDER[s])
                if s in CUM:
                    cum(n, CUM[s], ORDER[s])
                if s == 10:
                    turn(n)

            def prologue():
                pe.wait_ge(w_in, 16 * 5)
                pe.wait_ge(xnT_in[0], 16)
                for s in sorted(ORDER):
                    prep(0, 0, s)

            def up(c, u, s):
                pe.wait_ge(h_ok, NS * c + max(s - 1, 0))
                if s == 0:
                    pe.wait_ge(yT_ok, 2 * c + 2)
                if s < SW:
                    for half in range(2):
                        for f in range(KT):
                            m = t_.matmul(stream[s % 2][half][:], w_ug[:, f, half * UG + s * P:half * UG + (s + 1) * P],
                                          yT[:, f], start=(f == 0), stop=(f == KT - 1))
                else:
                    for f in range(KT):
                        m = t_.matmul(stream[s % 2][0][:], w_su[:, f, (s - SW) * P:(s - SW + 1) * P], xnT[:, u, f],
                                      start=(f == 0), stop=(f == KT - 1))
                m.then_inc(up_ok, 1)

            def down(c, s):
                pe.wait_ge(h_ok, NS * c + s + 1)
                if s == 0:
                    pe.wait_ge(res_ok, 2 * c)
                w = w_out[:, s] if s < SW else w_sd[:, s - SW]
                for t in range(TP):
                    m = t_.matmul(acc[t // 2][:, (t % 2) * D:(t % 2 + 1) * D], h[:, s % 3, t * P:(t + 1) * P], w,
                                  start=(s == 0 and t % 2 == 0), stop=(s == NS - 1), skip_group_check=True)
                m.then_inc(down_ok, 1)

            def body(c, i, u, more):
                up(c, u, 0)
                if more:
                    pe.wait_ge(xnT_in[1 - u], 16 * (i + 1 + u))
                for s in range(1, NS):
                    up(c, u, s)
                    if more:
                        prep(c + 1, 1 - u, s)
                    down(c, s - 1)
                down(c, NS - 1)

            chunks(pe, body, prologue)

        @block.vector
        def _(dve):
            v = nc.vector
            own_s = Chain(dve, dve_s, SW)
            own_p = Chain(dve, dve_p, 1 + 2 * TP)

            def norm(n, u):
                own_p.begin(n)
                dve.wait_ge(ssx_ok, n + 1)
                v.tensor_scalar(rms[:, u], ssx[:], 1.0 / D, RMS_EPS, ALU.mult, ALU.add).then_inc(mean_ok, 1)
                dve.wait_ge(pow_ok, n + 1)
                own_p.link(v.tensor_tensor(rms_sq[:, u], rms[:, u], rms[:, u], ALU.mult))
                v.tensor_scalar(rms_sq[:, u], rms_sq[:, u], 1.0 / D, None, ALU.mult)
                v.tensor_scalar(rms_pm[:, u, :, 0], rms[:, u], -1.0, None, ALU.mult)
                v.tensor_copy(rms_pm[:, u, :, 1], rms[:, u]).then_inc(rms_ok, 1)

            def qkv(n, t, u):
                dve.wait_ge(ss_ok, TP * n + t + 1)
                dve.wait_ge(rms_ok, n + 1)
                v.tensor_scalar(qk_mean[:], ssqk[:], rms_sq[:, u, t:t + 1], RMS_EPS, ALU.mult, ALU.add).then_inc(qkm_ok, 1)
                dve.wait_ge(qkp_ok, TP * n + t + 1)
                v.tensor_tensor(qk_scale[:], qk_pow[:], rms_pm[:, u, t], ALU.mult).then_inc(scale_ok, 1)
                dve.wait_ge(exp_ok, TP * n + t + 1)
                v.scalar_tensor_tensor(wv[:, t, 0:D], prep_b[:, 0:D], rms[:, u, t:t + 1], wv[:, t, D:2 * D],
                                       ALU.mult, ALU.mult).then_inc(prep_read, 1)

            def cum(n, t):
                dve.wait_ge(prep_mm, 9 * n + {0: 3, 1: 4, 2: 7, 3: 8}[t])
                dve.wait_ge(eq1_ok, TP * n + t + 1)
                own_p.link(v.scalar_tensor_tensor(den[:], prep_a[:, D:2 * D], 1e-6, eq[:, t], ALU.add, ALU.mult))
                own_p.link(v.reciprocal(den[:], den[:]))
                if t == 0:
                    dve.wait_ge(yT_ok, 2 * n)
                v.tensor_tensor(y[:, t], prep_a[:, 0:D], den[:], ALU.mult).then_inc(prep_read, 1)

            def prologue():
                norm(0, 0)
                for s in sorted(ORDER):
                    if s in QKV:
                        qkv(0, QKV[s], 0)
                    if s in CUM:
                        cum(0, CUM[s])
                own_p.end()

            def body(c, i, u, more):
                own_s.begin(c)
                for s in range(NS):
                    dve.wait_ge(gate_ok, NS * c + s + 1)
                    if s < SW:
                        own_s.link(v.scalar_tensor_tensor(gated[:, s % 2], gate[:, s % 2], 1.0, stream[s % 2][1][:], ALU.add, ALU.mult))
                        dve.wait_ge(down_ok, NS * c + max(s - 2, 0))
                        v.scalar_tensor_tensor(h[:, s % 3], gated[:, s % 2], 0.5, stream[s % 2][0][:], ALU.mult, ALU.mult).then_inc(h_ok, 1)
                    else:
                        dve.wait_ge(down_ok, NS * c + s - 2)
                        v.tensor_tensor(h[:, s % 3], gate[:, s % 2], gate[:, s % 2], ALU.mult).then_inc(h_ok, 1)
                    if more and s == 0:
                        norm(c + 1, 1 - u)
                    if more and s in QKV:
                        qkv(c + 1, QKV[s], 1 - u)
                    if more and s in CUM:
                        cum(c + 1, CUM[s])
                own_s.end()
                dve.wait_ge(down_ok, NS * c + NS)
                dve.wait_ge(xx_ok, c + 1)
                for b in range(2):
                    x2 = x_t[:, u, 2 * b:2 * b + 2].rearrange("p t d -> p (t d)")
                    v.tensor_tensor(x2, x2, acc[b][:], ALU.add).then_inc(res_ok, 1)

            chunks(dve, body, prologue)


def expert_blocks(nc, k, st):
    sem, sb = k.sem, lambda name, shape, dt=F32: k.sb(st, name, shape, dt)
    RING = 3
    xg = sb("e_xg", [P, RING, 2, D])
    xgT = sb("e_xgT", [P, 2, 2, KT, P])
    r = sb("e_r", [P, 2, 2, I0])
    actT = sb("e_actT", [P, 2, 2, P])
    ys = sb("e_ys", [P, RING, 2, D])
    x_in = [sem(f"e_x_in{n}") for n in range(RING)]
    y_out = [sem(f"e_y_out{n}") for n in range(RING)]
    turned, xgT_ok, up_ok, r_ok = sem("e_turned"), sem("e_xgT_ok"), sem("e_up_ok"), sem("e_r_ok")
    back, actT_ok, down_ok, y_ok = sem("e_back"), sem("e_actT_ok"), sem("e_down_ok"), sem("e_y_ok")
    xg_v = k.dram["xg"].rearrange("(q b p) d -> q p b d", p=P, b=2)
    y_v = k.dram["y"].rearrange("(q b p) d -> q p b d", p=P, b=2)
    NQ = NB // 2
    STEPS = 6
    LOOPS = (NQ - 5) // STEPS

    def steps(eng, step):
        def one(q):
            step(q, q % STEPS, q // STEPS)
        one(0)
        one(1)
        with eng.Fori(0, LOOPS) as i:
            for j in range(2, STEPS + 2):
                step(STEPS * i + j, j % STEPS, i + j // STEPS)
        for q in range(LOOPS * STEPS + 2, NQ):
            one(q)

    def ring(rem, i, n):
        return i * (STEPS // RING) + (rem + n) // RING

    def wait(eng, s, value):
        if not isinstance(value, int) or value > 0:
            eng.wait_ge(s, value)

    def known(q, n):
        return not isinstance(q, int) or 0 <= q + n < NQ

    with nc.Block() as block:

        @block.sync
        def _(sp):
            def load(q, rem, i, n):
                b = (rem + n) % RING
                sp.dma_start(xg[:, b], xg_v[q + n]).then_inc(x_in[b], 16)

            def step(q, rem, i):
                if known(q, RING):
                    sp.wait_ge(turned, q + 1)
                    load(q, rem, i, RING)
                sp.wait_ge(y_ok, q + 1)
                sp.dma_start(y_v[q], ys[:, rem % RING]).then_inc(y_out[rem % RING], 16)

            for n in range(RING):
                load(0, 0, 0, n)
            steps(sp, step)
            for b in range(RING):
                sp.wait_ge(y_out[b], 16 * len(range(b, NQ, RING)))

        @block.tensor
        def _(pe):
            t_ = nc.tensor

            def turn(q, rem, i, n):
                b, two = (rem + n) % RING, (rem + n) % 2
                pe.wait_ge(x_in[b], 16 * ring(rem, i, n) + 16)
                wait(pe, xgT_ok, q + n - 1)
                for blk in range(2):
                    for f in range(KT):
                        o = (blk * KT + f) * P
                        m = t_.transpose(k.ps[two][:, o:o + P], xg[:, b, blk, f * P:(f + 1) * P], k.ident[:])
                m.then_inc(turned, 1)

            def expert(q, n, blk):
                at = 2 * (q + n) + blk
                here = k.block_expert[0:1, bass.ds(at, 1)] if not isinstance(at, int) else k.block_expert[0:1, at:at + 1]
                return pe.value_load(here, min_val=0, max_val=E0 - 1)

            def up(q, rem, i, n, experts):
                two = (rem + n) % 2
                pe.wait_ge(xgT_ok, q + n + 1)
                wait(pe, r_ok, q + n - 1)
                for blk in range(2):
                    e = experts[blk]
                    for f in range(KT):
                        m = t_.matmul(k.ps[2 + two][:, blk * I0:(blk + 1) * I0], xgT[:, two, blk, f],
                                      k.wu[:, bass.ds(e, 1), f].rearrange("p a i -> p (a i)"), start=(f == 0), stop=(f == KT - 1))
                m.then_inc(up_ok, 1)

            def turn_back(q, rem, i):
                two = rem % 2
                pe.wait_ge(r_ok, q + 1)
                wait(pe, actT_ok, q - 1)
                for blk in range(2):
                    m = t_.transpose(k.ps[4 + two][:, blk * P:(blk + 1) * P], r[:, two, blk], k.ident[:])
                m.then_inc(back, 1)

            def down(q, rem, i, n, experts):
                two = (rem + n) % 2
                pe.wait_ge(actT_ok, q + n + 1)
                wait(pe, y_ok, q + n - 1)
                for blk in range(2):
                    e = experts[blk]
                    m = t_.matmul(k.ps[6 + two][:, blk * D:(blk + 1) * D], actT[:, two, blk],
                                  k.wd[:, bass.ds(e, 1)].rearrange("p a d -> p (a d)"), start=True, stop=True)
                m.then_inc(down_ok, 1)

            def step(q, rem, i):
                before = [expert(q, -1, blk) for blk in range(2)] if known(q, -1) else None
                behind = [expert(q, 1, blk) for blk in range(2)] if known(q, 1) else None
                if before:
                    down(q, rem, i, -1, before)
                if known(q, 2):
                    turn(q, rem, i, 2)
                turn_back(q, rem, i)
                if behind:
                    up(q, rem, i, 1, behind)

            pe.wait_ge(k.experts_in, k.NEXPERTS)
            turn(0, 0, 0, 0)
            turn(0, 0, 0, 1)
            up(0, 0, 0, 0, [expert(0, 0, blk) for blk in range(2)])
            steps(pe, step)
            down(NQ - 1, (NQ - 1) % STEPS, (NQ - 1) // STEPS, 0, [expert(NQ - 1, 0, blk) for blk in range(2)])

        @block.vector
        def _(dve):
            v = nc.vector

            def turned_out(q, rem, i, n):
                two = (rem + n) % 2
                dve.wait_ge(turned, q + n + 1)
                wait(dve, up_ok, q + n - 1)
                v.tensor_copy(xgT[:, two].rearrange("p b f n -> p (b f n)"), k.ps[two][:]).then_inc(xgT_ok, 1)

            def result(q, rem, i, n):
                b, two = (rem + n) % RING, (rem + n) % 2
                dve.wait_ge(down_ok, q + n + 1)
                wait(dve, y_out[b], 16 * ring(rem, i, n))
                v.tensor_copy(ys[:, b].rearrange("p b d -> p (b d)"), k.ps[6 + two][:]).then_inc(y_ok, 1)

            def step(q, rem, i):
                if known(q, -1):
                    result(q, rem, i, -1)
                if known(q, 2):
                    turned_out(q, rem, i, 2)

            turned_out(0, 0, 0, 0)
            turned_out(0, 0, 0, 1)
            steps(dve, step)
            result(NQ - 1, (NQ - 1) % STEPS, (NQ - 1) // STEPS, 0)

        @block.scalar
        def _(act):
            a = nc.scalar

            def relu(q, rem, i, n):
                two = (rem + n) % 2
                act.wait_ge(up_ok, q + n + 1)
                wait(act, back, q + n - 1)
                a.activation(r[:, two].rearrange("p b i -> p (b i)"), k.ps[2 + two][:, 0:2 * I0], ACT.Relu).then_inc(r_ok, 1)

            def square(q, rem, i):
                two = rem % 2
                act.wait_ge(back, q + 1)
                wait(act, down_ok, q - 1)
                a.activation(actT[:, two].rearrange("p b n -> p (b n)"), k.ps[4 + two][:, 0:2 * P], ACT.Square).then_inc(actT_ok, 1)

            def step(q, rem, i):
                square(q, rem, i)
                if known(q, 1):
                    relu(q, rem, i, 1)

            relu(0, 0, 0, 0)
            steps(act, step)


class Banks:

    def __init__(self, sem, tag, plan):
        self.at, self.per_round = {}, [0] * 8
        for name, bank in plan:
            assert name not in self.at, name
            self.at[name] = bank, self.per_round[bank]
            self.per_round[bank] += 1
        self.filled = [sem(f"{tag}_filled{b}") for b in range(8)]
        self.drained = [sem(f"{tag}_drained{b}") for b in range(8)]

    def fill(self, eng, name, c):
        bank, nth = self.at[name]
        eng.wait_ge(self.drained[bank], c * self.per_round[bank] + nth)
        return bank

    def full(self, ins, name):
        ins.then_inc(self.filled[self.at[name][0]], 1)

    def read(self, eng, name, c):
        bank, nth = self.at[name]
        eng.wait_ge(self.filled[bank], c * self.per_round[bank] + nth + 1)
        return bank

    def drain(self, ins, name):
        ins.then_inc(self.drained[self.at[name][0]], 1)

    def passed(self, eng, name, c):
        bank, nth = self.at[name]
        eng.wait_ge(self.drained[bank], c * self.per_round[bank] + nth + 1)

    def rounds(self, eng, name, c):
        bank, _ = self.at[name]
        eng.wait_ge(self.filled[bank], c * self.per_round[bank])


def load_layer1(nc, k, pool):
    g = nc.gpsimd
    n = 0
    for f in range(KT):
        for tile in (k.w1, k.w3):
            g.memset(tile[:, f, ROWS1:SLOTS1 * P].bitcast(F32), 0.0)
    g.memset(k.w2[:, SLOTS1 - 1].bitcast(F32), 0.0).then_inc(k.padded, 1)
    pool.wait_ge(k.padded, 1)
    for f in range(KT):
        for tile, name in ((k.w1, "w1"), (k.w3, "w3")):
            g.dma_start(tile[:, f, 0:ROWS1], k.io[name][f * P:(f + 1) * P]).then_inc(k.layer1_in, 16)
            n += 16
    full = ROWS1 // P
    g.dma_start(k.w2[:, 0:full], k.io["w2"][0:full * P].rearrange("(s p) d -> p s d", p=P)).then_inc(k.layer1_in, 16)
    g.dma_start(k.w2[0:ROWS1 - full * P, full], k.io["w2"][full * P:ROWS1]).then_inc(k.layer1_in, 16)
    assert n + 32 == k.NLAYER1


def layer1(nc, k, st):
    sem, sb = k.sem, lambda name, shape, dt=F32: k.sb(st, name, shape, dt)
    K = TOP0
    yk = sb("l_yk", [P, TP, K, D])
    x1 = sb("l_x1", [P, TP, D])
    xn = sb("l_xn", [P, TP, D])
    res = sb("l_res", [P, TP, D])
    slots = sb("l_slots", [P, TP * K], I32)
    w4 = sb("l_w4", [P, TP * K])
    stats = sb("l_stats", [P, TP, 6])
    mv = sb("l_mv", [P, TP, 2])
    var = sb("l_var", [P, TP])
    rstd = sb("l_rstd", [P, TP])
    ssx = sb("l_ssx", [P, TP])
    ms = sb("l_ms", [P, TP])
    rms = sb("l_rms", [P, TP])
    xh = sb("l_xh", [P, KT, CH], F32R)
    xl = sb("l_xl", [P, KT, CH], F32R)
    wqh, wql = sb("l_wqh", [P, KT, D], F32R), sb("l_wql", [P, KT, D], F32R)
    woh, wol = sb("l_woh", [P, KT, D], F32R), sb("l_wol", [P, KT, D], F32R)
    rms_w = sb("l_rms_w", [P, KT])
    bq, bo = sb("l_bq", [P, D]), sb("l_bo", [P, D])
    gate_w = sb("l_gate_w", [P, KT, E1])
    gwh, gwl = sb("l_gwh", [P, KT, E1], F32R), sb("l_gwl", [P, KT, E1], F32R)
    gate_b = sb("l_gate_b", [P, E1])
    root = sb("l_root", [P, TP * E1])
    absx, expx, wplus, lnw, zero, dif, score, biased = (sb(f"l_g{n}", [P, TP, E1]) for n in range(8))
    spos = sb("l_spos", [P, TP, E1])
    top8 = sb("l_top8", [P, TP, 8])
    index8 = sb("l_index8", [P, TP, 8], U32)
    chosen = sb("l_chosen", [P, TP, TOP1])
    onehot = sb("l_onehot", [P, TP, E1])
    onehot2 = sb("l_onehot2", [P, TP, E1])
    cw = sb("l_cw", [P, TP, E1])
    cwT = sb("l_cwT", [E1, CH])
    cb = sb("l_cb", [P, ROUTED1, CH])
    v_aug = sb("l_v", [P, TP, H1, DK + 1])
    cos, sin = sb("l_cos", [P, TP, DK]), sb("l_sin", [P, TP, DK])
    qr = sb("l_qr", [P, TP, H1, DK])
    rot = sb("l_rot", [P, TP, H1, DK])
    squares = rot[:].rearrange("p t h d -> p t (h d)")
    qa = sb("l_qa", [P, 2, H1, 64], F32R)
    kb = sb("l_kb", [P, 2, H1, 64], F32R)
    qaT = sb("l_qaT", [P, H1 // 2, S1], F32R)
    kbT = sb("l_kbT", [P, H1 // 2, S1], F32R)
    mx = sb("l_mx", [P, 2, 2, H1 // 2])
    pt0 = sb("l_pt0", [P, 2, 4, S1])
    wq = pt0[:, 0].rearrange("p (f a) n -> p f (a n)", f=KT)[:, :, 0:D]
    wo = pt0[:, 1].rearrange("p (f a) n -> p f (a n)", f=KT)[:, :, 0:D]
    pt1 = sb("l_pt1", [P, 2, 4, P])
    rsum = sb("l_rsum", [P, 2, 2, H1 // 2])
    on = sb("l_on", [P, 2, D])
    oh, ol = sb("l_oh", [P, KT, CH], F32R), sb("l_ol", [P, KT, CH], F32R)
    mask1, mask2, ident_bf = sb("l_mask1", [P, P], BF16), sb("l_mask2", [P, P], BF16), sb("l_ident_bf", [P, P], BF16)
    gate, gated = sb("l_gate", [P, 2, CH]), sb("l_gated", [P, 2, CH])
    hc = sb("l_hc", [P, 2, CH])
    hh, hl = sb("l_hh", [P, 2, CH], F32R), sb("l_hl", [P, 2, CH], F32R)

    SLOT = [ROUTED1 + n for n in range(SLOTS1 - ROUTED1)] + list(range(ROUTED1))
    WORK = [("ffn", 0), ("ffn", 1), ("split", 0), ("weights", 0)]
    turns = iter(range(2, SLOTS1))
    for b in range(2):
        WORK += [("sides", b), ("ffn", next(turns)), ("scores", b, 0), ("scores", b, 1)]
        if b == 1:
            WORK += [("turn_out", 0)]
        WORK += [("ffn", next(turns)), ("scores", b, 2), ("scores", b, 3), ("ffn", next(turns)), ("again", b)]
        WORK += [("ffn", next(turns)), ("probs", b, 0), ("probs", b, 1)]
        if b == 0:
            WORK += [("split", 1)]
        WORK += [("ffn", next(turns)), ("values", b, 0), ("probs", b, 2), ("probs", b, 3)]
        if b == 0:
            WORK += [("values", b, 1)]
    WORK += [("ffn", next(turns)), ("values", 1, 1), ("ffn", SLOTS1), ("turn_out", 1), ("ffn", SLOTS1 + 1)]
    assert next(turns, None) is None
    assert [w[1] for w in WORK if w[0] == "ffn"] == list(range(SLOTS1 + 2))
    GROUPS = [(g, kind, par, pp) for g in range(2) for kind, par, pp in
              [("two", 0, 0), ("two", 1, 0), ("two", 0, 1), ("two", 1, 1), ("four", 0, None), ("four", 1, None)]]
    SIDES = [(name, n) for n in range(4) for name in ("kb", "qa")]

    plan, turn = [], [0]

    def put(name):
        plan.append((name, 3 + turn[0] % 3))
        turn[0] += 1

    for f in range(KT):
        put(f"x{f}")
    put("logits")
    for t in range(TP):
        put(f"q{t}")
    for what, *at in WORK:
        if what == "ffn" and at[0] == 1:
            put("a1")
            put("b1")
        elif what == "ffn" and at[0] < SLOTS1:
            plan += [(f"a{at[0]}", 6), (f"b{at[0]}", 7)]
        if what == "weights":
            put("cw")
        if what == "sides":
            for name, n in SIDES:
                put(f"{name}{at[0]}{n}")
        if what == "scores":
            for n in range(3 * at[1], 3 * at[1] + 3):
                put(f"s{at[0]}{n}")
        if what == "again":
            for n in range(4):
                put(f"qm{at[0]}{n}")
        if what == "probs":
            for n in range(3 * at[1], 3 * at[1] + 3):
                put(f"p{at[0]}{n}")
        if what == "values":
            plan.append((f"o{at[0]}{at[1]}", 2))
        if what == "turn_out":
            put(f"oT{at[0]}")
    plan += [("acc0", 0), ("acc1", 1)]
    banks = Banks(sem, "l", plan)

    consts, NCL = sem("l_consts"), 16 * 13
    r_in, y_in, slots_ok, out_st = sem("l_r_in"), sem("l_y_in"), sem("l_slots_ok"), sem("l_out")
    comb_ok, var_ok, rstd_ok, xn_ok = sem("l_comb_ok"), sem("l_var_ok"), sem("l_rstd_ok"), sem("l_xn_ok")
    ssx_ok, ms_ok, rms_ok, xh_ok = sem("l_ssx_ok"), sem("l_ms_ok"), sem("l_rms_ok"), sem("l_xh_ok")
    abs_ok, exp_ok, wplus_ok, ln_ok = sem("l_abs_ok"), sem("l_exp_ok"), sem("l_wplus_ok"), sem("l_ln_ok")
    sp_ok, score_ok, cw_ok = sem("l_sp_ok"), sem("l_score_ok"), sem("l_cw_ok")
    c_out, cb_in = sem("l_c_out"), [sem(f"l_cb_in{s}") for s in range(ROUTED1)]
    rope_ok, hi_ok, lo_ok, mrow_ok = sem("l_rope_ok"), sem("l_hi_ok"), sem("l_lo_ok"), sem("l_mrow_ok")
    oh_ok = sem("l_oh_ok")
    prep_w, xx_ok = sem("l_prep_w"), sem("l_xx_ok")
    tanh_ok, h_ok, hh_ok, hl_ok, down_ok = sem("l_tanh_ok"), sem("l_h_ok"), sem("l_hh_ok"), sem("l_hl_ok"), sem("l_down_ok")
    dve_own, dve_front, pool_own, dve_once, stand = sem("l_dve"), sem("l_dve_front"), sem("l_pool"), sem("l_dve_once"), sem("l_stand")

    x_v = k.dram["r"].rearrange("(c t p) d -> c p t d", p=P, t=TP)
    out_v = k.out.rearrange("(c t p) d -> c p t d", p=P, t=TP)
    c_v = k.dram["cw"]
    ROWS = []
    for s in range(ROUTED1):
        p = 0
        while p < P:
            e = (s * P + p) // I1
            end = min(P, (e + 1) * I1 - s * P)
            ROWS.append((s, p, end, e))
            p = end

    PARTS = [len([r for r in ROWS if r[0] == s]) for s in range(ROUTED1)]

    with nc.Block() as block:

        @block.sync
        def _(sp):
            for tile, name in ((wq, "wq"), (wo, "wo"), (gate_w, "gate_w1")):
                sp.dma_start(tile if name != "gate_w1" else tile[:], k.io[name].rearrange("(f p) n -> p f n", p=P)).then_inc(consts, 16)
            for tile, name in ((rms_w, "rms_w"), (bq, "bq"), (bo, "bo"), (gate_b, "gate_b1"), (cos, "cos"), (sin, "sin"),
                               (mask1, "mask1"), (mask2, "mask2"), (ident_bf, "ident_bf")):
                sp.dma_start(tile[:], k.io[name]).then_inc(consts, 16)
            sp.dma_start(root[:], k.io["root"]).then_inc(consts, 16)
            sp.dma_start(x1[:], x_v[0]).then_inc(r_in, 16)

            def body(c, more):
                banks.passed(sp, "cw", c)
                sp.dma_start(c_v[c], cwT[:]).then_inc(c_out, 16)
                sp.wait_ge(c_out, 16 * c + 16)
                sp.sem_inc(stand, 1)
                sp.wait_ge(h_ok, SLOTS1 * c)
                sp.sem_inc(stand, 1)
                for s, p, end, e in ROWS:
                    sp.dma_start(cb[p:end, s], c_v[c, e:e + 1].to_broadcast([end - p, CH])).then_inc(cb_in[s], 16)
                if more:
                    sp.wait_ge(xx_ok, c + 1)
                    sp.dma_start(x1[:], x_v[c + 1]).then_inc(r_in, 16)
                for n in range(2):
                    banks.passed(sp, f"acc{n}", c)
                sp.dma_start(out_v[c], res[:]).then_inc(out_st, 16)

            with sp.Fori(0, NCH - 1) as c:
                body(c, True)
            body(NCH - 1, False)
            sp.wait_ge(out_st, 16 * NCH)

        @block.gpsimd
        def _(pool):
            g = nc.gpsimd
            own = Chain(pool, pool_own, 1)
            load_layer1(nc, k, pool)

            def slots_of(n):
                at = k.slot_of[:, bass.ds(n * TP * K, TP * K)] if not isinstance(n, int) else k.slot_of[:, n * TP * K:(n + 1) * TP * K]
                if not isinstance(n, int) or n:
                    pool.wait_ge(comb_ok, n)
                    pool.sem_inc(stand, 1)
                g.tensor_copy(slots[:], at).then_inc(slots_ok, 1)
                pool.wait_ge(slots_ok, n + 1)
                pool.sem_inc(stand, 1)

            def gather(numbers):
                for n in numbers:
                    g.indirect_dma_start(yk[:, n // K, n % K], None, k.dram["y"],
                                         bass.IndirectOffsetOnAxis(ap=slots[:, n:n + 1], axis=0)).then_inc(y_in, 16)

            def std(n):
                pool.wait_ge(var_ok, n + 1)
                g.tensor_tensor(rstd[:], var[:], k.power[:, 0:TP], ALU.pow).then_inc(rstd_ok, 1)

            def rms_of(n):
                pool.wait_ge(ms_ok, n + 1)
                g.tensor_tensor(rms[:], ms[:], k.power[:, 0:TP], ALU.pow).then_inc(rms_ok, 1)

            def body(c, more):
                own.begin(c)
                pool.wait_ge(out_st, 16 * c)
                own.link(g.tensor_tensor(res[:], x1[:], xn[:], ALU.add))
                g.tensor_tensor(res[:], res[:], bo[:].unsqueeze(1).to_broadcast([P, TP, D]), ALU.add).then_inc(xx_ok, 1)
                pool.wait_ge(sp_ok, c + 1)
                g.tensor_tensor(score[:].rearrange("p t e -> p (t e)"), spos[:].rearrange("p t e -> p (t e)"),
                                root[:], ALU.pow).then_inc(score_ok, 1)
                own.end()
                for n in range(1, SLOTS1 + 1):
                    if more and n == 2:
                        slots_of(c + 1)
                    if more and 3 <= n < 11:
                        gather(range(2 * n - 6, 2 * n - 4))
                    s = n - 1
                    pool.wait_ge(hh_ok, SLOTS1 * c + s + 1)
                    pool.wait_ge(down_ok, (SLOTS1 - 1) * c + max(s - 1, 0))
                    g.tensor_tensor(hl[:, s % 2], hc[:, s % 2], hh[:, s % 2].bitcast(F32), ALU.subtract).then_inc(hl_ok, 1)
                    if more and n == SLOTS1 - 1:
                        std(c + 1)
                if more:
                    rms_of(c + 1)

            slots_of(0)
            gather(range(TP * K))
            std(0)
            rms_of(0)
            with pool.Fori(0, NCH - 1) as c:
                body(c, True)
            body(NCH - 1, False)

        @block.scalar
        def _(act):
            a = nc.scalar
            act.wait_ge(consts, NCL)

            def squared(n):
                act.wait_ge(xn_ok, TP * n + TP)
                if not isinstance(n, int) or n:
                    act.wait_ge(ms_ok, n)
                for t in range(TP):
                    ins = a.activation(squares[:, t], xn[:, t], ACT.Square, accum_out=ssx[:, t:t + 1])
                ins.then_inc(ssx_ok, 1)

            def ffn(c, n):
                if 1 <= n <= SLOTS1:
                    s = n - 1
                    act.wait_ge(h_ok, SLOTS1 * c + s + 1)
                    act.wait_ge(down_ok, (SLOTS1 - 1) * c + max(s - 1, 0))
                    a.activation(hh[:, s % 2], hc[:, s % 2], ACT.Copy).then_inc(hh_ok, 1)
                if n < SLOTS1:
                    bank = banks.read(act, f"a{n}", c)
                    a.activation(gate[:, n % 2], k.ps[bank][:], ACT.Tanh, scale=0.5).then_inc(tanh_ok, 1)

            def split(c, b):
                act.wait_ge(rope_ok, c + 1)
                if b:
                    for n in range(1, 4):
                        banks.read(act, f"qm{b - 1}{n}", c)
                src = qr[:, 2 * b:2 * b + 2].rearrange("p t h d -> p (t h) d")
                kbv = kb[:].rearrange("p t h d -> p (t h) d")
                qav = qa[:].rearrange("p t h d -> p (t h) d")
                for dst, lo in ((kbv, 0), (kbv, DK), (qav, 0), (qav, 2 * DK)):
                    a.activation(dst[:, :, lo:lo + DK], src, ACT.Copy).then_inc(hi_ok, 1)

            def turned(c, name, tile, n):
                bank = banks.read(act, name, c)
                banks.drain(a.activation(tile[:, 2 * n:2 * n + 2].rearrange("p a n -> p (a n)"), k.ps[bank][:], ACT.Copy), name)

            def body(c, more):
                for f in range(KT):
                    bank = banks.read(act, f"x{f}", c)
                    a.activation(xh[:, f], k.ps[bank][:], ACT.Copy).then_inc(xh_ok, 1)
                banks.passed(act, "logits", c)
                a.activation(expx[:], absx[:], ACT.Exp, scale=-1.0).then_inc(exp_ok, 1)
                act.wait_ge(wplus_ok, c + 1)
                a.activation(lnw[:], wplus[:], ACT.Ln).then_inc(ln_ok, 1)
                for what, *at in WORK:
                    b = at[0]
                    if what == "ffn":
                        ffn(c, at[0])
                    if what == "weights":
                        bank = banks.read(act, "cw", c)
                        act.wait_ge(c_out, 16 * c)
                        banks.drain(a.activation(cwT[:], k.ps[bank][0:E1, :], ACT.Copy), "cw")
                    if what == "split":
                        split(c, b)
                    if what == "sides":
                        for n in range(4):
                            turned(c, f"kb{b}{n}", kbT, n)
                    if what == "again":
                        for n in (1, 3):
                            turned(c, f"qm{b}{n}", qaT, n)
                    if what == "probs":
                        for n in range(3 * at[1], 3 * at[1] + 3):
                            g, kind, par, pp = GROUPS[n]
                            bank = banks.read(act, f"p{b}{n}", c)
                            if n == 6:
                                banks.read(act, f"o{b}0", c)
                            dst = pt0[:, par, 2 * pp:2 * pp + 2] if kind == "two" else pt1[:, par]
                            banks.drain(a.activation(dst.rearrange("p a n -> p (a n)"), k.ps[bank][:], ACT.Exp, scale=DK ** -0.5), f"p{b}{n}")
                    if what == "turn_out":
                        bank = banks.read(act, f"oT{b}", c)
                        a.activation(oh[:, :, b * S1:(b + 1) * S1], k.ps[bank][:].rearrange("p (f n) -> p f n", f=KT), ACT.Copy).then_inc(oh_ok, 1)
                if more:
                    squared(c + 1)

            squared(0)
            with act.Fori(0, NCH - 1) as c:
                body(c, True)
            body(NCH - 1, False)

        @block.tensor
        def _(pe):
            t_ = nc.tensor
            pe.wait_ge(consts, NCL)
            pe.wait_ge(k.layer1_in, k.NLAYER1)
            pe.wait_ge(prep_w, 4)

            def three(out, left, right, start, stop, **kw):
                parts = [(l, r, f) for l, r in ((0, 0), (1, 0), (0, 1)) for f in range(KT)]
                for n, (l, r, f) in enumerate(parts):
                    m = t_.matmul(out, left(l, f), right(r, f), start=(start and n == 0), stop=(stop and n == len(parts) - 1), **kw)
                return m

            def side(c, name, tile, n):
                bank = banks.fill(pe, name, c)
                for a in range(2):
                    for t in range(2):
                        o, pair = (a * 2 + t) * P, 2 * n + a
                        m = t_.transpose(k.ps[bank][:, o:o + P], tile[:, t].bitcast(F32).rearrange("p h d -> p (h d)")[:, pair * P:(pair + 1) * P], k.ident[:])
                banks.full(m, name)

            def score_bank(c, name, n, first, rows_used, left, right, mask):
                g, kind, par, pp = GROUPS[n]
                bank = banks.fill(pe, name, c)
                rows = slice(64 * par, 64 * par + rows_used)
                heads = range(4 * g, 4 * g + 4) if kind == "four" else range(4 * g + 2 * pp, 4 * g + 2 * pp + 2)
                for a, pair in enumerate(heads):
                    if kind == "two":
                        o, l, r = slice(a * S1, (a + 1) * S1), slice(first * P, (first + 1) * P), slice(0, S1)
                    else:
                        o = slice(a * P, (a + 1) * P)
                        l = r = slice((1 - first) * P, (2 - first) * P)
                    t_.matmul(k.ps[bank][:, o], left[rows, pair, l], right[rows, pair, r], start=(a == 0), stop=False, skip_group_check=True)
                masked = k.ps[bank][:].rearrange("p (a n) -> p a n", a=len(heads))
                if kind == "two":
                    masked = masked[:, :, first * P:(first + 1) * P]
                m = t_.matmul(masked, ident_bf[:], mask[:].unsqueeze(1).to_broadcast([P, len(heads), P]),
                              start=False, stop=True, skip_group_check=True)
                banks.full(m, name)

            def values(c, b, g):
                for n in range(6 * g + 3, 6 * g + 6):
                    banks.passed(pe, f"p{b}{n}", c)
                bank = banks.fill(pe, f"o{b}{g}", c)
                for a in range(4):
                    for par in range(2):
                        head = 2 * (4 * g + a) + par
                        o = [slice((t * 8 + 2 * a + par) * (DK + 1), (t * 8 + 2 * a + par + 1) * (DK + 1)) for t in range(2)]
                        v0, v1 = v_aug[:, 2 * b, head], v_aug[:, 2 * b + 1, head]
                        t_.matmul(k.ps[bank][:, o[0]], pt0[:, par, a, 0:P], v0, start=True, stop=True)
                        t_.matmul(k.ps[bank][:, o[1]], pt0[:, par, a, P:S1], v0, start=True, stop=False)
                        m = t_.matmul(k.ps[bank][:, o[1]], pt1[:, par, a], v1, start=False, stop=True)
                banks.full(m, f"o{b}{g}")

            def up(c, n):
                s = SLOT[n]
                for name, w in (("a", k.w1), ("b", k.w3)):
                    bank = banks.fill(pe, f"{name}{n}", c)
                    parts = [(x, f) for x in (xh, xl) for f in range(KT)]
                    for i, (x, f) in enumerate(parts):
                        m = t_.matmul(k.ps[bank][:], w[:, f, s * P:(s + 1) * P], x[:, f], start=(i == 0), stop=(i == len(parts) - 1))
                    banks.full(m, f"{name}{n}")

            def down(c, n):
                if n == 0:
                    for i in range(2):
                        banks.fill(pe, f"acc{i}", c)
                pe.wait_ge(hh_ok, SLOTS1 * c + n + 1)
                pe.wait_ge(hl_ok, SLOTS1 * c + n + 1)
                for i, x in enumerate((hh, hl)):
                    for t in range(TP):
                        m = t_.matmul(k.ps[t // 2][:, (t % 2) * D:(t % 2 + 1) * D], x[:, n % 2, t * P:(t + 1) * P], k.w2[:, SLOT[n]],
                                      start=(n == 0 and i == 0 and t % 2 == 0), stop=False, skip_group_check=True)
                if n < SLOTS1 - 1:
                    m.then_inc(down_ok, 1)

            def body(c):
                pe.wait_ge(xn_ok, TP * c + TP)
                for f in range(KT):
                    bank = banks.fill(pe, f"x{f}", c)
                    for t in range(TP):
                        m = t_.transpose(k.ps[bank][:, t * P:(t + 1) * P], xn[:, t, f * P:(f + 1) * P], k.ident[:])
                    banks.full(m, f"x{f}")
                for f in range(KT):
                    banks.passed(pe, f"x{f}", c)
                bank = banks.fill(pe, "logits", c)
                for t in range(TP):
                    m = three(k.ps[bank][:, t * E1:(t + 1) * E1], lambda l, f: (xh, xl)[l][:, f, t * P:(t + 1) * P],
                              lambda r, f: (gwh, gwl)[r][:, f], True, True)
                banks.full(m, "logits")
                for t in range(TP):
                    bank = banks.fill(pe, f"q{t}", c)
                    m = three(k.ps[bank][:, 0:D], lambda l, f: (xh, xl)[l][:, f, t * P:(t + 1) * P],
                              lambda r, f: (wqh, wql)[r][:, f], True, True)
                    banks.full(m, f"q{t}")
                for what, *at in WORK:
                    b = at[0]
                    if what == "ffn":
                        n = at[0]
                        if n < SLOTS1:
                            up(c, n)
                        if n >= 2:
                            down(c, n - 2)
                    if what == "weights":
                        bank = banks.fill(pe, "cw", c)
                        pe.wait_ge(cw_ok, c + 1)
                        for t in range(TP):
                            m = t_.transpose(k.ps[bank][0:E1, t * P:(t + 1) * P], cw[:, t], k.ident[:])
                        banks.full(m, "cw")
                    if what == "sides":
                        pe.wait_ge(hi_ok, 4 * (2 * c + b) + 4)
                        pe.wait_ge(lo_ok, 2 * (2 * c + b) + 2)
                        for name, n in SIDES:
                            side(c, f"{name}{b}{n}", {"kb": kb, "qa": qa}[name], n)
                    if what == "scores":
                        if at[1] == 0:
                            for name, n in SIDES[-3:]:
                                banks.passed(pe, f"{name}{b}{n}", c)
                        for n in range(3 * at[1], 3 * at[1] + 3):
                            score_bank(c, f"s{b}{n}", n, 1, 3 * DK, qaT, kbT, mask1)
                    if what == "again":
                        pe.wait_ge(mrow_ok, 2 * c + b + 1)
                        for n in range(4):
                            side(c, f"qm{b}{n}", qa, n)
                    if what == "probs":
                        if at[1] == 0:
                            for n in range(1, 4):
                                banks.passed(pe, f"qm{b}{n}", c)
                        for n in range(3 * at[1], 3 * at[1] + 3):
                            score_bank(c, f"p{b}{n}", n, 0, 3 * DK + 2, kbT, qaT, mask2)
                    if what == "values":
                        values(c, b, at[1])
                    if what == "turn_out":
                        bank = banks.fill(pe, f"oT{b}", c)
                        banks.passed(pe, f"o{b}1", c)
                        for f in range(KT):
                            for t in range(2):
                                m = t_.transpose(k.ps[bank][:, (f * 2 + t) * P:(f * 2 + t + 1) * P], on[:, t, f * P:(f + 1) * P], k.ident[:])
                        banks.full(m, f"oT{b}")
                for b in range(2):
                    banks.passed(pe, f"oT{b}", c)
                for t in range(TP):
                    m = three(k.ps[t // 2][:, (t % 2) * D:(t % 2 + 1) * D], lambda l, f: (oh, ol)[l][:, f, t * P:(t + 1) * P],
                              lambda r, f: (woh, wol)[r][:, f], False, True, skip_group_check=True)
                    if t % 2:
                        banks.full(m, f"acc{t // 2}")

            with pe.Fori(0, NCH) as c:
                body(c)

        @block.vector
        def _(dve):
            v = nc.vector
            own, own_f = Chain(dve, dve_own, k.DVE_L, stand), Chain(dve, dve_front, 7, stand)
            once = Chain(dve, dve_once, 0)
            dve.wait_ge(consts, NCL)
            v.memset(qa[:].bitcast(U32), 0)
            v.memset(v_aug[:], 1.0)
            once.link(v.memset(kb[:].bitcast(U32), 0))
            v.tensor_copy(kb[:, :, :, 3 * DK:3 * DK + 2], k.ones[:, 0:2 * H1 * 2].rearrange("p (t h a) -> p t h a", t=2, a=2))
            for f in range(KT):
                ins = v.tensor_scalar(wq[:, f], wq[:, f], rms_w[:, f:f + 1], None, ALU.mult)
            once.link(ins)
            v.tensor_copy(gwh[:], gate_w[:])
            v.tensor_copy(wqh[:], wq).then_inc(prep_w, 1)
            once.link(v.tensor_copy(woh[:], wo))
            dve.wait_ge(prep_w, 1)
            v.tensor_tensor(gwl[:], gate_w[:], gwh[:].bitcast(F32), ALU.subtract)
            v.tensor_tensor(wql[:], wq, wqh[:].bitcast(F32), ALU.subtract).then_inc(prep_w, 1)
            v.tensor_tensor(wol[:], wo, woh[:].bitcast(F32), ALU.subtract).then_inc(prep_w, 2)

            def combine(n, first):
                if first:
                    own_f.begin(n)
                    at = k.weight_of[:, bass.ds(n * TP * K, TP * K)] if not isinstance(n, int) else k.weight_of[:, n * TP * K:(n + 1) * TP * K]
                    own_f.link(v.tensor_copy(w4[:], at))
                    dve.wait_ge(r_in, 16 * n + 16)
                    dve.wait_ge(y_in, 16 * TP * K * (n + 1))
                for j in (0, 1) if first else (2, 3):
                    for t in range(TP):
                        i = t * K + j
                        ins = v.scalar_tensor_tensor(x1[:, t], yk[:, t, j], w4[:, i:i + 1], x1[:, t], ALU.mult, ALU.add)
                    own_f.link(ins)
                if first:
                    return
                dve.sem_inc(comb_ok, 1)
                for t in range(TP):
                    ins = v.bn_stats(stats[:, t], x1[:, t])
                own_f.link(ins, apart=True)
                for t in range(TP):
                    ins = v.bn_aggr(mv[:, t], stats[:, t])
                own_f.link(ins)
                v.tensor_scalar(var[:], mv[:, :, 1], LN_EPS, None, ALU.add).then_inc(var_ok, 1)
                own_f.end()

            def normed(n):
                dve.wait_ge(rstd_ok, n + 1)
                for t in range(TP):
                    v.tensor_scalar(xn[:, t], x1[:, t], mv[:, t, 0:1], rstd[:, t:t + 1], ALU.subtract, ALU.mult).then_inc(xn_ok, 1)

            def mean_square(n):
                dve.wait_ge(ssx_ok, n + 1)
                v.tensor_scalar(ms[:], ssx[:], 1.0 / D, RMS_EPS, ALU.mult, ALU.add).then_inc(ms_ok, 1)

            def choose_two(c):
                dve.wait_ge(score_ok, c + 1)
                own.link(v.tensor_tensor(biased[:], score[:], gate_b[:].unsqueeze(1).to_broadcast([P, TP, E1]), ALU.add), apart=True)
                for t in range(TP):
                    ins = v.max(top8[:, t], biased[:, t])
                own.link(ins, apart=True)
                for t in range(TP):
                    ins = v.max_index(index8[:, t], top8[:, t], biased[:, t])
                own.link(ins)
                own.link(v.tensor_copy(chosen[:], index8[:, :, 0:TOP1]))
                experts = k.iota[:, 0:E1].unsqueeze(1).to_broadcast([P, TP, E1])
                v.tensor_tensor(onehot[:], experts, chosen[:, :, 0:1].to_broadcast([P, TP, E1]), ALU.is_equal)
                own.link(v.tensor_tensor(onehot2[:], experts, chosen[:, :, 1:2].to_broadcast([P, TP, E1]), ALU.is_equal))
                own.link(v.tensor_tensor(onehot[:], onehot[:], onehot2[:], ALU.add))
                v.tensor_tensor(cw[:], onehot[:], score[:], ALU.mult).then_inc(cw_ok, 1)

            def softplus(c):
                dve.wait_ge(wplus_ok, c + 1)
                own.link(v.tensor_scalar(dif[:], wplus[:], -1.0, None, ALU.add))
                own.link(v.tensor_scalar(zero[:], dif[:], 0.0, None, ALU.is_equal))
                own.link(v.tensor_tensor(dif[:], dif[:], zero[:], ALU.add))
                own.link(v.reciprocal(dif[:], dif[:]))
                dve.wait_ge(ln_ok, c + 1)
                own.link(v.tensor_tensor(lnw[:], lnw[:], zero[:], ALU.add))
                own.link(v.tensor_tensor(lnw[:], lnw[:], expx[:], ALU.mult))
                own.link(v.tensor_tensor(lnw[:], lnw[:], dif[:], ALU.mult))
                v.tensor_tensor(spos[:], spos[:], lnw[:], ALU.add).then_inc(sp_ok, 1)

            def rope():
                vq, half = v_aug[:, :, :, 0:DK], DK // 2
                v.tensor_tensor(qr[:], vq, cos[:].unsqueeze(2).to_broadcast([P, TP, H1, DK]), ALU.mult)
                v.tensor_tensor(rot[:, :, :, 0:half], vq[:, :, :, half:DK], sin[:, :, 0:half].unsqueeze(2).to_broadcast([P, TP, H1, half]), ALU.mult)
                own.link(v.tensor_tensor(rot[:, :, :, half:DK], vq[:, :, :, 0:half], sin[:, :, half:DK].unsqueeze(2).to_broadcast([P, TP, H1, half]), ALU.mult))
                v.tensor_tensor(qr[:], qr[:], rot[:], ALU.add).then_inc(rope_ok, 1)

            def ffn(c, n):
                if 1 <= n <= SLOTS1:
                    weighted(c, n - 1)
                if n < SLOTS1:
                    dve.wait_ge(tanh_ok, SLOTS1 * c + n + 1)
                    bank = banks.read(dve, f"a{n}", c)
                    banks.drain(v.scalar_tensor_tensor(gated[:, n % 2], gate[:, n % 2], 1.0, k.ps[bank][:], ALU.add, ALU.mult), f"a{n}")
                    banks.passed(dve, f"a{n}", c)
                    dve.wait_ge(hh_ok, SLOTS1 * c + max(n - 1, 0))
                    dve.wait_ge(hl_ok, SLOTS1 * c + max(n - 1, 0))
                    bank = banks.read(dve, f"b{n}", c)
                    banks.drain(v.scalar_tensor_tensor(hc[:, n % 2], gated[:, n % 2], 0.5, k.ps[bank][:], ALU.mult, ALU.mult), f"b{n}")

            def weighted(c, n):
                banks.passed(dve, f"b{n}", c)
                if SLOT[n] < ROUTED1:
                    dve.wait_ge(cb_in[SLOT[n]], 16 * PARTS[SLOT[n]] * (c + 1))
                    v.tensor_tensor(hc[:, n % 2], hc[:, n % 2], cb[:, SLOT[n]], ALU.mult).then_inc(h_ok, 1)
                else:
                    dve.sem_inc(h_ok, 1)

            def turned(c, name, n):
                bank = banks.read(dve, name, c)
                banks.drain(v.tensor_copy(qaT[:, 2 * n:2 * n + 2].rearrange("p a n -> p (a n)"), k.ps[bank][:]), name)

            def max_rows(c, b):
                for n in (9, 10, 11):
                    banks.passed(dve, f"s{b}{n}", c)
                own.link(v.tensor_scalar(mx[:], mx[:], -1.0, None, ALU.mult))
                top = qa[:].rearrange("p t (q r) d -> p t r q d", r=2)
                for t in range(2):
                    ins = v.tensor_copy(top[:, t, :, :, 3 * DK], mx[:, t])
                own.link(ins)
                for t in range(2):
                    ins = v.tensor_tensor(top[:, t, :, :, 3 * DK + 1], mx[:, t], top[:, t, :, :, 3 * DK].bitcast(F32), ALU.subtract)
                ins.then_inc(mrow_ok, 1)

            def body(c, more):
                own.begin(c)
                for f in range(KT):
                    bank = banks.read(dve, f"x{f}", c)
                    dve.wait_ge(xh_ok, KT * c + f + 1)
                    banks.drain(v.tensor_tensor(xl[:, f], k.ps[bank][:], xh[:, f].bitcast(F32), ALU.subtract), f"x{f}")
                bank = banks.read(dve, "logits", c)
                logits = k.ps[bank][:, 0:TP * E1].rearrange("p (t e) -> p t e", e=E1)
                own.link(v.tensor_scalar(spos[:], logits, 0.0, None, ALU.max))
                banks.drain(v.scalar_tensor_tensor(absx[:], spos[:], 2.0, logits, ALU.mult, ALU.subtract), "logits")
                dve.wait_ge(rms_ok, c + 1)
                for t in range(TP):
                    if t == 1:
                        dve.wait_ge(exp_ok, c + 1)
                        v.tensor_scalar(wplus[:], expx[:], 1.0, None, ALU.add).then_inc(wplus_ok, 1)
                    if t == 2:
                        softplus(c)
                    bank = banks.read(dve, f"q{t}", c)
                    banks.drain(v.scalar_tensor_tensor(v_aug[:, t, :, 0:DK], k.ps[bank][:, 0:D].rearrange("p (h d) -> p h d", h=H1), rms[:, t:t + 1],
                                                       bq[:].rearrange("p (h d) -> p h d", h=H1), ALU.mult, ALU.add), f"q{t}")
                ffn(c, 0)
                for t in range(1, TP):
                    banks.passed(dve, f"q{t}", c)
                rope()
                for what, *at in WORK:
                    b = at[0]
                    if what == "ffn":
                        if at[0]:
                            ffn(c, at[0])
                        if at[0] == 1:
                            choose_two(c)
                        if more and at[0] in (SLOTS1 - 3, SLOTS1 - 2):
                            combine(c + 1, at[0] == SLOTS1 - 3)
                        if more and at[0] == SLOTS1 - 1:
                            normed(c + 1)
                    if what == "split":
                        dve.wait_ge(hi_ok, 4 * (2 * c + b) + 4)
                        q2 = qr[:, 2 * b:2 * b + 2].rearrange("p t h d -> p (t h) d")
                        kbv, qav = kb[:].rearrange("p t h d -> p (t h) d"), qa[:].rearrange("p t h d -> p (t h) d")
                        hi = kbv[:, :, 0:DK].bitcast(F32)
                        v.tensor_tensor(kbv[:, :, 2 * DK:3 * DK], q2, hi, ALU.subtract).then_inc(lo_ok, 1)
                        v.tensor_tensor(qav[:, :, DK:2 * DK], q2, hi, ALU.subtract).then_inc(lo_ok, 1)
                    if what == "sides":
                        for n in range(4):
                            turned(c, f"qa{b}{n}", n)
                    if what == "scores":
                        for n in range(3 * at[1], 3 * at[1] + 3):
                            g, kind, par, pp = GROUPS[n]
                            bank = banks.read(dve, f"s{b}{n}", c)
                            if kind == "two":
                                o, a = mx[:, 1, par, 4 * g + 2 * pp:4 * g + 2 * pp + 2], 2
                            else:
                                o, a = mx[:, 0, par, 4 * g:4 * g + 4], 4
                            banks.drain(v.tensor_reduce(o, k.ps[bank][:].rearrange("p (a n) -> p a n", a=a), AX, ALU.max), f"s{b}{n}")
                        if at[1] == 3:
                            max_rows(c, b)
                    if what == "again":
                        for n in (0, 2):
                            turned(c, f"qm{b}{n}", n)
                    if what == "values":
                        g = at[1]
                        bank = banks.read(dve, f"o{b}{g}", c)
                        o = k.ps[bank][:, 0:H1 * (DK + 1)].rearrange("p (t h d) -> p t h d", t=2, h=H1 // 2)
                        own.link(v.reciprocal(rsum[:, g], o[:, :, :, DK]))
                        banks.drain(v.tensor_tensor(on[:, :, g * P:(g + 1) * P].rearrange("p t (h d) -> p t h d", h=H1 // 2), o[:, :, :, 0:DK],
                                                    rsum[:, g].unsqueeze(3).to_broadcast([P, 2, H1 // 2, DK]), ALU.mult), f"o{b}{g}")
                    if what == "turn_out":
                        bank = banks.read(dve, f"oT{b}", c)
                        dve.wait_ge(oh_ok, 2 * c + b + 1)
                        part = slice(b * S1, (b + 1) * S1)
                        banks.drain(v.tensor_tensor(ol[:, :, part], k.ps[bank][:].rearrange("p (f n) -> p f n", f=KT), oh[:, :, part].bitcast(F32), ALU.subtract), f"oT{b}")
                if more:
                    mean_square(c + 1)
                dve.wait_ge(xx_ok, c + 1)
                for n in range(2):
                    x2 = res[:, 2 * n:2 * n + 2].rearrange("p t d -> p (t d)")
                    banks.read(dve, f"acc{n}", c)
                    banks.drain(v.tensor_tensor(x2, x2, k.ps[n][:], ALU.add), f"acc{n}")
                own.end()

            combine(0, True)
            combine(0, False)
            normed(0)
            mean_square(0)
            with dve.Fori(0, NCH - 1) as c:
                body(c, True)
            body(NCH - 1, False)


def program(nc, io, dram, out):
    with ExitStack() as top:
        def sem(name):
            return top.enter_context(nc.semaphore(name))

        def sb(stack, name, shape, dt=F32):
            return stack.enter_context(nc.sbuf_tensor(name, shape, dt))

        k = Shared()
        k.io, k.dram, k.out, k.sem, k.sb = io, dram, out, sem, sb
        k.ps = [top.enter_context(nc.psum_tensor(f"bank{i}", [P, 512], F32)) for i in range(8)]
        k.ident = sb(top, "ident", [P, P])
        k.upto = sb(top, "upto", [P, P])
        k.ones = sb(top, "ones", [P, P])
        k.before_bf = sb(top, "before_bf", [P, P], BF16)
        k.ones_bf = sb(top, "ones_bf", [P, P], BF16)
        k.iota = sb(top, "iota", [P, NB])
        k.power = sb(top, "power", [P, 32])
        k.slot_of = sb(top, "slot_of", [P, NT * TOP0], I32)
        k.weight_of = sb(top, "weight_of", [P, NT * TOP0])
        k.expert_of = sb(top, "expert_of", [P, NT * TOP0])
        k.rank_of = sb(top, "rank_of", [P, NT * TOP0])
        k.block_f = sb(top, "block_f", [P, NB])
        k.block_expert = sb(top, "block_expert", [P, NB], I32)
        k.consts_in, k.NCONST = sem("consts_in"), 7 * 16
        k.zero_out = sem("zero_out")
        k.DVE_A = 25
        k.DVE_L = 23

        k.NZERO = 16 * (SLOTS // (8 * P))
        k.experts_in, k.NEXPERTS = sem("experts_in"), 16 * 2 * (E0 // 8)
        with ExitStack() as experts:
            k.wu = sb(experts, "wu", [P, E0, KT, I0])
            k.wd = sb(experts, "wd", [P, E0, D])
            with ExitStack() as st:
                route_tokens(nc, k, st)
            with ExitStack() as st:
                mix_tokens(nc, k, st)
            with ExitStack() as st:
                expert_blocks(nc, k, st)
        with ExitStack() as st:
            k.w1 = sb(st, "w1", [P, KT, SLOTS1 * P], F32R)
            k.w3 = sb(st, "w3", [P, KT, SLOTS1 * P], F32R)
            k.w2 = sb(st, "w2", [P, SLOTS1, D], F32R)
            k.layer1_in, k.NLAYER1, k.padded = sem("layer1_in"), 16 * 6, sem("padded")
            layer1(nc, k, st)


def constants():
    import numpy as np
    p = np.arange(P)
    inv = (1.0 / 10000.0 ** (np.arange(0, DK, 2, dtype=np.float32) / DK)).astype(np.float32)
    angle = np.arange(S1, dtype=np.float32)[:, None] * inv[None, :]

    def table(first, second):
        one = np.concatenate([first, second], axis=-1).astype(np.float32)
        return np.ascontiguousarray(np.concatenate([one] * (CH // S1)).reshape(TP, P, DK).transpose(1, 0, 2))

    return {
        "ident": np.eye(P, dtype=np.float32),
        "upto": (p[:, None] <= p[None, :]).astype(np.float32),
        "ones": np.ones((P, P), np.float32),
        "iota": np.ascontiguousarray(np.broadcast_to(np.arange(NB, dtype=np.float32), (P, NB))),
        "before_bf": (p[:, None] < p[None, :]).astype(mybir.dt.np(BF16)),
        "ones_bf": np.ones((P, P), mybir.dt.np(BF16)),
        "power": np.full((P, 32), -0.5, np.float32),
        "root": np.full((P, 32), 0.5, np.float32),
        "cos": table(np.cos(angle), np.cos(angle)),
        "sin": table(-np.sin(angle), np.sin(angle)),
        "mask1": np.where(p[None, :] > p[:, None], np.float32(-1e30), np.float32(0)).astype(mybir.dt.np(BF16)),
        "mask2": np.where(p[:, None] > p[None, :], np.float32(-1e30), np.float32(0)).astype(mybir.dt.np(BF16)),
        "ident_bf": np.eye(P, dtype=np.float32).astype(mybir.dt.np(BF16)),
    }


def scratch(nc, kind="Internal"):
    def d(name, *shape):
        return nc.dram_tensor("s_" + name, shape, F32, kind=kind).ap()

    return {"xn": d("xn", T, D), "xnT": d("xnT", D, T), "xg": d("xg", SLOTS, D), "y": d("y", SLOTS, D),
            "r": d("r", T, D), "cw": d("cw", NCH, E1, CH)}


def lay_out(inp):
    import numpy as np
    a = dict(constants())
    n = {name: np.asarray(v) for name, v in inp.items()}
    c = np.ascontiguousarray

    def rows(v):
        return c(np.broadcast_to(v, (P, v.shape[-1])))

    a["x"] = c(n["L0_attn_x"].reshape(T, D))
    a["gate_w0"] = c(n["L0_ffn_gate_w"])
    a["w_qkv"] = c(n["L0_attn_w_qkv"].T)
    a["w_ug"] = c(n["L0_attn_w_swiglu"].T)
    a["w_out"] = c(n["L0_attn_w_out"].T)
    a["w_su"] = c(n["L0_ffn_Wsu"])
    a["w_sd"] = c(n["L0_ffn_Wsd"])
    a["wu"] = c(n["L0_ffn_Wu"].reshape(E0, KT, P, I0).transpose(2, 0, 1, 3))
    a["wd"] = c(n["L0_ffn_Wd"].transpose(1, 0, 2))
    cat = np.concatenate
    a["w1"] = c(cat([n["L1_ffn_w1"].reshape(-1, D), n["L1_ffn_sw1"]]).T)
    a["w3"] = c(cat([n["L1_ffn_w3"].reshape(-1, D), n["L1_ffn_sw3"]]).T)
    a["w2"] = c(cat([n["L1_ffn_w2"].transpose(0, 2, 1).reshape(-1, D), n["L1_ffn_sw2"].T]))
    a["wq"] = c(n["L1_attn_Wq_w"].T)
    a["wo"] = c(n["L1_attn_Wo_w"].T)
    a["bq"] = rows(n["L1_attn_Wq_b"])
    a["bo"] = rows(n["L1_attn_Wo_b"])
    a["rms_w"] = c(n["L1_attn_rms_w"].reshape(KT, P).T)
    a["gate_w1"] = c(n["L1_ffn_gate_w"].T)
    a["gate_b1"] = rows(n["L1_ffn_gate_b"])
    a["bias0"] = rows(n["L0_ffn_e_bias"])
    return a


def kernel(**inputs):
    import concourse.bacc as bacc
    import numpy as np
    from concourse.bass_utils import run_bass_kernel_spmd

    arrays = lay_out(inputs)
    nc = bacc.Bacc("TRN2", target_bir_lowering=False, num_devices=1)
    io = {name: nc.dram_tensor("in_" + name, v.shape, mybir.dt.from_np(v.dtype), kind="ExternalInput").ap()
          for name, v in arrays.items()}
    out = nc.dram_tensor("out", (T, D), F32, kind="ExternalOutput").ap()
    program(nc, io, scratch(nc), out)
    result = run_bass_kernel_spmd(nc, [{"in_" + name: v for name, v in arrays.items()}], core_ids=[0]).results[0]
    return np.asarray(result["out"]).reshape(T // S1, S1, D)
```

```python
from contextlib import ExitStack

import concourse.bass as bass
from concourse import mybir

F32 = mybir.dt.float32
F32R = mybir.dt.float32r
BF16 = mybir.dt.bfloat16
I32 = mybir.dt.int32
U32 = mybir.dt.uint32
ALU = mybir.AluOpType
ACT = mybir.ActivationFunctionType
AX = mybir.AxisListType.X

P = 128
D = 256
KT = D // P
T = 4096
CH = 512
NCH = T // CH
TP = CH // P
TPR = 2 * TP
CHR = TPR * P
NCR = T // CHR
NT = T // P
E0, TOP0, I0 = 32, 4, 128
G0 = 4
EG = E0 // G0
SCALE0 = 2.5
NB = (T * TOP0 + E0 * (P - 1)) // P + 1
SLOTS = NB * P
UG = 1024
SI = 512
E1, TOP1, I1 = 8, 2, 176
ROWS1 = (E1 + 1) * I1
SLOTS1 = -(-ROWS1 // P)
ROUTED1 = E1 * I1 // P
H1, S1 = 16, 256
DK = D // H1
LN_EPS = 1e-5
RMS_EPS = 1.1920929e-07


class Shared:
    pass


class Chain:

    def __init__(self, eng, sem, per_round, done=None):
        self.eng, self.sem, self.per_round, self.done = eng, sem, per_round, done
        self.base, self.n = 0, 0

    def begin(self, rounds_before):
        self.base, self.n = rounds_before * self.per_round, 0

    def count(self, ins):
        self.n += 1
        ins.then_inc(self.sem, 1)

    def link(self, ins, apart=False):
        self.count(ins)
        self.eng.wait_ge(self.sem, self.base + self.n)
        if apart:
            self.eng.sem_inc(self.done, 1)

    def end(self):
        assert self.n == self.per_round, self.n


def tiles_of(tile, c, n):
    return tile[:, c * n:(c + 1) * n] if isinstance(c, int) else tile[:, bass.ds(c * n, n)]


def route_tokens(nc, k, st):
    sem, sb = k.sem, lambda name, shape, dt=F32: k.sb(st, name, shape, dt)
    E, K = E0, TOP0
    x_t = sb("a_x", [P, 2, TPR, D])
    xn = sb("a_xn", [P, 2, TPR, D])
    xnT = sb("a_xnT", [P, 2, KT, CHR])
    gate_w = sb("a_gate_w", [P, KT, E])
    bias = sb("a_bias", [P, E])
    stats = sb("a_stats", [P, TPR, 6])
    mv = sb("a_mv", [P, TPR, 2])
    var = sb("a_var", [P, 2, TPR])
    rstd = sb("a_rstd", [P, 2, TPR])
    expn = sb("a_expn", [P, 2, TPR * E])
    score = sb("a_score", [P, TPR, E])
    biased = sb("a_biased", [P, TPR, E])
    top8g = sb("a_top8g", [P, TPR * G0, 8])
    gscore = sb("a_gscore", [P, TPR, G0])
    beats = sb("a_beats", [P, TPR, G0, G0])
    gmask = sb("a_gmask", [P, TPR, G0])
    top8 = sb("a_top8", [P, TPR, 8])
    index8 = sb("a_index8", [P, TPR, 8], U32)
    chosen = sb("a_chosen", [P, TPR, K])
    onehot = sb("a_onehot", [P, TPR, K, E])
    picked = sb("a_picked", [P, TPR, K, E])
    weight = sb("a_weight", [P, TPR, K])
    wsum = sb("a_wsum", [P, TPR])
    takes = sb("a_takes", [P, 2, TPR, E], BF16)
    rank = sb("a_rank", [P, TPR, E])
    count = sb("a_count", [P, E])
    blocks = sb("a_blocks", [P, E])
    blocks_i = sb("a_blocks_i", [P, E], I32)
    zeros = k.zeros

    w_in, x_in = sem("a_w_in"), [sem("a_x_in0"), sem("a_x_in1")]
    var_ok, rstd_ok, xn_ok = sem("a_var_ok"), sem("a_rstd_ok"), sem("a_xn_ok")
    turned, xnT_ok, logits_ok, exp_ok = sem("a_turned"), sem("a_xnT_ok"), sem("a_logits_ok"), sem("a_exp_ok")
    takes_ok, ranks_ok = sem("a_takes_ok"), sem("a_ranks_ok")
    xn_out, xnT_out, zeros_ok, zero_out = [sem("a_xn_out0"), sem("a_xn_out1")], [sem("a_xnT_out0"), sem("a_xnT_out1")], sem("a_zeros_ok"), k.zero_out
    dve_own = sem("a_dve_own")

    TURNS = [(f, half) for f in range(KT) for half in range(TPR // 4)]
    logits = [k.ps[4], k.ps[5]]
    ranks = [k.ps[6], k.ps[7]]
    x_v = k.io["x"].rearrange("(c t p) d -> c p t d", p=P, t=TPR)
    xn_v = k.dram["xn"].rearrange("(c t p) d -> c p t d", p=P, t=TPR)
    xnT_v = k.dram["xnT"].rearrange("(f p) (c n) -> c p f n", p=P, n=CHR)

    def steps(eng, front, back):
        front(0, 0, 0)
        with eng.Fori(0, NCR // 2 - 1) as i:
            front(2 * i + 1, i, 1)
            back(2 * i, i, 0)
            front(2 * i + 2, i + 1, 0)
            back(2 * i + 1, i, 1)
        front(NCR - 1, NCR // 2 - 1, 1)
        back(NCR - 2, NCR // 2 - 1, 0)
        back(NCR - 1, NCR // 2 - 1, 1)

    with nc.Block() as block:

        @block.sync
        def _(sp):
            consts = [(k.ident, "ident"), (k.upto, "upto"), (k.ones, "ones"), (k.iota, "iota"),
                      (k.before_bf, "before_bf"), (k.ones_bf, "ones_bf"), (k.power, "power")]
            for u in range(2):
                sp.dma_start(x_t[:, u], x_v[u]).then_inc(x_in[u], 16)
            for tile, name in consts:
                sp.dma_start(tile[:], k.io[name]).then_inc(k.consts_in, 16)
            sp.dma_start(gate_w[:], k.io["gate_w0"].rearrange("(f p) e -> p f e", p=P)).then_inc(w_in, 16)
            sp.dma_start(bias[:], k.io["bias0"]).then_inc(w_in, 16)
            sp.wait_ge(zeros_ok, 1)
            NZ = SLOTS // (4 * P) // NCR
            zv = k.dram["xg"].rearrange("(c z p r) d -> c z p (r d)", p=P, r=4, z=NZ)

            def stores(c, u):
                sp.wait_ge(xn_ok, TPR * c + TPR)
                sp.dma_start(xn_v[c], xn[:, u]).then_inc(xn_out[u], 16)
                sp.wait_ge(xnT_ok, 4 * c + 4)
                sp.dma_start(xnT_v[c], xnT[:, u]).then_inc(xnT_out[u], 16)
                for z in range(NZ):
                    sp.dma_start(zv[c, z], zeros[:]).then_inc(zero_out, 16)

            with sp.Fori(0, NCR // 2 - 1) as i:
                for u in range(2):
                    c = 2 * i + u
                    sp.wait_ge(xn_ok, TPR * c + TPR)
                    sp.dma_start(x_t[:, u], x_v[c + 2]).then_inc(x_in[u], 16)
                    stores(c, u)
            for tile, name in ((k.w_qkv, "w_qkv"), (k.w_ug, "w_ug"), (k.w_out, "w_out"), (k.w_su, "w_su"), (k.w_sd, "w_sd")):
                sp.dma_start(tile if name == "w_ug" else tile[:], k.io[name].rearrange("(f p) n -> p f n", p=P)).then_inc(k.mix_in, 16)
            for u in range(2):
                stores(NCR - 2 + u, u)
            for u in range(2):
                sp.wait_ge(xn_out[u], 16 * NCR // 2)
                sp.wait_ge(xnT_out[u], 16 * NCR // 2)

        @block.gpsimd
        def _(pool):
            nc.gpsimd.memset(zeros[:], 0.0).then_inc(zeros_ok, 1)
            pool.wait_ge(k.consts_in, k.NCONST)
            with pool.Fori(0, NCR // 2) as i:
                for u in range(2):
                    c = 2 * i + u
                    pool.wait_ge(var_ok, c + 1)
                    nc.gpsimd.tensor_tensor(rstd[:, u], var[:, u], k.power[:, 0:TPR], ALU.pow).then_inc(rstd_ok, 1)

        @block.scalar
        def _(act):
            with act.Fori(0, NCR // 2) as i:
                for u in range(2):
                    c = 2 * i + u
                    for n, (f, half) in enumerate(TURNS):
                        act.wait_ge(turned, 4 * c + n + 1)
                        act.wait_ge(xnT_out[u], 16 * i)
                        nc.scalar.activation(xnT[:, u, f, half * 4 * P:(half + 1) * 4 * P], k.ps[n][:], ACT.Copy).then_inc(xnT_ok, 1)
                    act.wait_ge(logits_ok, c + 1)
                    nc.scalar.activation(expn[:, u], logits[u][:, 0:TPR * E], ACT.Exp, scale=-1.0).then_inc(exp_ok, 1)

        @block.tensor
        def _(pe):
            pe.wait_ge(k.consts_in, k.NCONST)
            pe.wait_ge(w_in, 32)

            def front(c, i, u):
                pe.wait_ge(xnT_ok, 4 * c)
                pe.wait_ge(xn_ok, TPR * c + TPR)
                for n, (f, half) in enumerate(TURNS):
                    for t in range(4):
                        m = nc.tensor.transpose(k.ps[n][:, t * P:(t + 1) * P],
                                                xn[:, u, 4 * half + t, f * P:(f + 1) * P], k.ident[:])
                    m.then_inc(turned, 1)
                pe.wait_ge(xnT_ok, 4 * c + 4)
                for t in range(TPR):
                    for f in range(KT):
                        m = nc.tensor.matmul(logits[u][:, t * E:(t + 1) * E], xnT[:, u, f, t * P:(t + 1) * P],
                                             gate_w[:, f], start=(f == 0), stop=(f == KT - 1))
                m.then_inc(logits_ok, 1)

            def back(c, i, u):
                pe.wait_ge(takes_ok, c + 1)
                for t in range(TPR + 1):
                    o = ranks[u][:, t * E:(t + 1) * E]
                    for s in range(min(t + 1, TPR)):
                        m = nc.tensor.matmul(o, (k.before_bf if s == t else k.ones_bf)[:], takes[:, u, s],
                                             start=(s == 0), stop=(s == min(t, TPR - 1)))
                m.then_inc(ranks_ok, 1)

            steps(pe, front, back)

        @block.vector
        def _(dve):
            v = nc.vector
            stand = sem("a_stand")
            own, own_n = Chain(dve, dve_own, k.DVE_A - 2, stand), Chain(dve, sem("a_dve_norm"), 2, stand)
            dve.wait_ge(k.consts_in, k.NCONST)
            dve.wait_ge(w_in, 32)
            with nc.allow_low_precision("0 and 1 are exact in bf16"):
                v.memset(count[:], 0.0)
                v.memset(beats[:], 0.0)

                def front(c, i, u):
                    own_n.begin(c)
                    dve.wait_ge(x_in[u], 16 * i + 16)
                    for t in range(TPR):
                        ins = v.bn_stats(stats[:, t], x_t[:, u, t])
                    own_n.link(ins, apart=True)
                    for t in range(TPR):
                        ins = v.bn_aggr(mv[:, t], stats[:, t])
                    own_n.link(ins)
                    v.tensor_scalar(var[:, u], mv[:, :, 1], LN_EPS, None, ALU.add).then_inc(var_ok, 1)
                    dve.wait_ge(rstd_ok, c + 1)
                    dve.wait_ge(xn_out[u], 16 * i)
                    dve.wait_ge(turned, 4 * c)
                    for t in range(TPR):
                        v.tensor_scalar(xn[:, u, t], x_t[:, u, t], mv[:, t, 0:1], rstd[:, u, t:t + 1],
                                        ALU.subtract, ALU.mult).then_inc(xn_ok, 1)
                    own_n.end()

                def back(c, i, u):
                    own.begin(c)
                    dve.wait_ge(exp_ok, c + 1)
                    own.link(v.tensor_scalar(biased[:].rearrange("p t e -> p (t e)"), expn[:, u], 1.0, None, ALU.add))
                    own.link(v.reciprocal(score[:], biased[:]))
                    own.link(v.tensor_tensor(biased[:], score[:], bias[:].unsqueeze(1).to_broadcast([P, TPR, E]), ALU.add), apart=True)
                    grouped = biased[:].rearrange("p t (g e) -> p (t g) e", e=EG)
                    for g in range(TPR * G0):
                        ins = v.max(top8g[:, g], grouped[:, g])
                    own.link(ins)
                    own.link(v.tensor_tensor(gscore[:].rearrange("p t g -> p (t g)"), top8g[:, :, 0], top8g[:, :, 1], ALU.add))
                    for g in range(G0):
                        for lo, hi, op in ((0, g, ALU.is_ge), (g + 1, G0, ALU.is_gt)):
                            if lo < hi:
                                ins = v.tensor_tensor(beats[:, :, g, lo:hi], gscore[:, :, lo:hi],
                                                      gscore[:, :, g:g + 1].to_broadcast([P, TPR, hi - lo]), op)
                    own.link(ins)
                    own.link(v.tensor_reduce(gmask[:], beats[:], AX, ALU.add))
                    own.link(v.tensor_scalar(gmask[:], gmask[:], 2.0, None, ALU.is_lt))
                    own.link(v.tensor_tensor(biased[:].rearrange("p t (g e) -> p (t g) e", e=EG), grouped,
                                             gmask[:].rearrange("p t g -> p (t g)").unsqueeze(2).to_broadcast([P, TPR * G0, EG]), ALU.mult), apart=True)
                    choose(nc, k, own, c, u, E, K, biased, score, top8, index8, chosen, onehot, picked, weight,
                           takes, takes_ok, ranks_ok, ranks, rank, count)
                    own.link(v.tensor_reduce(wsum[:], weight[:], AX, ALU.add))
                    own.link(v.tensor_scalar(wsum[:], wsum[:], 1e-20, None, ALU.add))
                    own.link(v.reciprocal(wsum[:], wsum[:]))
                    own.link(v.scalar_tensor_tensor(tiles_of(k.weight_of, c, TPR * K).rearrange("p (t k) -> p t k", k=K),
                                                    weight[:], SCALE0, wsum[:].unsqueeze(2).to_broadcast([P, TPR, K]), ALU.mult, ALU.mult))
                    own.end()

                steps(dve, front, back)

                last = Chain(dve, sem("a_dve_last"), 0)
                last.link(v.tensor_scalar(blocks_i[:], count[:], float(P - 1), None, ALU.add))
                last.link(v.tensor_scalar(blocks_i[:], blocks_i[:], 7, None, ALU.arith_shift_right))
                last.link(v.tensor_copy(blocks[:], blocks_i[:]))
                last.link(v.tensor_tensor_scan(k.upto_blocks[:], k.ones[:, 0:E], blocks[:], 0.0, ALU.mult, ALU.add))
                last.link(v.tensor_tensor(k.start[:], k.upto_blocks[:], blocks[:], ALU.subtract))
                last.link(v.tensor_scalar(k.start[:], k.start[:], float(P), None, ALU.mult))


def choose(nc, k, own, c, u, E, K, biased, score, top8, index8, chosen, onehot, picked, weight, takes, takes_ok, ranks_ok, ranks, rank, count):
    v, dve = nc.vector, nc.vector
    for t in range(TPR):
        ins = v.max(top8[:, t], biased[:, t])
    own.link(ins, apart=True)
    for t in range(TPR):
        ins = v.max_index(index8[:, t], top8[:, t], biased[:, t])
    own.link(ins)
    own.link(v.tensor_copy(chosen[:], index8[:, :, 0:K]))
    v.tensor_copy(tiles_of(k.expert_of, c, TPR * K).rearrange("p (t k) -> p t k", k=K), chosen[:])
    own.link(v.tensor_tensor(onehot[:], k.iota[:, 0:E].unsqueeze(1).unsqueeze(1).to_broadcast([P, TPR, K, E]),
                             chosen[:].unsqueeze(3).to_broadcast([P, TPR, K, E]), ALU.is_equal))
    v.tensor_reduce(takes[:, u], onehot[:].rearrange("p t k e -> p t e k"), AX, ALU.add).then_inc(takes_ok, 1)
    own.link(v.tensor_tensor(picked[:], onehot[:], score[:].unsqueeze(2).to_broadcast([P, TPR, K, E]), ALU.mult))
    own.link(v.tensor_reduce(weight[:], picked[:], AX, ALU.add))
    dve.wait_ge(ranks_ok, c + 1)
    own.link(v.tensor_tensor(rank[:], ranks[u][:, 0:TPR * E].rearrange("p (t e) -> p t e", e=E),
                             count[:].unsqueeze(1).to_broadcast([P, TPR, E]), ALU.add))
    own.link(v.tensor_tensor(count[:], count[:], ranks[u][:, TPR * E:TPR * E + E], ALU.add))
    own.link(v.tensor_tensor(picked[:], onehot[:], rank[:].unsqueeze(2).to_broadcast([P, TPR, K, E]), ALU.mult))
    own.link(v.tensor_reduce(tiles_of(k.rank_of, c, TPR * K).rearrange("p (t k) -> p t k", k=K), picked[:], AX, ALU.add))


def mix_tokens(nc, k, st):
    sem, sb = k.sem, lambda name, shape, dt=F32: k.sb(st, name, shape, dt)
    x_t = sb("m_x", [P, 2, TP, D])
    xn = sb("m_xn", [P, 2, TP, D])
    xnT = sb("m_xnT", [P, 2, KT, CH])
    squares = sb("m_squares", [P, TP, D])
    squares_qk = sb("m_squares_qk", [P, 2, D])
    ssx = sb("m_ssx", [P, TP])
    rms = sb("m_rms", [P, 2, TP])
    rms_sq = sb("m_rms_sq", [P, 2, TP])
    rms_pm = sb("m_rms_pm", [P, 2, TP, 2])
    ssqk = sb("m_ssqk", [P, 2])
    qk_mean = sb("m_qk_mean", [P, 2])
    qk_pow = sb("m_qk_pow", [P, 2])
    qk_scale = sb("m_qk_scale", [P, 2])
    eq = sb("m_eq", [P, TP, D])
    wv = sb("m_wv", [P, TP, 2 * D])
    den = sb("m_den", [P, D])
    y = sb("m_y", [P, TP, D])
    yTh, yTl = sb("m_yTh", [P, KT, CH], F32R), sb("m_yTl", [P, KT, CH], F32R)
    gate = sb("m_gate", [P, 2, CH])
    gated = sb("m_gated", [P, 2, CH])
    h = sb("m_h", [P, 3, CH])
    slots = sb("m_slots", [P, 2, TP * TOP0], I32)

    wide = sb("m_wide", [P, 40 * E0])
    start_of = sb("m_start_of", [P, TP * TOP0])
    w_qkv, w_ugh, w_ugl, w_out, w_su, w_sd = k.w_qkv, k.w_ugh, k.w_ugl, k.w_out, k.w_su, k.w_sd

    NS, SW = UG // P + SI // P, UG // P
    x_in, xnT_in = [sem("m_x_in0"), sem("m_x_in1")], [sem("m_xnT_in0"), sem("m_xnT_in1")]
    up_ok, gate_ok, h_ok, down_ok = sem("m_up_ok"), sem("m_gate_ok"), sem("m_h_ok"), sem("m_down_ok")
    xx_ok, res_ok, r_out = sem("m_xx_ok"), sem("m_res_ok"), [sem("m_r_out0"), sem("m_r_out1")]
    ssx_ok, mean_ok, pow_ok, rms_ok = sem("m_ssx_ok"), sem("m_mean_ok"), sem("m_pow_ok"), sem("m_rms_ok")
    prep_mm, prep_read = sem("m_prep_mm"), sem("m_prep_read")
    ss_ok, qkm_ok, qkp_ok, scale_ok = sem("m_ss_ok"), sem("m_qkm_ok"), sem("m_qkp_ok"), sem("m_scale_ok")
    exp_ok, eq1_ok, yT_ok, yTl_ok, ug_ok = sem("m_exp_ok"), sem("m_eq1_ok"), sem("m_yT_ok"), sem("m_yTl_ok"), sem("m_ug_ok")
    dve_s, dve_p = sem("m_dve_s"), sem("m_dve_p")
    slot_of_ok, block_of_ok = sem("m_slot_of_ok"), sem("m_block_of_ok")
    slots_ok, scattered, stand = sem("m_slots_ok"), [sem("m_scattered0"), sem("m_scattered1")], sem("m_stand")

    acc = [k.ps[0], k.ps[1]]
    stream = [[k.ps[2], k.ps[3]], [k.ps[4], k.ps[5]]]
    prep_a, prep_b = k.ps[6], k.ps[7]
    x_v = k.io["x"].rearrange("(c t p) d -> c p t d", p=P, t=TP)
    xn_v = k.dram["xn"].rearrange("(c t p) d -> c p t d", p=P, t=TP)
    r_v = k.dram["r"].rearrange("(c t p) d -> c p t d", p=P, t=TP)
    xnT_v = k.dram["xnT"].rearrange("(f p) (c n) -> c p f n", p=P, n=CH)
    QKV = {2: 0, 3: 1, 6: 2, 7: 3}
    CUM = {4: 0, 5: 1, 8: 2, 9: 3}
    TURN = 11
    ORDER = {2: 0, 3: 1, 4: 2, 5: 3, 6: 4, 7: 5, 8: 6, 9: 7, TURN: 8}

    def chunks(eng, body, prologue):
        prologue()
        with eng.Fori(0, NCH // 2 - 1) as i:
            for u in range(2):
                body(2 * i + u, i, u, True)
        for u in range(2):
            body(NCH - 2 + u, NCH // 2 - 1, u, u == 0)

    with nc.Block() as block:

        @block.sync
        def _(sp):
            def load(c, u):
                sp.dma_start(xnT[:, u], xnT_v[c]).then_inc(xnT_in[u], 16)
                sp.dma_start(xn[:, u], xn_v[c]).then_inc(x_in[u], 16)
                sp.dma_start(x_t[:, u], x_v[c]).then_inc(x_in[u], 16)

            load(0, 0)
            load(1, 1)
            sp.wait_ge(ug_ok, 2)
            for e in range(0, E0, 8):
                sp.dma_start(k.wu[:, e:e + 8], k.io["wu"][:, e:e + 8]).then_inc(k.experts_in, 16)
                sp.dma_start(k.wd[:, e:e + 8], k.io["wd"][:, e:e + 8]).then_inc(k.experts_in, 16)

            def body(c, i, u, more):
                if more:
                    sp.wait_ge(up_ok, NS * c + NS)
                    sp.dma_start(xnT[:, u], xnT_v[c + 2]).then_inc(xnT_in[u], 16)
                    sp.wait_ge(scattered[u], 16 * TP * TOP0 * (i + 1))
                    sp.dma_start(xn[:, u], xn_v[c + 2]).then_inc(x_in[u], 16)
                sp.wait_ge(res_ok, 2 * c + 2)
                sp.dma_start(r_v[c], x_t[:, u]).then_inc(r_out[u], 16)
                if more:
                    sp.wait_ge(r_out[u], 16 * i + 16)
                    sp.dma_start(x_t[:, u], x_v[c + 2]).then_inc(x_in[u], 16)

            with sp.Fori(0, NCH // 2 - 1) as i:
                for u in range(2):
                    body(2 * i + u, i, u, True)
            for u in range(2):
                body(NCH - 2 + u, 0, u, False)
            for u in range(2):
                sp.wait_ge(r_out[u], 16 * NCH // 2)
                sp.wait_ge(scattered[u], 16 * TP * TOP0 * NCH // 2)

        @block.gpsimd
        def _(pool):
            g = nc.gpsimd

            def norm(n, u, i):
                pool.wait_ge(mean_ok, n + 1)
                g.tensor_tensor(rms[:, u], rms[:, u], k.power[:, 0:TP], ALU.pow).then_inc(pow_ok, 1)

            def qkv(n, t, u):
                pool.wait_ge(qkm_ok, TP * n + t + 1)
                g.tensor_tensor(qk_pow[:], qk_mean[:], k.power[:, 0:2], ALU.pow).then_inc(qkp_ok, 1)
                pool.wait_ge(exp_ok, TP * n + t + 1)
                pool.sem_inc(stand, 1)
                g.tensor_scalar(eq[:, t], eq[:, t], 1.0, None, ALU.add).then_inc(eq1_ok, 1)

            def prologue():
                norm(0, 0, 0)
                for t in range(TP):
                    qkv(0, t, 0)
                pool.wait_ge(k.zero_out, k.NZERO)

            def body(c, i, u, more):
                pool.wait_ge(slot_of_ok, c + 1)
                pool.sem_inc(stand, 1)
                g.tensor_copy(slots[:, u], tiles_of(k.slot_of, c, TP * TOP0)).then_inc(slots_ok, 1)
                pool.wait_ge(x_in[u], 32 * i + 32)
                g.tensor_tensor(x_t[:, u], x_t[:, u], xn[:, u], ALU.add).then_inc(xx_ok, 1)
                pool.wait_ge(slots_ok, c + 1)
                pool.sem_inc(stand, 1)
                if more:
                    norm(c + 1, 1 - u, i)
                done = 0
                for s in range(NS):
                    if more and s in QKV:
                        qkv(c + 1, QKV[s], 1 - u)
                        pool.sem_inc(stand, 1)
                    for _ in range(2):
                        if done < TP * TOP0:
                            t, j = divmod(done, TOP0)
                            g.indirect_dma_start(k.dram["xg"], bass.IndirectOffsetOnAxis(ap=slots[:, u, done:done + 1], axis=0),
                                                 xn[:, u, t], None).then_inc(scattered[u], 16)
                            done += 1
                assert done == TP * TOP0

            chunks(pool, body, prologue)

        @block.scalar
        def _(act):
            a = nc.scalar

            def norm(n, u, i, load):
                act.wait_ge(x_in[u], load)
                act.wait_ge(mean_ok, n)
                for t in range(TP):
                    ins = a.activation(squares[:, t], xn[:, u, t], ACT.Square, accum_out=ssx[:, t:t + 1])
                ins.then_inc(ssx_ok, 1)

            def qkv(n, t):
                act.wait_ge(prep_mm, 9 * n + {0: 1, 1: 2, 2: 5, 3: 6}[t])
                act.wait_ge(qkm_ok, TP * n + t)
                a.activation(squares_qk[:, 0], prep_a[:, 0:D], ACT.Square, accum_out=ssqk[:, 0:1])
                a.activation(squares_qk[:, 1], prep_a[:, D:2 * D], ACT.Square, accum_out=ssqk[:, 1:2]).then_inc(ss_ok, 1)
                act.wait_ge(scale_ok, TP * n + t + 1)
                act.wait_ge(prep_read, 8 * n)
                a.activation(eq[:, t], prep_a[:, 0:D], ACT.Exp, scale=qk_scale[:, 0:1])
                a.activation(wv[:, t, D:2 * D], prep_a[:, D:2 * D], ACT.Exp, scale=qk_scale[:, 1:2]).then_inc(exp_ok, 1)

            def turn(n):
                act.wait_ge(prep_mm, 9 * n + 9)
                for f in range(KT):
                    a.activation(yTh[:, f], (prep_a, prep_b)[f][:], ACT.Copy).then_inc(yT_ok, 1)

            def prologue():
                norm(0, 0, 0, 32)
                for t in range(TP):
                    qkv(0, t)
                turn(0)

            def body(c, i, u, more):
                for s in range(NS):
                    act.wait_ge(up_ok, NS * c + s + 1)
                    if s < SW:
                        a.activation(gate[:, s % 2], stream[s % 2][1][:], ACT.Tanh, scale=0.5).then_inc(gate_ok, 1)
                    else:
                        a.activation(gate[:, s % 2], stream[s % 2][0][:], ACT.Relu).then_inc(gate_ok, 1)
                    if more and s == 1:
                        norm(c + 1, 1 - u, i, 32 * (i + 1 + u))
                    if more and s in QKV:
                        qkv(c + 1, QKV[s])
                    if more and s == TURN:
                        turn(c + 1)

            chunks(act, body, prologue)

        @block.tensor
        def _(pe):
            t_ = nc.tensor

            def qkv(n, t, u, j):
                pe.wait_ge(prep_read, 8 * n + j)
                if j == 0:
                    pe.wait_ge(yTl_ok, 2 * n)
                for f in range(KT):
                    t_.matmul(prep_a[:, 0:2 * D], xnT[:, u, f, t * P:(t + 1) * P], w_qkv[:, f, 0:2 * D], start=(f == 0), stop=(f == KT - 1))
                for f in range(KT):
                    m = t_.matmul(prep_b[:, 0:D], xnT[:, u, f, t * P:(t + 1) * P], w_qkv[:, f, 2 * D:3 * D], start=(f == 0), stop=(f == KT - 1))
                m.then_inc(prep_mm, 1)

            def cum(n, t, j):
                pe.wait_ge(prep_read, 8 * n + j)
                m = t_.matmul(prep_a[:], k.upto[:], wv[:, t], start=True, stop=(t % 2 == 0))
                if t % 2:
                    m = t_.matmul(prep_a[:], k.ones[:], wv[:, t - 1], start=False, stop=True)
                m.then_inc(prep_mm, 1)

            def turn(n):
                pe.wait_ge(prep_read, 8 * n + 8)
                for f in range(KT):
                    for t in range(TP):
                        m = t_.transpose((prep_a, prep_b)[f][:, t * P:(t + 1) * P], y[:, t, f * P:(f + 1) * P], k.ident[:])
                m.then_inc(prep_mm, 1)

            def prep(n, u, s):
                if s in QKV:
                    qkv(n, QKV[s], u, ORDER[s])
                if s in CUM:
                    cum(n, CUM[s], ORDER[s])
                if s == TURN:
                    turn(n)

            def prologue():
                pe.wait_ge(k.mix_in, 16 * 5)
                pe.wait_ge(xnT_in[0], 16)
                for s in sorted(ORDER):
                    prep(0, 0, s)
                pe.wait_ge(ug_ok, 2)

            def up(c, u, s):
                pe.wait_ge(h_ok, NS * c + max(s - 1, 0))
                if s == 0:
                    pe.wait_ge(yTl_ok, 2 * c + 2)
                if s < SW:
                    for half in range(2):
                        parts = [(w, y_, f) for w, y_ in ((w_ugh, yTh), (w_ugl, yTh), (w_ugh, yTl)) for f in range(KT)]
                        for n, (w, y_, f) in enumerate(parts):
                            m = t_.matmul(stream[s % 2][half][:], w[:, f, half * UG + s * P:half * UG + (s + 1) * P],
                                          y_[:, f], start=(n == 0), stop=(n == len(parts) - 1))
                else:
                    for f in range(KT):
                        m = t_.matmul(stream[s % 2][0][:], w_su[:, f, (s - SW) * P:(s - SW + 1) * P], xnT[:, u, f],
                                      start=(f == 0), stop=(f == KT - 1))
                m.then_inc(up_ok, 1)

            def down(c, s):
                pe.wait_ge(h_ok, NS * c + s + 1)
                if s == 0:
                    pe.wait_ge(res_ok, 2 * c)
                w = w_out[:, s] if s < SW else w_sd[:, s - SW]
                for t in range(TP):
                    m = t_.matmul(acc[t // 2][:, (t % 2) * D:(t % 2 + 1) * D], h[:, s % 3, t * P:(t + 1) * P], w,
                                  start=(s == 0 and t % 2 == 0), stop=(s == NS - 1), skip_group_check=True)
                m.then_inc(down_ok, 1)

            def body(c, i, u, more):
                up(c, u, 0)
                if more:
                    pe.wait_ge(xnT_in[1 - u], 16 * (i + 1 + u))
                for s in range(1, NS):
                    up(c, u, s)
                    if more:
                        prep(c + 1, 1 - u, s)
                    down(c, s - 1)
                down(c, NS - 1)

            chunks(pe, body, prologue)

        @block.vector
        def _(dve):
            v = nc.vector
            own_s = Chain(dve, dve_s, SW)
            own_p = Chain(dve, dve_p, 1 + 2 * TP)
            own_r = Chain(dve, sem("m_dve_r"), 3)
            own_b = Chain(dve, block_of_ok, 9)

            def slot_of(n):
                own_r.begin(n)
                w = wide[:, 0:TP * TOP0 * E0].rearrange("p (j e) -> p j e", e=E0)
                own_r.link(v.tensor_tensor(w, k.iota[:, 0:E0].unsqueeze(1).to_broadcast([P, TP * TOP0, E0]),
                                           tiles_of(k.expert_of, n, TP * TOP0).unsqueeze(2).to_broadcast([P, TP * TOP0, E0]), ALU.is_equal))
                own_r.link(v.tensor_tensor(w, w, k.start[:].unsqueeze(1).to_broadcast([P, TP * TOP0, E0]), ALU.mult))
                own_r.link(v.tensor_reduce(start_of[:], w, AX, ALU.add))
                v.tensor_tensor(tiles_of(k.slot_of, n, TP * TOP0), start_of[:], tiles_of(k.rank_of, n, TP * TOP0), ALU.add).then_inc(slot_of_ok, 1)
                own_r.end()

            def block_of(part):
                j, step = 40 * part, 40
                w = wide[:].rearrange("p (j e) -> p j e", e=E0)
                own_b.link(v.tensor_tensor(w, k.upto_blocks[:].unsqueeze(1).to_broadcast([P, step, E0]),
                                           k.iota[:, j:j + step].unsqueeze(2).to_broadcast([P, step, E0]), ALU.is_le))
                own_b.link(v.tensor_reduce(k.block_f[:, j:j + step], w, AX, ALU.add))
                if part == NB // step - 1:
                    own_b.link(v.tensor_scalar(k.block_expert[:], k.block_f[:], float(E0 - 1), None, ALU.min))

            def norm(n, u):
                own_p.begin(n)
                dve.wait_ge(ssx_ok, n + 1)
                v.tensor_scalar(rms[:, u], ssx[:], 1.0 / D, RMS_EPS, ALU.mult, ALU.add).then_inc(mean_ok, 1)
                dve.wait_ge(pow_ok, n + 1)
                own_p.link(v.tensor_tensor(rms_sq[:, u], rms[:, u], rms[:, u], ALU.mult))
                v.tensor_scalar(rms_sq[:, u], rms_sq[:, u], 1.0 / D, None, ALU.mult)
                v.tensor_scalar(rms_pm[:, u, :, 0], rms[:, u], -1.0, None, ALU.mult)
                v.tensor_copy(rms_pm[:, u, :, 1], rms[:, u]).then_inc(rms_ok, 1)

            def qkv(n, t, u):
                dve.wait_ge(ss_ok, TP * n + t + 1)
                dve.wait_ge(rms_ok, n + 1)
                v.tensor_scalar(qk_mean[:], ssqk[:], rms_sq[:, u, t:t + 1], RMS_EPS, ALU.mult, ALU.add).then_inc(qkm_ok, 1)
                dve.wait_ge(qkp_ok, TP * n + t + 1)
                v.tensor_tensor(qk_scale[:], qk_pow[:], rms_pm[:, u, t], ALU.mult).then_inc(scale_ok, 1)
                dve.wait_ge(exp_ok, TP * n + t + 1)
                v.scalar_tensor_tensor(wv[:, t, 0:D], prep_b[:, 0:D], rms[:, u, t:t + 1], wv[:, t, D:2 * D],
                                       ALU.mult, ALU.mult).then_inc(prep_read, 1)

            def cum(n, t):
                dve.wait_ge(prep_mm, 9 * n + {0: 3, 1: 4, 2: 7, 3: 8}[t])
                dve.wait_ge(eq1_ok, TP * n + t + 1)
                own_p.link(v.scalar_tensor_tensor(den[:], prep_a[:, D:2 * D], 1e-6, eq[:, t], ALU.add, ALU.mult))
                own_p.link(v.reciprocal(den[:], den[:]))
                if t == 0:
                    dve.wait_ge(yT_ok, 2 * n)
                v.tensor_tensor(y[:, t], prep_a[:, 0:D], den[:], ALU.mult).then_inc(prep_read, 1)

            def turned(n):
                for f in range(KT):
                    dve.wait_ge(yT_ok, 2 * n + f + 1)
                    if f == 0:
                        dve.wait_ge(up_ok, NS * n)
                    v.tensor_tensor(yTl[:, f], (prep_a, prep_b)[f][:], yTh[:, f].bitcast(F32), ALU.subtract).then_inc(yTl_ok, 1)

            def prologue():
                dve.wait_ge(k.mix_in, 16 * 5)
                v.tensor_copy(w_ugh[:], k.w_ug).then_inc(ug_ok, 1)
                dve.wait_ge(ug_ok, 1)
                v.tensor_tensor(w_ugl[:], k.w_ug, w_ugh[:].bitcast(F32), ALU.subtract).then_inc(ug_ok, 1)
                slot_of(0)
                norm(0, 0)
                for s in sorted(ORDER):
                    if s in QKV:
                        qkv(0, QKV[s], 0)
                    if s in CUM:
                        cum(0, CUM[s])
                own_p.end()
                turned(0)

            def body(c, i, u, more):
                own_s.begin(c)
                for s in range(NS):
                    dve.wait_ge(gate_ok, NS * c + s + 1)
                    if s < SW:
                        own_s.link(v.scalar_tensor_tensor(gated[:, s % 2], gate[:, s % 2], 1.0, stream[s % 2][1][:], ALU.add, ALU.mult))
                        dve.wait_ge(down_ok, NS * c + max(s - 2, 0))
                        v.scalar_tensor_tensor(h[:, s % 3], gated[:, s % 2], 0.5, stream[s % 2][0][:], ALU.mult, ALU.mult).then_inc(h_ok, 1)
                    else:
                        dve.wait_ge(down_ok, NS * c + s - 2)
                        v.tensor_tensor(h[:, s % 3], gate[:, s % 2], gate[:, s % 2], ALU.mult).then_inc(h_ok, 1)
                    if more and s == 1:
                        norm(c + 1, 1 - u)
                    if more and s in QKV:
                        qkv(c + 1, QKV[s], 1 - u)
                    if more and s in CUM:
                        cum(c + 1, CUM[s])
                    if more and s == 10:
                        slot_of(c + 1)
                    if more and s == TURN:
                        turned(c + 1)
                    if not more and s % 2 and s < 8:
                        block_of(s // 2)
                own_s.end()
                dve.wait_ge(down_ok, NS * c + NS)
                dve.wait_ge(xx_ok, c + 1)
                for b in range(2):
                    x2 = x_t[:, u, 2 * b:2 * b + 2].rearrange("p t d -> p (t d)")
                    v.tensor_tensor(x2, x2, acc[b][:], ALU.add).then_inc(res_ok, 1)

            chunks(dve, body, prologue)


def expert_blocks(nc, k, st):
    sem, sb = k.sem, lambda name, shape, dt=F32: k.sb(st, name, shape, dt)
    AHEAD, RING = 6, 3
    xg = sb("e_xg", [P, AHEAD, 2, D])
    xgT = sb("e_xgT", [P, 2, 2, KT, P])
    r = sb("e_r", [P, 2, 2, I0])
    actT = sb("e_actT", [P, 2, 2, P])
    ys = sb("e_ys", [P, RING, 2, D])
    x_in = [sem(f"e_x_in{n}") for n in range(AHEAD)]
    y_out = [sem(f"e_y_out{n}") for n in range(RING)]
    turned, xgT_ok, up_ok, r_ok = sem("e_turned"), sem("e_xgT_ok"), sem("e_up_ok"), sem("e_r_ok")
    back, actT_ok, down_ok, y_ok = sem("e_back"), sem("e_actT_ok"), sem("e_down_ok"), sem("e_y_ok")
    xg_v = k.dram["xg"].rearrange("(q b p) d -> q p b d", p=P, b=2)
    y_v = k.dram["y"].rearrange("(q b p) d -> q p b d", p=P, b=2)
    NQ = NB // 2
    STEPS = 6
    FIRST = 3
    LOOPS = (NQ - FIRST - AHEAD) // STEPS

    def steps(eng, step):
        def one(q):
            step(q, q % STEPS, q // STEPS)
        for q in range(FIRST):
            one(q)
        with eng.Fori(0, LOOPS) as i:
            for j in range(FIRST, STEPS + FIRST):
                step(STEPS * i + j, j % STEPS, i + j // STEPS)
        for q in range(LOOPS * STEPS + FIRST, NQ):
            one(q)

    def lap(size, rem, i, n):
        return i * (STEPS // size) + (rem + n) // size

    def wait(eng, s, value):
        if not isinstance(value, int) or value > 0:
            eng.wait_ge(s, value)

    def known(q, n):
        return not isinstance(q, int) or 0 <= q + n < NQ

    with nc.Block() as block:

        @block.sync
        def _(sp):
            def load(q, rem, i, n):
                b = (rem + n) % AHEAD
                sp.dma_start(xg[:, b], xg_v[q + n]).then_inc(x_in[b], 16)

            def step(q, rem, i):
                if known(q, AHEAD):
                    sp.wait_ge(turned, q + 1)
                    load(q, rem, i, AHEAD)
                sp.wait_ge(y_ok, q + 1)
                sp.dma_start(y_v[q], ys[:, rem % RING]).then_inc(y_out[rem % RING], 16)

            for n in range(AHEAD):
                load(0, 0, 0, n)
            steps(sp, step)
            for b in range(RING):
                sp.wait_ge(y_out[b], 16 * len(range(b, NQ, RING)))

        @block.tensor
        def _(pe):
            t_ = nc.tensor

            def turn(q, rem, i, n):
                b, two = (rem + n) % AHEAD, (rem + n) % 2
                pe.wait_ge(x_in[b], 16 * lap(AHEAD, rem, i, n) + 16)
                wait(pe, xgT_ok, q + n - 1)
                for blk in range(2):
                    for f in range(KT):
                        o = (blk * KT + f) * P
                        m = t_.transpose(k.ps[two][:, o:o + P], xg[:, b, blk, f * P:(f + 1) * P], k.ident[:])
                m.then_inc(turned, 1)

            held = {}

            def load_experts(q, rem, n):
                at = 2 * (q + n)
                here = k.block_expert[0:1, bass.ds(at, 4)] if not isinstance(q, int) else k.block_expert[0:1, at:at + 4]
                _, values = nc.values_load_multi_w_load_instructions(
                    here, engines=(mybir.EngineType.PE,), min_val=0, max_val=E0 - 1,
                    skip_runtime_bounds_check_because="block_expert is a minimum with E0 - 1")
                held[(rem + n) % STEPS], held[(rem + n + 1) % STEPS] = values[0:2], values[2:4]

            def expert(rem, n, blk):
                return held[(rem + n) % STEPS][blk]

            def up(q, rem, i, n):
                two = (rem + n) % 2
                pe.wait_ge(xgT_ok, q + n + 1)
                wait(pe, r_ok, q + n - 1)
                for blk in range(2):
                    e = expert(rem, n, blk)
                    for f in range(KT):
                        m = t_.matmul(k.ps[2 + two][:, blk * I0:(blk + 1) * I0], xgT[:, two, blk, f],
                                      k.wu[:, bass.ds(e, 1), f].rearrange("p a i -> p (a i)"), start=(f == 0), stop=(f == KT - 1))
                m.then_inc(up_ok, 1)

            def turn_back(q, rem, i):
                two = rem % 2
                pe.wait_ge(r_ok, q + 1)
                wait(pe, actT_ok, q - 1)
                for blk in range(2):
                    m = t_.transpose(k.ps[4 + two][:, blk * P:(blk + 1) * P], r[:, two, blk], k.ident[:])
                m.then_inc(back, 1)

            def down(q, rem, i, n):
                two = (rem + n) % 2
                pe.wait_ge(actT_ok, q + n + 1)
                wait(pe, y_ok, q + n - 1)
                for blk in range(2):
                    e = expert(rem, n, blk)
                    m = t_.matmul(k.ps[6 + two][:, blk * D:(blk + 1) * D], actT[:, two, blk],
                                  k.wd[:, bass.ds(e, 1)].rearrange("p a d -> p (a d)"), start=True, stop=True)
                m.then_inc(down_ok, 1)

            def step(q, rem, i):
                if rem == FIRST % STEPS and (not isinstance(q, int) or q >= LOOPS * STEPS + FIRST):
                    load_experts(q, rem, -1)
                if known(q, 1) and (q + 1) % 2 == 0 if isinstance(q, int) else (rem + 1) % 2 == 0:
                    load_experts(q, rem, 1)
                if known(q, -1):
                    down(q, rem, i, -1)
                if known(q, 2):
                    turn(q, rem, i, 2)
                turn_back(q, rem, i)
                if known(q, 1):
                    up(q, rem, i, 1)

            pe.wait_ge(k.experts_in, k.NEXPERTS)
            turn(0, 0, 0, 0)
            turn(0, 0, 0, 1)
            load_experts(0, 0, 0)
            up(0, 0, 0, 0)
            steps(pe, step)
            down(NQ - 1, (NQ - 1) % STEPS, (NQ - 1) // STEPS, 0)

        @block.vector
        def _(dve):
            v = nc.vector

            def turned_out(q, rem, i, n):
                two = (rem + n) % 2
                dve.wait_ge(turned, q + n + 1)
                wait(dve, up_ok, q + n - 1)
                v.tensor_copy(xgT[:, two].rearrange("p b f n -> p (b f n)"), k.ps[two][:]).then_inc(xgT_ok, 1)

            def result(q, rem, i, n):
                b, two = (rem + n) % RING, (rem + n) % 2
                dve.wait_ge(down_ok, q + n + 1)
                wait(dve, y_out[b], 16 * lap(RING, rem, i, n))
                v.tensor_copy(ys[:, b].rearrange("p b d -> p (b d)"), k.ps[6 + two][:]).then_inc(y_ok, 1)

            def step(q, rem, i):
                if known(q, -1):
                    result(q, rem, i, -1)
                if known(q, 2):
                    turned_out(q, rem, i, 2)

            turned_out(0, 0, 0, 0)
            turned_out(0, 0, 0, 1)
            steps(dve, step)
            result(NQ - 1, (NQ - 1) % STEPS, (NQ - 1) // STEPS, 0)

        @block.scalar
        def _(act):
            a = nc.scalar

            def relu(q, rem, i, n):
                two = (rem + n) % 2
                act.wait_ge(up_ok, q + n + 1)
                wait(act, back, q + n - 1)
                a.activation(r[:, two].rearrange("p b i -> p (b i)"), k.ps[2 + two][:, 0:2 * I0], ACT.Relu).then_inc(r_ok, 1)

            def square(q, rem, i):
                two = rem % 2
                act.wait_ge(back, q + 1)
                wait(act, down_ok, q - 1)
                a.activation(actT[:, two].rearrange("p b n -> p (b n)"), k.ps[4 + two][:, 0:2 * P], ACT.Square).then_inc(actT_ok, 1)

            def step(q, rem, i):
                square(q, rem, i)
                if known(q, 1):
                    relu(q, rem, i, 1)

            relu(0, 0, 0, 0)
            steps(act, step)


class Banks:

    def __init__(self, sem, tag, plan):
        self.at, self.per_round = {}, [0] * 8
        for name, bank in plan:
            assert name not in self.at, name
            self.at[name] = bank, self.per_round[bank]
            self.per_round[bank] += 1
        self.filled = [sem(f"{tag}_filled{b}") for b in range(8)]
        self.drained = [sem(f"{tag}_drained{b}") for b in range(8)]

    def fill(self, eng, name, c):
        bank, nth = self.at[name]
        eng.wait_ge(self.drained[bank], c * self.per_round[bank] + nth)
        return bank

    def full(self, ins, name):
        ins.then_inc(self.filled[self.at[name][0]], 1)

    def read(self, eng, name, c):
        bank, nth = self.at[name]
        eng.wait_ge(self.filled[bank], c * self.per_round[bank] + nth + 1)
        return bank

    def drain(self, ins, name):
        ins.then_inc(self.drained[self.at[name][0]], 1)

    def passed(self, eng, name, c):
        bank, nth = self.at[name]
        eng.wait_ge(self.drained[bank], c * self.per_round[bank] + nth + 1)

    def rounds(self, eng, name, c):
        bank, _ = self.at[name]
        eng.wait_ge(self.filled[bank], c * self.per_round[bank])


def load_layer1(nc, k, pool):
    g = nc.gpsimd
    n = 0
    for f in range(KT):
        for tile in (k.w1, k.w3):
            g.memset(tile[:, f, ROWS1:SLOTS1 * P].bitcast(F32), 0.0)
    g.memset(k.w2[:, SLOTS1 - 1].bitcast(F32), 0.0).then_inc(k.padded, 1)
    pool.wait_ge(k.padded, 1)
    for f in range(KT):
        for tile, name in ((k.w1, "w1"), (k.w3, "w3")):
            g.dma_start(tile[:, f, 0:ROWS1], k.io[name][f * P:(f + 1) * P]).then_inc(k.layer1_in, 16)
            n += 16
    full = ROWS1 // P
    g.dma_start(k.w2[:, 0:full], k.io["w2"][0:full * P].rearrange("(s p) d -> p s d", p=P)).then_inc(k.layer1_in, 16)
    g.dma_start(k.w2[0:ROWS1 - full * P, full], k.io["w2"][full * P:ROWS1]).then_inc(k.layer1_in, 16)
    assert n + 32 == k.NLAYER1


def layer1(nc, k, st):
    sem, sb = k.sem, lambda name, shape, dt=F32: k.sb(st, name, shape, dt)
    K = TOP0
    yk = sb("l_yk", [P, TP, K, D])
    x1 = sb("l_x1", [P, TP, D])
    xn = sb("l_xn", [P, TP, D])
    res = sb("l_res", [P, TP, D])
    slots = sb("l_slots", [P, TP * K], I32)
    w4 = sb("l_w4", [P, TP * K])
    stats = sb("l_stats", [P, TP, 6])
    mv = sb("l_mv", [P, TP, 2])
    var = sb("l_var", [P, TP])
    rstd = sb("l_rstd", [P, TP])
    ssx = sb("l_ssx", [P, TP])
    ms = sb("l_ms", [P, TP])
    rms = sb("l_rms", [P, TP])
    xh = sb("l_xh", [P, KT, CH], F32R)
    xl = sb("l_xl", [P, KT, CH], F32R)
    wqh, wql = sb("l_wqh", [P, KT, D + E1], F32R), sb("l_wql", [P, KT, D + E1], F32R)
    woh, wol = sb("l_woh", [P, KT, D], F32R), sb("l_wol", [P, KT, D], F32R)
    rms_w = sb("l_rms_w", [P, KT])
    bq, bo = sb("l_bq", [P, D]), sb("l_bo", [P, D])
    gate_w = sb("l_gate_w", [P, KT, E1])
    logits = sb("l_logits", [P, TP, E1])
    gate_b = sb("l_gate_b", [P, E1])
    root = sb("l_root", [P, TP * E1])
    absx, expx, wplus, lnw, zero, dif, score, biased = (sb(f"l_g{n}", [P, TP, E1]) for n in range(8))
    spos = sb("l_spos", [P, TP, E1])
    top8 = sb("l_top8", [P, TP, 8])
    index8 = sb("l_index8", [P, TP, 8], U32)
    chosen = sb("l_chosen", [P, TP, TOP1])
    onehot = sb("l_onehot", [P, TP, E1])
    onehot2 = sb("l_onehot2", [P, TP, E1])
    cw = sb("l_cw", [P, TP, E1])
    cwT = sb("l_cwT", [E1, CH])
    cb = sb("l_cb", [P, ROUTED1, CH])
    v_aug = sb("l_v", [P, TP, H1, DK + 1])
    cos, sin = sb("l_cos", [P, TP, DK]), sb("l_sin", [P, TP, DK])
    qr = sb("l_qr", [P, TP, H1, DK])
    rot = sb("l_rot", [P, TP, H1, DK])
    squares = rot[:].rearrange("p t h d -> p t (h d)")
    qa = sb("l_qa", [P, 2, H1, 64], F32R)
    kb = sb("l_kb", [P, 2, H1, 64], F32R)
    qaT = sb("l_qaT", [P, H1 // 2, S1], F32R)
    kbT = sb("l_kbT", [P, H1 // 2, S1], F32R)
    mx = sb("l_mx", [P, 2, 2, H1 // 2])
    pt0 = sb("l_pt0", [P, 2, 4, S1])
    wq = pt0[:, 0].rearrange("p (f a) n -> p f (a n)", f=KT)[:, :, 0:D]
    wo = pt0[:, 1].rearrange("p (f a) n -> p f (a n)", f=KT)[:, :, 0:D]
    pt1 = sb("l_pt1", [P, 2, 4, P])
    rsum = sb("l_rsum", [P, 2, 2, H1 // 2])
    on = sb("l_on", [P, 2, D])
    oh, ol = sb("l_oh", [P, KT, CH], F32R), sb("l_ol", [P, KT, CH], F32R)
    mask1, mask2, ident_bf = sb("l_mask1", [P, P], BF16), sb("l_mask2", [P, P], BF16), sb("l_ident_bf", [P, P], BF16)
    gate, gated = sb("l_gate", [P, 2, CH]), sb("l_gated", [P, 2, CH])
    hc = sb("l_hc", [P, 2, CH])
    hh, hl = sb("l_hh", [P, 2, CH], F32R), sb("l_hl", [P, 2, CH], F32R)

    SLOT = [ROUTED1 + n for n in range(SLOTS1 - ROUTED1)] + list(range(ROUTED1))
    WORK = [("ffn", 0), ("split", 0), ("ffn", 1)]
    turns = iter(range(2, SLOTS1))
    for b in range(2):
        WORK += [("sides", b), ("ffn", next(turns))]
        if b == 0:
            WORK += [("weights", 0)]
        WORK += [("scores", b, 0), ("scores", b, 1)]
        if b == 1:
            WORK += [("turn_out", 0)]
        WORK += [("ffn", next(turns)), ("scores", b, 2), ("scores", b, 3), ("ffn", next(turns)), ("again", b)]
        WORK += [("ffn", next(turns)), ("probs", b, 0)]
        if b == 0:
            WORK += [("split", 1)]
        WORK += [("probs", b, 1)]
        WORK += [("ffn", next(turns)), ("values", b, 0), ("probs", b, 2), ("probs", b, 3)]
        if b == 0:
            WORK += [("values", b, 1)]
    WORK += [("ffn", next(turns)), ("values", 1, 1), ("turn_in", None), ("ffn", SLOTS1), ("turn_out", 1), ("query", None), ("ffn", SLOTS1 + 1)]
    assert next(turns, None) is None
    assert [w[1] for w in WORK if w[0] == "ffn"] == list(range(SLOTS1 + 2))
    GROUPS = [(g, kind, par, pp) for g in range(2) for kind, par, pp in
              [("two", 0, 0), ("two", 1, 0), ("two", 0, 1), ("two", 1, 1), ("four", 0, None), ("four", 1, None)]]
    SIDES = [(name, n) for n in range(4) for name in ("kb", "qa")]

    plan, turn = [], [0]

    def put(name):
        plan.append((name, 3 + turn[0] % 3))
        turn[0] += 1

    plan += [(f"x{f}", 6 + f) for f in range(KT)] + [(f"q{t}", 6 + t % 2) for t in range(TP)]
    for what, *at in WORK:
        if what == "ffn" and at[0] == 1:
            put("a1")
            put("b1")
        elif what == "ffn" and at[0] < SLOTS1:
            plan += [(f"a{at[0]}", 6), (f"b{at[0]}", 7)]
        if what == "weights":
            put("cw")
        if what == "sides":
            for name, n in SIDES:
                put(f"{name}{at[0]}{n}")
        if what == "scores":
            for n in range(3 * at[1], 3 * at[1] + 3):
                put(f"s{at[0]}{n}")
        if what == "again":
            for n in range(4):
                put(f"qm{at[0]}{n}")
        if what == "probs":
            for n in range(3 * at[1], 3 * at[1] + 3):
                put(f"p{at[0]}{n}")
        if what == "values":
            plan.append((f"o{at[0]}{at[1]}", 2))
        if what == "turn_out":
            put(f"oT{at[0]}")
    plan += [("acc0", 0), ("acc1", 1)]
    banks = Banks(sem, "l", plan)

    consts, NCL = sem("l_consts"), 16 * 13
    r_in, y_in, slots_ok, out_st = sem("l_r_in"), sem("l_y_in"), sem("l_slots_ok"), sem("l_out")
    comb_ok, var_ok, rstd_ok, xn_ok = sem("l_comb_ok"), sem("l_var_ok"), sem("l_rstd_ok"), sem("l_xn_ok")
    ssx_ok, ms_ok, rms_ok, xh_ok = sem("l_ssx_ok"), sem("l_ms_ok"), sem("l_rms_ok"), sem("l_xh_ok")
    abs_ok, exp_ok, wplus_ok, ln_ok = sem("l_abs_ok"), sem("l_exp_ok"), sem("l_wplus_ok"), sem("l_ln_ok")
    sp_ok, score_ok, cw_ok = sem("l_sp_ok"), sem("l_score_ok"), sem("l_cw_ok")
    c_out, cb_in = sem("l_c_out"), [sem(f"l_cb_in{s}") for s in range(ROUTED1)]
    rope_ok, hi_ok, lo_ok, mrow_ok = sem("l_rope_ok"), sem("l_hi_ok"), sem("l_lo_ok"), sem("l_mrow_ok")
    oh_ok = sem("l_oh_ok")
    prep_w, xx_ok = sem("l_prep_w"), sem("l_xx_ok")
    tanh_ok, h_ok, hh_ok, hl_ok, down_ok = sem("l_tanh_ok"), sem("l_h_ok"), sem("l_hh_ok"), sem("l_hl_ok"), sem("l_down_ok")
    dve_own, dve_front, pool_own, dve_once, stand = sem("l_dve"), sem("l_dve_front"), sem("l_pool"), sem("l_dve_once"), sem("l_stand")

    x_v = k.dram["r"].rearrange("(c t p) d -> c p t d", p=P, t=TP)
    out_v = k.out.rearrange("(c t p) d -> c p t d", p=P, t=TP)
    c_v = k.dram["cw"]
    ROWS = []
    for s in range(ROUTED1):
        p = 0
        while p < P:
            e = (s * P + p) // I1
            end = min(P, (e + 1) * I1 - s * P)
            ROWS.append((s, p, end, e))
            p = end

    PARTS = [len([r for r in ROWS if r[0] == s]) for s in range(ROUTED1)]

    with nc.Block() as block:

        @block.sync
        def _(sp):
            for tile, name in ((wq, "wq"), (wo, "wo"), (gate_w, "gate_w1")):
                sp.dma_start(tile if name != "gate_w1" else tile[:], k.io[name].rearrange("(f p) n -> p f n", p=P)).then_inc(consts, 16)
            for tile, name in ((rms_w, "rms_w"), (bq, "bq"), (bo, "bo"), (gate_b, "gate_b1"), (cos, "cos"), (sin, "sin"),
                               (mask1, "mask1"), (mask2, "mask2"), (ident_bf, "ident_bf")):
                sp.dma_start(tile[:], k.io[name]).then_inc(consts, 16)
            sp.dma_start(root[:], k.io["root"]).then_inc(consts, 16)
            sp.dma_start(x1[:], x_v[0]).then_inc(r_in, 16)

            def body(c, more):
                banks.passed(sp, "cw", c)
                sp.dma_start(c_v[c], cwT[:]).then_inc(c_out, 16)
                sp.wait_ge(c_out, 16 * c + 16)
                sp.sem_inc(stand, 1)
                sp.wait_ge(h_ok, SLOTS1 * c)
                sp.sem_inc(stand, 1)
                for s, p, end, e in ROWS:
                    sp.dma_start(cb[p:end, s], c_v[c, e:e + 1].to_broadcast([end - p, CH])).then_inc(cb_in[s], 16)
                if more:
                    sp.wait_ge(xx_ok, c + 1)
                    sp.dma_start(x1[:], x_v[c + 1]).then_inc(r_in, 16)
                for n in range(2):
                    banks.passed(sp, f"acc{n}", c)
                sp.dma_start(out_v[c], res[:]).then_inc(out_st, 16)

            with sp.Fori(0, NCH - 1) as c:
                body(c, True)
            body(NCH - 1, False)
            sp.wait_ge(out_st, 16 * NCH)

        @block.gpsimd
        def _(pool):
            g = nc.gpsimd
            own = Chain(pool, pool_own, 1)

            def slots_of(n):
                at = k.slot_of[:, bass.ds(n * TP * K, TP * K)] if not isinstance(n, int) else k.slot_of[:, n * TP * K:(n + 1) * TP * K]
                if not isinstance(n, int) or n:
                    pool.wait_ge(comb_ok, n)
                    pool.sem_inc(stand, 1)
                g.tensor_copy(slots[:], at).then_inc(slots_ok, 1)
                pool.wait_ge(slots_ok, n + 1)
                pool.sem_inc(stand, 1)

            def gather(numbers):
                for n in numbers:
                    g.indirect_dma_start(yk[:, n // K, n % K], None, k.dram["y"],
                                         bass.IndirectOffsetOnAxis(ap=slots[:, n:n + 1], axis=0)).then_inc(y_in, 16)

            def std(n):
                pool.wait_ge(var_ok, n + 1)
                g.tensor_tensor(rstd[:], var[:], k.power[:, 0:TP], ALU.pow).then_inc(rstd_ok, 1)

            def rms_of(n):
                pool.wait_ge(ms_ok, n + 1)
                g.tensor_tensor(rms[:], ms[:], k.power[:, 0:TP], ALU.pow).then_inc(rms_ok, 1)

            def body(c, more):
                own.begin(c)
                pool.wait_ge(sp_ok, c + 1)
                g.tensor_tensor(score[:].rearrange("p t e -> p (t e)"), spos[:].rearrange("p t e -> p (t e)"),
                                root[:], ALU.pow).then_inc(score_ok, 1)
                pool.wait_ge(out_st, 16 * c)
                own.link(g.tensor_tensor(res[:], x1[:], xn[:], ALU.add))
                g.tensor_tensor(res[:], res[:], bo[:].unsqueeze(1).to_broadcast([P, TP, D]), ALU.add).then_inc(xx_ok, 1)
                own.end()
                for n in range(1, SLOTS1 + 1):
                    if more and n == 2:
                        slots_of(c + 1)
                    if more and 3 <= n < 11:
                        gather(range(2 * n - 6, 2 * n - 4))
                    s = n - 1
                    pool.wait_ge(hh_ok, SLOTS1 * c + s + 1)
                    pool.wait_ge(down_ok, (SLOTS1 - 1) * c + max(s - 1, 0))
                    g.tensor_tensor(hl[:, s % 2], hc[:, s % 2], hh[:, s % 2].bitcast(F32), ALU.subtract).then_inc(hl_ok, 1)
                    if more and n == SLOTS1 - 1:
                        std(c + 1)
                        rms_of(c + 1)

            slots_of(0)
            gather(range(TP * K))
            load_layer1(nc, k, pool)
            std(0)
            rms_of(0)
            with pool.Fori(0, NCH - 1) as c:
                body(c, True)
            body(NCH - 1, False)

        @block.scalar
        def _(act):
            a = nc.scalar
            act.wait_ge(consts, NCL)

            def squared(n):
                act.wait_ge(xn_ok, TP * n + TP)
                if not isinstance(n, int) or n:
                    act.wait_ge(ms_ok, n)
                for t in range(TP):
                    ins = a.activation(squares[:, t], xn[:, t], ACT.Square, accum_out=ssx[:, t:t + 1])
                ins.then_inc(ssx_ok, 1)

            def ffn(c, n):
                if 1 <= n <= SLOTS1:
                    s = n - 1
                    act.wait_ge(h_ok, SLOTS1 * c + s + 1)
                    act.wait_ge(down_ok, (SLOTS1 - 1) * c + max(s - 1, 0))
                    a.activation(hh[:, s % 2], hc[:, s % 2], ACT.Copy).then_inc(hh_ok, 1)
                if n < SLOTS1:
                    bank = banks.read(act, f"a{n}", c)
                    a.activation(gate[:, n % 2], k.ps[bank][:], ACT.Tanh, scale=0.5).then_inc(tanh_ok, 1)

            def split(c, b):
                act.wait_ge(rope_ok, c + 1)
                if b:
                    for n in range(1, 4):
                        banks.read(act, f"qm{b - 1}{n}", c)
                src = qr[:, 2 * b:2 * b + 2].rearrange("p t h d -> p (t h) d")
                kbv = kb[:].rearrange("p t h d -> p (t h) d")
                qav = qa[:].rearrange("p t h d -> p (t h) d")
                for dst, lo in ((kbv, 0), (kbv, DK), (qav, 0), (qav, 2 * DK)):
                    a.activation(dst[:, :, lo:lo + DK], src, ACT.Copy).then_inc(hi_ok, 1)

            def turned(c, name, tile, n):
                bank = banks.read(act, name, c)
                banks.drain(a.activation(tile[:, 2 * n:2 * n + 2].rearrange("p a n -> p (a n)"), k.ps[bank][:], ACT.Copy), name)

            def turn_in(n):
                for f in range(KT):
                    bank = banks.read(act, f"x{f}", n)
                    a.activation(xh[:, f], k.ps[bank][:], ACT.Copy).then_inc(xh_ok, 1)

            def query(n):
                act.wait_ge(abs_ok, n + 1)
                a.activation(expx[:], absx[:], ACT.Exp, scale=-1.0).then_inc(exp_ok, 1)
                act.wait_ge(wplus_ok, n + 1)
                a.activation(lnw[:], wplus[:], ACT.Ln).then_inc(ln_ok, 1)

            def body(c, more):
                for what, *at in WORK:
                    b = at[0]
                    if what == "ffn":
                        ffn(c, at[0])
                        if more and at[0] == SLOTS1 - 1:
                            squared(c + 1)
                    if more and what == "turn_in":
                        turn_in(c + 1)
                    if more and what == "query":
                        query(c + 1)
                    if what == "weights":
                        bank = banks.read(act, "cw", c)
                        act.wait_ge(c_out, 16 * c)
                        banks.drain(a.activation(cwT[:], k.ps[bank][0:E1, :], ACT.Copy), "cw")
                    if what == "split":
                        split(c, b)
                    if what == "sides":
                        for n in range(4):
                            turned(c, f"kb{b}{n}", kbT, n)
                    if what == "again":
                        for n in (1, 3):
                            turned(c, f"qm{b}{n}", qaT, n)
                    if what == "probs":
                        for n in range(3 * at[1], 3 * at[1] + 3):
                            g, kind, par, pp = GROUPS[n]
                            bank = banks.read(act, f"p{b}{n}", c)
                            if n == 6:
                                banks.read(act, f"o{b}0", c)
                            dst = pt0[:, par, 2 * pp:2 * pp + 2] if kind == "two" else pt1[:, par]
                            banks.drain(a.activation(dst.rearrange("p a n -> p (a n)"), k.ps[bank][:], ACT.Exp, scale=DK ** -0.5), f"p{b}{n}")
                    if what == "turn_out":
                        bank = banks.read(act, f"oT{b}", c)
                        a.activation(oh[:, :, b * S1:(b + 1) * S1], k.ps[bank][:].rearrange("p (f n) -> p f n", f=KT), ACT.Copy).then_inc(oh_ok, 1)

            squared(0)
            turn_in(0)
            query(0)
            with act.Fori(0, NCH - 1) as c:
                body(c, True)
            body(NCH - 1, False)

        @block.tensor
        def _(pe):
            t_ = nc.tensor
            pe.wait_ge(consts, NCL)
            pe.wait_ge(prep_w, 4)

            def three(out, left, right, start, stop, **kw):
                parts = [(l, r, f) for l, r in ((0, 0), (1, 0), (0, 1)) for f in range(KT)]
                for n, (l, r, f) in enumerate(parts):
                    m = t_.matmul(out, left(l, f), right(r, f), start=(start and n == 0), stop=(stop and n == len(parts) - 1), **kw)
                return m

            def side(c, name, tile, n):
                bank = banks.fill(pe, name, c)
                for a in range(2):
                    for t in range(2):
                        o, pair = (a * 2 + t) * P, 2 * n + a
                        m = t_.transpose(k.ps[bank][:, o:o + P], tile[:, t].bitcast(F32).rearrange("p h d -> p (h d)")[:, pair * P:(pair + 1) * P], k.ident[:])
                banks.full(m, name)

            def score_bank(c, name, n, first, rows_used, left, right, mask):
                g, kind, par, pp = GROUPS[n]
                bank = banks.fill(pe, name, c)
                rows = slice(64 * par, 64 * par + rows_used)
                heads = range(4 * g, 4 * g + 4) if kind == "four" else range(4 * g + 2 * pp, 4 * g + 2 * pp + 2)
                for a, pair in enumerate(heads):
                    if kind == "two":
                        o, l, r = slice(a * S1, (a + 1) * S1), slice(first * P, (first + 1) * P), slice(0, S1)
                    else:
                        o = slice(a * P, (a + 1) * P)
                        l = r = slice((1 - first) * P, (2 - first) * P)
                    t_.matmul(k.ps[bank][:, o], left[rows, pair, l], right[rows, pair, r], start=(a == 0), stop=False, skip_group_check=True)
                masked = k.ps[bank][:].rearrange("p (a n) -> p a n", a=len(heads))
                if kind == "two":
                    masked = masked[:, :, first * P:(first + 1) * P]
                m = t_.matmul(masked, ident_bf[:], mask[:].unsqueeze(1).to_broadcast([P, len(heads), P]),
                              start=False, stop=True, skip_group_check=True)
                banks.full(m, name)

            def values(c, b, g):
                for n in range(6 * g + 3, 6 * g + 6):
                    banks.passed(pe, f"p{b}{n}", c)
                bank = banks.fill(pe, f"o{b}{g}", c)
                for a in range(4):
                    for par in range(2):
                        head = 2 * (4 * g + a) + par
                        o = [slice((t * 8 + 2 * a + par) * (DK + 1), (t * 8 + 2 * a + par + 1) * (DK + 1)) for t in range(2)]
                        v0, v1 = v_aug[:, 2 * b, head], v_aug[:, 2 * b + 1, head]
                        t_.matmul(k.ps[bank][:, o[0]], pt0[:, par, a, 0:P], v0, start=True, stop=True)
                        t_.matmul(k.ps[bank][:, o[1]], pt0[:, par, a, P:S1], v0, start=True, stop=False)
                        m = t_.matmul(k.ps[bank][:, o[1]], pt1[:, par, a], v1, start=False, stop=True)
                banks.full(m, f"o{b}{g}")

            def up(c, n):
                s = SLOT[n]
                for name, w in (("a", k.w1), ("b", k.w3)):
                    bank = banks.fill(pe, f"{name}{n}", c)
                    parts = [(x, f) for x in (xh, xl) for f in range(KT)]
                    for i, (x, f) in enumerate(parts):
                        m = t_.matmul(k.ps[bank][:], w[:, f, s * P:(s + 1) * P], x[:, f], start=(i == 0), stop=(i == len(parts) - 1))
                    banks.full(m, f"{name}{n}")

            def down(c, n):
                if n == 0:
                    for i in range(2):
                        banks.fill(pe, f"acc{i}", c)
                pe.wait_ge(hh_ok, SLOTS1 * c + n + 1)
                pe.wait_ge(hl_ok, SLOTS1 * c + n + 1)
                for i, x in enumerate((hh, hl)):
                    for t in range(TP):
                        m = t_.matmul(k.ps[t // 2][:, (t % 2) * D:(t % 2 + 1) * D], x[:, n % 2, t * P:(t + 1) * P], k.w2[:, SLOT[n]],
                                      start=(n == 0 and i == 0 and t % 2 == 0), stop=False, skip_group_check=True)
                if n < SLOTS1 - 1:
                    m.then_inc(down_ok, 1)

            def turn_in(n):
                pe.wait_ge(xn_ok, TP * n + TP)
                for f in range(KT):
                    bank = banks.fill(pe, f"x{f}", n)
                    for t in range(TP):
                        m = t_.transpose(k.ps[bank][:, t * P:(t + 1) * P], xn[:, t, f * P:(f + 1) * P], k.ident[:])
                    banks.full(m, f"x{f}")

            def query(n):
                for f in range(KT):
                    banks.passed(pe, f"x{f}", n)
                for t in range(TP):
                    bank = banks.fill(pe, f"q{t}", n)
                    m = three(k.ps[bank][:, 0:D + E1], lambda l, f: (xh, xl)[l][:, f, t * P:(t + 1) * P],
                              lambda r, f: (wqh, wql)[r][:, f], True, True)
                    banks.full(m, f"q{t}")

            def body(c, more):
                for what, *at in WORK:
                    b = at[0]
                    if what == "ffn":
                        n = at[0]
                        if n < SLOTS1:
                            up(c, n)
                        if n >= 2:
                            down(c, n - 2)
                    if more and what == "turn_in":
                        turn_in(c + 1)
                    if more and what == "query":
                        query(c + 1)
                    if what == "weights":
                        bank = banks.fill(pe, "cw", c)
                        pe.wait_ge(cw_ok, c + 1)
                        for t in range(TP):
                            m = t_.transpose(k.ps[bank][0:E1, t * P:(t + 1) * P], cw[:, t], k.ident[:])
                        banks.full(m, "cw")
                    if what == "sides":
                        pe.wait_ge(hi_ok, 4 * (2 * c + b) + 4)
                        pe.wait_ge(lo_ok, 2 * (2 * c + b) + 2)
                        for name, n in SIDES:
                            side(c, f"{name}{b}{n}", {"kb": kb, "qa": qa}[name], n)
                    if what == "scores":
                        if at[1] == 0:
                            for name, n in SIDES[-3:]:
                                banks.passed(pe, f"{name}{b}{n}", c)
                        for n in range(3 * at[1], 3 * at[1] + 3):
                            score_bank(c, f"s{b}{n}", n, 1, 3 * DK, qaT, kbT, mask1)
                    if what == "again":
                        pe.wait_ge(mrow_ok, 2 * c + b + 1)
                        for n in range(4):
                            side(c, f"qm{b}{n}", qa, n)
                    if what == "probs":
                        if at[1] == 0:
                            for n in range(1, 4):
                                banks.passed(pe, f"qm{b}{n}", c)
                        for n in range(3 * at[1], 3 * at[1] + 3):
                            score_bank(c, f"p{b}{n}", n, 0, 3 * DK + 2, kbT, qaT, mask2)
                    if what == "values":
                        values(c, b, at[1])
                    if what == "turn_out":
                        bank = banks.fill(pe, f"oT{b}", c)
                        banks.passed(pe, f"o{b}1", c)
                        for f in range(KT):
                            for t in range(2):
                                m = t_.transpose(k.ps[bank][:, (f * 2 + t) * P:(f * 2 + t + 1) * P], on[:, t, f * P:(f + 1) * P], k.ident[:])
                        banks.full(m, f"oT{b}")
                for b in range(2):
                    banks.passed(pe, f"oT{b}", c)
                for t in range(TP):
                    m = three(k.ps[t // 2][:, (t % 2) * D:(t % 2 + 1) * D], lambda l, f: (oh, ol)[l][:, f, t * P:(t + 1) * P],
                              lambda r, f: (woh, wol)[r][:, f], False, True, skip_group_check=True)
                    if t % 2:
                        banks.full(m, f"acc{t // 2}")

            turn_in(0)
            query(0)
            pe.wait_ge(k.layer1_in, k.NLAYER1)
            with pe.Fori(0, NCH - 1) as c:
                body(c, True)
            body(NCH - 1, False)

        @block.vector
        def _(dve):
            v = nc.vector
            own, own_f = Chain(dve, dve_own, k.DVE_L, stand), Chain(dve, dve_front, 16, stand)
            once = Chain(dve, dve_once, 0)
            dve.wait_ge(consts, NCL)
            v.memset(qa[:].bitcast(U32), 0)
            v.memset(v_aug[:], 1.0)
            once.link(v.memset(kb[:].bitcast(U32), 0))
            v.tensor_copy(kb[:, :, :, 3 * DK:3 * DK + 2], k.ones[:, 0:2 * H1 * 2].rearrange("p (t h a) -> p t h a", t=2, a=2))
            for f in range(KT):
                ins = v.tensor_scalar(wq[:, f], wq[:, f], rms_w[:, f:f + 1], None, ALU.mult)
            once.link(ins)
            v.tensor_copy(wqh[:, :, D:], gate_w[:])
            v.tensor_copy(wqh[:, :, 0:D], wq).then_inc(prep_w, 1)
            once.link(v.tensor_copy(woh[:], wo))
            dve.wait_ge(prep_w, 1)
            v.tensor_tensor(wql[:, :, D:], gate_w[:], wqh[:, :, D:].bitcast(F32), ALU.subtract)
            v.tensor_tensor(wql[:, :, 0:D], wq, wqh[:, :, 0:D].bitcast(F32), ALU.subtract).then_inc(prep_w, 1)
            v.tensor_tensor(wol[:], wo, woh[:].bitcast(F32), ALU.subtract).then_inc(prep_w, 2)

            def combine(n, first):
                if first:
                    own_f.begin(n)
                    at = k.weight_of[:, bass.ds(n * TP * K, TP * K)] if not isinstance(n, int) else k.weight_of[:, n * TP * K:(n + 1) * TP * K]
                    own_f.link(v.tensor_copy(w4[:], at))
                    dve.wait_ge(r_in, 16 * n + 16)
                    dve.wait_ge(y_in, 16 * TP * K * (n + 1))
                for j in (0, 1) if first else (2, 3):
                    for t in range(TP):
                        i = t * K + j
                        ins = v.scalar_tensor_tensor(x1[:, t], yk[:, t, j], w4[:, i:i + 1], x1[:, t], ALU.mult, ALU.add)
                    own_f.link(ins)
                if first:
                    return
                dve.sem_inc(comb_ok, 1)
                for t in range(TP):
                    ins = v.bn_stats(stats[:, t], x1[:, t])
                own_f.link(ins, apart=True)
                for t in range(TP):
                    ins = v.bn_aggr(mv[:, t], stats[:, t])
                own_f.link(ins)
                v.tensor_scalar(var[:], mv[:, :, 1], LN_EPS, None, ALU.add).then_inc(var_ok, 1)

            def normed(n):
                dve.wait_ge(rstd_ok, n + 1)
                for t in range(TP):
                    v.tensor_scalar(xn[:, t], x1[:, t], mv[:, t, 0:1], rstd[:, t:t + 1], ALU.subtract, ALU.mult).then_inc(xn_ok, 1)

            def mean_square(n):
                dve.wait_ge(ssx_ok, n + 1)
                v.tensor_scalar(ms[:], ssx[:], 1.0 / D, RMS_EPS, ALU.mult, ALU.add).then_inc(ms_ok, 1)

            def choose_two(c):
                dve.wait_ge(score_ok, c + 1)
                own.link(v.tensor_tensor(biased[:], score[:], gate_b[:].unsqueeze(1).to_broadcast([P, TP, E1]), ALU.add), apart=True)
                for t in range(TP):
                    ins = v.max(top8[:, t], biased[:, t])
                own.link(ins, apart=True)
                for t in range(TP):
                    ins = v.max_index(index8[:, t], top8[:, t], biased[:, t])
                own.link(ins)
                own.link(v.tensor_copy(chosen[:], index8[:, :, 0:TOP1]))
                experts = k.iota[:, 0:E1].unsqueeze(1).to_broadcast([P, TP, E1])
                v.tensor_tensor(onehot[:], experts, chosen[:, :, 0:1].to_broadcast([P, TP, E1]), ALU.is_equal)
                own.link(v.tensor_tensor(onehot2[:], experts, chosen[:, :, 1:2].to_broadcast([P, TP, E1]), ALU.is_equal))
                own.link(v.tensor_tensor(onehot[:], onehot[:], onehot2[:], ALU.add))
                v.tensor_tensor(cw[:], onehot[:], score[:], ALU.mult).then_inc(cw_ok, 1)

            def softplus(c):
                dve.wait_ge(wplus_ok, c + 1)
                own_f.link(v.tensor_scalar(dif[:], wplus[:], -1.0, None, ALU.add))
                own_f.link(v.tensor_scalar(zero[:], dif[:], 0.0, None, ALU.is_equal))
                own_f.link(v.tensor_tensor(dif[:], dif[:], zero[:], ALU.add))
                own_f.link(v.reciprocal(dif[:], dif[:]))
                dve.wait_ge(ln_ok, c + 1)
                own_f.link(v.tensor_tensor(lnw[:], lnw[:], zero[:], ALU.add))
                own_f.link(v.tensor_tensor(lnw[:], lnw[:], expx[:], ALU.mult))
                own_f.link(v.tensor_tensor(lnw[:], lnw[:], dif[:], ALU.mult))
                v.tensor_tensor(spos[:], spos[:], lnw[:], ALU.add).then_inc(sp_ok, 1)

            def rope():
                vq, half = v_aug[:, :, :, 0:DK], DK // 2
                v.tensor_tensor(qr[:], vq, cos[:].unsqueeze(2).to_broadcast([P, TP, H1, DK]), ALU.mult)
                v.tensor_tensor(rot[:, :, :, 0:half], vq[:, :, :, half:DK], sin[:, :, 0:half].unsqueeze(2).to_broadcast([P, TP, H1, half]), ALU.mult)
                own_f.link(v.tensor_tensor(rot[:, :, :, half:DK], vq[:, :, :, 0:half], sin[:, :, half:DK].unsqueeze(2).to_broadcast([P, TP, H1, half]), ALU.mult))
                v.tensor_tensor(qr[:], qr[:], rot[:], ALU.add).then_inc(rope_ok, 1)

            def ffn(c, n):
                if 1 <= n <= SLOTS1:
                    weighted(c, n - 1)
                if n < SLOTS1:
                    dve.wait_ge(tanh_ok, SLOTS1 * c + n + 1)
                    bank = banks.read(dve, f"a{n}", c)
                    banks.drain(v.scalar_tensor_tensor(gated[:, n % 2], gate[:, n % 2], 1.0, k.ps[bank][:], ALU.add, ALU.mult), f"a{n}")
                    banks.passed(dve, f"a{n}", c)
                    dve.wait_ge(hh_ok, SLOTS1 * c + max(n - 1, 0))
                    dve.wait_ge(hl_ok, SLOTS1 * c + max(n - 1, 0))
                    bank = banks.read(dve, f"b{n}", c)
                    banks.drain(v.scalar_tensor_tensor(hc[:, n % 2], gated[:, n % 2], 0.5, k.ps[bank][:], ALU.mult, ALU.mult), f"b{n}")

            def weighted(c, n):
                banks.passed(dve, f"b{n}", c)
                if SLOT[n] < ROUTED1:
                    dve.wait_ge(cb_in[SLOT[n]], 16 * PARTS[SLOT[n]] * (c + 1))
                    v.tensor_tensor(hc[:, n % 2], hc[:, n % 2], cb[:, SLOT[n]], ALU.mult).then_inc(h_ok, 1)
                else:
                    dve.sem_inc(h_ok, 1)

            def turned(c, name, n):
                bank = banks.read(dve, name, c)
                banks.drain(v.tensor_copy(qaT[:, 2 * n:2 * n + 2].rearrange("p a n -> p (a n)"), k.ps[bank][:]), name)

            def max_rows(c, b):
                for n in (9, 10, 11):
                    banks.passed(dve, f"s{b}{n}", c)
                own.link(v.tensor_scalar(mx[:], mx[:], -1.0, None, ALU.mult))
                top = qa[:].rearrange("p t (q r) d -> p t r q d", r=2)
                for t in range(2):
                    ins = v.tensor_copy(top[:, t, :, :, 3 * DK], mx[:, t])
                own.link(ins)
                for t in range(2):
                    ins = v.tensor_tensor(top[:, t, :, :, 3 * DK + 1], mx[:, t], top[:, t, :, :, 3 * DK].bitcast(F32), ALU.subtract)
                ins.then_inc(mrow_ok, 1)

            def turn_in(n):
                for f in range(KT):
                    bank = banks.read(dve, f"x{f}", n)
                    dve.wait_ge(xh_ok, KT * n + f + 1)
                    banks.drain(v.tensor_tensor(xl[:, f], k.ps[bank][:], xh[:, f].bitcast(F32), ALU.subtract), f"x{f}")

            def query(n):
                dve.wait_ge(rms_ok, n + 1)
                for t in range(TP):
                    bank = banks.read(dve, f"q{t}", n)
                    v.tensor_copy(logits[:, t], k.ps[bank][:, D:D + E1])
                    banks.drain(v.scalar_tensor_tensor(v_aug[:, t, :, 0:DK], k.ps[bank][:, 0:D].rearrange("p (h d) -> p h d", h=H1), rms[:, t:t + 1],
                                                       bq[:].rearrange("p (h d) -> p h d", h=H1), ALU.mult, ALU.add), f"q{t}")
                for t in (TP - 2, TP - 1):
                    banks.passed(dve, f"q{t}", n)
                own_f.link(v.tensor_scalar(spos[:], logits[:], 0.0, None, ALU.max))
                v.scalar_tensor_tensor(absx[:], spos[:], 2.0, logits[:], ALU.mult, ALU.subtract).then_inc(abs_ok, 1)
                dve.wait_ge(exp_ok, n + 1)
                v.tensor_scalar(wplus[:], expx[:], 1.0, None, ALU.add).then_inc(wplus_ok, 1)
                rope()
                softplus(n)
                own_f.end()

            def body(c, more):
                own.begin(c)
                for what, *at in WORK:
                    b = at[0]
                    if what == "ffn":
                        ffn(c, at[0])
                        if more and at[0] in (SLOTS1 - 3, SLOTS1 - 2):
                            combine(c + 1, at[0] == SLOTS1 - 3)
                        if more and at[0] == SLOTS1 - 1:
                            normed(c + 1)
                            mean_square(c + 1)
                    if more and what == "turn_in":
                        turn_in(c + 1)
                    if more and what == "query":
                        query(c + 1)
                    if what == "split":
                        dve.wait_ge(hi_ok, 4 * (2 * c + b) + 1)
                        q2 = qr[:, 2 * b:2 * b + 2].rearrange("p t h d -> p (t h) d")
                        kbv, qav = kb[:].rearrange("p t h d -> p (t h) d"), qa[:].rearrange("p t h d -> p (t h) d")
                        hi = kbv[:, :, 0:DK].bitcast(F32)
                        v.tensor_tensor(kbv[:, :, 2 * DK:3 * DK], q2, hi, ALU.subtract).then_inc(lo_ok, 1)
                        v.tensor_tensor(qav[:, :, DK:2 * DK], q2, hi, ALU.subtract).then_inc(lo_ok, 1)
                    if what == "sides":
                        for n in range(4):
                            turned(c, f"qa{b}{n}", n)
                        if b == 0:
                            choose_two(c)
                    if what == "scores":
                        for n in range(3 * at[1], 3 * at[1] + 3):
                            g, kind, par, pp = GROUPS[n]
                            bank = banks.read(dve, f"s{b}{n}", c)
                            if kind == "two":
                                o, a = mx[:, 1, par, 4 * g + 2 * pp:4 * g + 2 * pp + 2], 2
                            else:
                                o, a = mx[:, 0, par, 4 * g:4 * g + 4], 4
                            banks.drain(v.tensor_reduce(o, k.ps[bank][:].rearrange("p (a n) -> p a n", a=a), AX, ALU.max), f"s{b}{n}")
                        if at[1] == 3:
                            max_rows(c, b)
                    if what == "again":
                        for n in (0, 2):
                            turned(c, f"qm{b}{n}", n)
                    if what == "values":
                        g = at[1]
                        bank = banks.read(dve, f"o{b}{g}", c)
                        o = k.ps[bank][:, 0:H1 * (DK + 1)].rearrange("p (t h d) -> p t h d", t=2, h=H1 // 2)
                        own.link(v.reciprocal(rsum[:, g], o[:, :, :, DK]))
                        banks.drain(v.tensor_tensor(on[:, :, g * P:(g + 1) * P].rearrange("p t (h d) -> p t h d", h=H1 // 2), o[:, :, :, 0:DK],
                                                    rsum[:, g].unsqueeze(3).to_broadcast([P, 2, H1 // 2, DK]), ALU.mult), f"o{b}{g}")
                    if what == "turn_out":
                        bank = banks.read(dve, f"oT{b}", c)
                        dve.wait_ge(oh_ok, 2 * c + b + 1)
                        part = slice(b * S1, (b + 1) * S1)
                        banks.drain(v.tensor_tensor(ol[:, :, part], k.ps[bank][:].rearrange("p (f n) -> p f n", f=KT), oh[:, :, part].bitcast(F32), ALU.subtract), f"oT{b}")
                dve.wait_ge(xx_ok, c + 1)
                for n in range(2):
                    x2 = res[:, 2 * n:2 * n + 2].rearrange("p t d -> p (t d)")
                    banks.read(dve, f"acc{n}", c)
                    banks.drain(v.tensor_tensor(x2, x2, k.ps[n][:], ALU.add), f"acc{n}")
                own.end()

            combine(0, True)
            combine(0, False)
            normed(0)
            mean_square(0)
            turn_in(0)
            query(0)
            with dve.Fori(0, NCH - 1) as c:
                body(c, True)
            body(NCH - 1, False)


def program(nc, io, dram, out):
    with ExitStack() as top:
        def sem(name):
            return top.enter_context(nc.semaphore(name))

        def sb(stack, name, shape, dt=F32):
            return stack.enter_context(nc.sbuf_tensor(name, shape, dt))

        k = Shared()
        k.io, k.dram, k.out, k.sem, k.sb = io, dram, out, sem, sb
        k.ps = [top.enter_context(nc.psum_tensor(f"bank{i}", [P, 512], F32)) for i in range(8)]
        k.ident = sb(top, "ident", [P, P])
        k.upto = sb(top, "upto", [P, P])
        k.ones = sb(top, "ones", [P, P])
        k.before_bf = sb(top, "before_bf", [P, P], BF16)
        k.ones_bf = sb(top, "ones_bf", [P, P], BF16)
        k.iota = sb(top, "iota", [P, NB])
        k.power = sb(top, "power", [P, 32])
        k.slot_of = sb(top, "slot_of", [P, NT * TOP0], I32)
        k.weight_of = sb(top, "weight_of", [P, NT * TOP0])
        k.expert_of = sb(top, "expert_of", [P, NT * TOP0])
        k.rank_of = sb(top, "rank_of", [P, NT * TOP0])
        k.block_f = sb(top, "block_f", [P, NB])
        k.block_expert = sb(top, "block_expert", [P, NB], I32)
        k.start = sb(top, "start", [P, E0])
        k.upto_blocks = sb(top, "upto_blocks", [P, E0])
        k.consts_in, k.NCONST = sem("consts_in"), 7 * 16
        k.zero_out = sem("zero_out")
        k.DVE_A = 25
        k.DVE_L = 14

        k.NZERO = 16 * (SLOTS // (4 * P))
        k.experts_in, k.NEXPERTS = sem("experts_in"), 16 * 2 * (E0 // 8)
        with ExitStack() as experts:
            k.wu = sb(experts, "wu", [P, E0, KT, I0])
            k.wd = sb(experts, "wd", [P, E0, D])
            k.w_qkv = sb(experts, "w_qkv", [P, KT, 3 * D])
            k.w_ugh = sb(experts, "w_ugh", [P, KT, 2 * UG], F32R)
            k.w_ugl = sb(experts, "w_ugl", [P, KT, 2 * UG], F32R)
            k.w_ug = k.wu[:].rearrange("p e f i -> p (e f i)")[:, 0:KT * 2 * UG].rearrange("p (f n) -> p f n", f=KT)
            k.w_out = sb(experts, "w_out", [P, UG // P, D])
            k.w_su = sb(experts, "w_su", [P, KT, SI])
            k.w_sd = sb(experts, "w_sd", [P, SI // P, D])
            k.zeros = sb(experts, "zeros", [P, 4 * D])
            k.mix_in = sem("mix_in")
            with ExitStack() as st:
                route_tokens(nc, k, st)
            with ExitStack() as st:
                mix_tokens(nc, k, st)
            with ExitStack() as st:
                expert_blocks(nc, k, st)
        with ExitStack() as st:
            k.w1 = sb(st, "w1", [P, KT, SLOTS1 * P], F32R)
            k.w3 = sb(st, "w3", [P, KT, SLOTS1 * P], F32R)
            k.w2 = sb(st, "w2", [P, SLOTS1, D], F32R)
            k.layer1_in, k.NLAYER1, k.padded = sem("layer1_in"), 16 * 6, sem("padded")
            layer1(nc, k, st)


def constants():
    import numpy as np
    p = np.arange(P)
    inv = (1.0 / 10000.0 ** (np.arange(0, DK, 2, dtype=np.float32) / DK)).astype(np.float32)
    angle = np.arange(S1, dtype=np.float32)[:, None] * inv[None, :]

    def table(first, second):
        one = np.concatenate([first, second], axis=-1).astype(np.float32)
        return np.ascontiguousarray(np.concatenate([one] * (CH // S1)).reshape(TP, P, DK).transpose(1, 0, 2))

    return {
        "ident": np.eye(P, dtype=np.float32),
        "upto": (p[:, None] <= p[None, :]).astype(np.float32),
        "ones": np.ones((P, P), np.float32),
        "iota": np.ascontiguousarray(np.broadcast_to(np.arange(NB, dtype=np.float32), (P, NB))),
        "before_bf": (p[:, None] < p[None, :]).astype(mybir.dt.np(BF16)),
        "ones_bf": np.ones((P, P), mybir.dt.np(BF16)),
        "power": np.full((P, 32), -0.5, np.float32),
        "root": np.full((P, 32), 0.5, np.float32),
        "cos": table(np.cos(angle), np.cos(angle)),
        "sin": table(-np.sin(angle), np.sin(angle)),
        "mask1": np.where(p[None, :] > p[:, None], np.float32(-1e30), np.float32(0)).astype(mybir.dt.np(BF16)),
        "mask2": np.where(p[:, None] > p[None, :], np.float32(-1e30), np.float32(0)).astype(mybir.dt.np(BF16)),
        "ident_bf": np.eye(P, dtype=np.float32).astype(mybir.dt.np(BF16)),
    }


def scratch(nc, kind="Internal"):
    def d(name, *shape):
        return nc.dram_tensor("s_" + name, shape, F32, kind=kind).ap()

    return {"xn": d("xn", T, D), "xnT": d("xnT", D, T), "xg": d("xg", SLOTS, D), "y": d("y", SLOTS, D),
            "r": d("r", T, D), "cw": d("cw", NCH, E1, CH)}


def lay_out(inp):
    import numpy as np
    a = dict(constants())
    n = {name: np.asarray(v) for name, v in inp.items()}
    c = np.ascontiguousarray

    def rows(v):
        return c(np.broadcast_to(v, (P, v.shape[-1])))

    a["x"] = c(n["L0_attn_x"].reshape(T, D))
    a["gate_w0"] = c(n["L0_ffn_gate_w"])
    a["w_qkv"] = c(n["L0_attn_w_qkv"].T)
    a["w_ug"] = c(n["L0_attn_w_swiglu"].T)
    a["w_out"] = c(n["L0_attn_w_out"].T)
    a["w_su"] = c(n["L0_ffn_Wsu"])
    a["w_sd"] = c(n["L0_ffn_Wsd"])
    a["wu"] = c(n["L0_ffn_Wu"].reshape(E0, KT, P, I0).transpose(2, 0, 1, 3))
    a["wd"] = c(n["L0_ffn_Wd"].transpose(1, 0, 2))
    cat = np.concatenate
    a["w1"] = c(cat([n["L1_ffn_w1"].reshape(-1, D), n["L1_ffn_sw1"]]).T)
    a["w3"] = c(cat([n["L1_ffn_w3"].reshape(-1, D), n["L1_ffn_sw3"]]).T)
    a["w2"] = c(cat([n["L1_ffn_w2"].transpose(0, 2, 1).reshape(-1, D), n["L1_ffn_sw2"].T]))
    a["wq"] = c(n["L1_attn_Wq_w"].T)
    a["wo"] = c(n["L1_attn_Wo_w"].T)
    a["bq"] = rows(n["L1_attn_Wq_b"])
    a["bo"] = rows(n["L1_attn_Wo_b"])
    a["rms_w"] = c(n["L1_attn_rms_w"].reshape(KT, P).T)
    a["gate_w1"] = c(n["L1_ffn_gate_w"].T)
    a["gate_b1"] = rows(n["L1_ffn_gate_b"])
    a["bias0"] = rows(n["L0_ffn_e_bias"])
    return a


def kernel(**inputs):
    import concourse.bacc as bacc
    import numpy as np
    from concourse.bass_utils import run_bass_kernel_spmd

    arrays = lay_out(inputs)
    nc = bacc.Bacc("TRN2", target_bir_lowering=False, num_devices=1)
    io = {name: nc.dram_tensor("in_" + name, v.shape, mybir.dt.from_np(v.dtype), kind="ExternalInput").ap()
          for name, v in arrays.items()}
    out = nc.dram_tensor("out", (T, D), F32, kind="ExternalOutput").ap()
    program(nc, io, scratch(nc), out)
    result = run_bass_kernel_spmd(nc, [{"in_" + name: v for name, v in arrays.items()}], core_ids=[0]).results[0]
    return np.asarray(result["out"]).reshape(T // S1, S1, D)
```
